# Optimizing a Trainium2 kernel written in Bass

```python
import numpy as np
import jax
import jax.numpy as jnp

def _softmax(x, axis=-1):
    return jax.nn.softmax(x, axis=axis)

def _gelu(x):
    return jax.nn.gelu(x, approximate=True)

def _silu(x):
    return jax.nn.silu(x)

def _sigmoid(x):
    return jax.nn.sigmoid(x)

def _layernorm(x, axis=-1, eps=1e-05):
    m = jnp.mean(x, axis=axis, keepdims=True)
    v = jnp.var(x, axis=axis, keepdims=True)
    return (x - m) / jnp.sqrt(v + eps)

def _scatter_add(tgt, idx, src, axis=0):
    return tgt.at[idx].add(src)

def _segment_sum(src, seg, n):
    return jax.ops.segment_sum(src, seg, n)
kernel_name = 'mk_flamingo_gated_d2_seqx_r2_5520ff'

def setup_inputs(seed: int=0):
    np.random.seed(seed)
    _w = jnp.asarray

    def _rec_inputs():
        import jax
        import jax.numpy as jnp
        _rk = jax.random.key(seed)
        x = -0.0002928 + 1 * jax.random.normal(jax.random.fold_in(_rk, 1), (8, 100, 512), jnp.float32)
        _lenS = 100 - jax.random.randint(jax.random.fold_in(_rk, 7), (8,), 0, max(1, 100 // 4) + 1, jnp.int32)
        _lenS2 = 722 - jax.random.randint(jax.random.fold_in(_rk, 8), (8,), 0, max(1, 722 // 4) + 1, jnp.int32)
        _ctx_1024P = jax.random.normal(jax.random.fold_in(_rk, 11), (8, 16, 512), jnp.float32)
        _ctx_1024c = jax.random.dirichlet(jax.random.fold_in(_rk, 511), 0.3 * jnp.ones((16,), jnp.float32), (8, 722))
        _ctx_1024t = jnp.einsum('bsk,bkd->bsd', _ctx_1024c, _ctx_1024P)
        _ctx_1024t = _ctx_1024t * jax.lax.rsqrt(jnp.mean(jnp.square(_ctx_1024t)) + 1e-12) * 0.953939
        ctx_1024 = -1.39393e-06 + 0.999914 * (_ctx_1024t + 0.3 * jax.random.normal(jax.random.fold_in(_rk, 611), (8, 722, 512), jnp.float32))
        _validS = jnp.arange(100)[None, :] < _lenS[:, None]
        _validS2 = jnp.arange(722)[None, :] < _lenS2[:, None]
        _causal = jnp.tril(jnp.ones((100, 100), dtype=bool))
        mask_Bx1x1xS2_ik0 = jnp.where(jnp.broadcast_to(_validS2[:, None, None, :], (8, 1, 1, 722)), 0, 1).astype(jnp.int32)
        _g = jax.random.normal(jax.random.fold_in(_rk, 9001), (2, 2), jnp.float32)
        _g = jnp.sign(_g) * jnp.maximum(jnp.abs(_g), 1.0) + (_g == 0) * 1.0
        g_xattn = _g[0]
        g_ffn = _g[1]
        return (x, ctx_1024, mask_Bx1x1xS2_ik0, g_xattn, g_ffn)
    x, ctx_1024, mask_Bx1x1xS2_ik0, g_xattn, g_ffn = _rec_inputs()

    def _L0_xattn_setup():
        import jax, jax.numpy as jnp
        import numpy as np
        NUM_HEADS = 16
        D_MODEL = 512
        HEAD_DIM = D_MODEL // NUM_HEADS
        SCALE = 8.0 / HEAD_DIM
        LN_EPS = 1e-05

        def _layernorm(x, g, b):
            mu = jnp.mean(x, axis=-1, keepdims=True)
            var = jnp.mean(jnp.square(x - mu), axis=-1, keepdims=True)
            return (x - mu) * jax.lax.rsqrt(var + LN_EPS) * g + b
        key = jax.random.key(seed)
        ks = jax.random.split(key, 8)
        B, N, M = (2, 1024, 1024)
        std = 1.0 / np.sqrt(D_MODEL)
        return {'x1': jax.random.normal(ks[0], (B, N, D_MODEL), jnp.float32), 'x2': jax.random.normal(ks[1], (B, M, D_MODEL), jnp.float32), 'Wq': jax.random.normal(ks[2], (D_MODEL, D_MODEL), jnp.float32) * std, 'Wk': jax.random.normal(ks[3], (D_MODEL, D_MODEL), jnp.float32) * std, 'Wv': jax.random.normal(ks[4], (D_MODEL, D_MODEL), jnp.float32) * std, 'Wp': jax.random.normal(ks[5], (D_MODEL, D_MODEL), jnp.float32) * std, 'bp': jnp.zeros((D_MODEL,), jnp.float32), 'ln_g': jnp.ones((HEAD_DIM,), jnp.float32), 'ln_b': jnp.zeros((HEAD_DIM,), jnp.float32)}
    _L0_xattn_all = _L0_xattn_setup()
    _L0_xattn_in = {k: v for k, v in _L0_xattn_all.items() if k in ('Wq', 'Wk', 'Wv', 'Wp', 'bp', 'ln_g', 'ln_b')}
    del _L0_xattn_all

    def _L0_ffn_setup():
        import jax, jax.numpy as jnp
        import numpy as np
        H = 512
        I = 256
        E = 32
        TOP_K = 6
        N_GROUP = 8
        TOPK_GROUP = 4
        SCALE = 2.5
        N_SHARED = 2
        SI = I * N_SHARED
        B, S = (2, 512)
        key = jax.random.key(seed)
        ks = jax.random.split(key, 8)
        x = jax.random.normal(ks[0], (B, S, H), jnp.float32)
        gate_weight = jax.random.normal(ks[1], (E, H), jnp.float32) * 0.02
        e_score_correction_bias = jax.random.normal(ks[2], (E,), jnp.float32) * 0.01
        experts_gate_up = jax.random.normal(ks[3], (E, 2 * I, H), jnp.float32) * 0.02
        experts_down = jax.random.normal(ks[4], (E, H, I), jnp.float32) * 0.02
        shared_gate_w = jax.random.normal(ks[5], (SI, H), jnp.float32) * 0.02
        shared_up_w = jax.random.normal(ks[6], (SI, H), jnp.float32) * 0.02
        shared_down_w = jax.random.normal(ks[7], (H, SI), jnp.float32) * 0.02
        return {'x': x, 'gate_weight': gate_weight, 'e_score_correction_bias': e_score_correction_bias, 'experts_gate_up': experts_gate_up, 'experts_down': experts_down, 'shared_gate_w': shared_gate_w, 'shared_up_w': shared_up_w, 'shared_down_w': shared_down_w}
    _L0_ffn_all = _L0_ffn_setup()
    _L0_ffn_in = {k: v for k, v in _L0_ffn_all.items() if k in ('gate_weight', 'e_score_correction_bias', 'experts_gate_up', 'experts_down', 'shared_gate_w', 'shared_up_w', 'shared_down_w')}
    del _L0_ffn_all

    def _L1_xattn_setup():
        import jax, jax.numpy as jnp
        import numpy as np
        D_MODEL = 512
        NUM_HEADS = 16
        D_K = D_MODEL // NUM_HEADS
        B, S = (2, 1024)
        NEG = -1000000000.0

        def _split_heads(x):
            b, s, _ = x.shape
            return x.reshape(b, s, NUM_HEADS, D_K).transpose(0, 2, 1, 3)
        key = jax.random.key(seed)
        ks = jax.random.split(key, 13)
        std = 0.02
        inp = {'q': jax.random.normal(ks[0], (B, S, D_MODEL), dtype=jnp.float32), 'k': jax.random.normal(ks[1], (B, S, D_MODEL), dtype=jnp.float32), 'v': jax.random.normal(ks[2], (B, S, D_MODEL), dtype=jnp.float32), 'mask': jax.random.randint(ks[3], (B, 1, 1, S), 0, 2, dtype=jnp.int32), 'Wq': jax.random.normal(ks[4], (D_MODEL, D_MODEL), dtype=jnp.float32) * std, 'bq': jnp.zeros((D_MODEL,), dtype=jnp.float32), 'Wk': jax.random.normal(ks[5], (D_MODEL, D_MODEL), dtype=jnp.float32) * std, 'bk': jnp.zeros((D_MODEL,), dtype=jnp.float32), 'Wv': jax.random.normal(ks[6], (D_MODEL, D_MODEL), dtype=jnp.float32) * std, 'bv': jnp.zeros((D_MODEL,), dtype=jnp.float32), 'Wo': jax.random.normal(ks[7], (D_MODEL, D_MODEL), dtype=jnp.float32) * std, 'bo': jnp.zeros((D_MODEL,), dtype=jnp.float32)}
        return inp
    _L1_xattn_all = _L1_xattn_setup()
    _L1_xattn_in = {k: v for k, v in _L1_xattn_all.items() if k in ('Wq', 'bq', 'Wk', 'bk', 'Wv', 'bv', 'Wo', 'bo')}
    del _L1_xattn_all

    def _L1_ffn_setup():
        import math
        import jax, jax.numpy as jnp
        import numpy as np
        D_MODEL = 512
        D_HIDDEN = 1024
        N_EXPERTS = 8
        TOP_K = 2
        CAPACITY_FACTOR = 1.25

        def _moe_forward(x, w_router, w_gate, w_down):
            B, T, D = x.shape
            N = B * T
            xf = x.reshape(N, D)
            logits = xf.astype(jnp.float32) @ w_router.T
            gates = jax.nn.softmax(logits, axis=-1)
            topk_gates, topk_idx = jax.lax.top_k(gates, TOP_K)
            expert_mask = jax.nn.one_hot(topk_idx, N_EXPERTS, dtype=jnp.int32).sum(axis=1)
            capacity = math.ceil(N / N_EXPERTS * CAPACITY_FACTOR)
            position_in_expert = jnp.cumsum(expert_mask, axis=0) - 1
            expert_mask = expert_mask * (position_in_expert < capacity)
            keep = jnp.take_along_axis(expert_mask, topk_idx, axis=1) > 0
            topk_gates = topk_gates * keep
            topk_gates = topk_gates / (topk_gates.sum(axis=-1, keepdims=True) + 1e-06)
            hidden = jax.nn.silu(xf @ w_gate.T)
            combine = (topk_gates[:, :, None] * jax.nn.one_hot(topk_idx, N_EXPERTS, dtype=topk_gates.dtype)).sum(axis=1)
            y = jnp.zeros((N, D), dtype=x.dtype)
            for e in range(N_EXPERTS):
                y = y + combine[:, e:e + 1] * (hidden @ w_down[e].T)
            return y.reshape(B, T, D)
        key = jax.random.key(seed)
        k0, k1, k2, k3 = jax.random.split(key, 4)
        B, T = (2, 1024)
        x = jax.random.normal(k0, (B, T, D_MODEL), dtype=jnp.float32)
        w_router = jax.random.normal(k1, (N_EXPERTS, D_MODEL), dtype=jnp.float32) * 0.02
        w_gate = jax.random.normal(k2, (D_HIDDEN, D_MODEL), dtype=jnp.float32) * 0.02
        w_down = jax.random.normal(k3, (N_EXPERTS, D_MODEL, D_HIDDEN), dtype=jnp.float32) * 0.02
        return {'x': x, 'w_router': w_router, 'w_gate': w_gate, 'w_down': w_down}
    _L1_ffn_all = _L1_ffn_setup()
    _L1_ffn_in = {k: v for k, v in _L1_ffn_all.items() if k in ('w_router', 'w_gate', 'w_down')}
    del _L1_ffn_all
    return {'x': x, 'ctx_1024': ctx_1024, 'mask_Bx1x1xS2_ik0': mask_Bx1x1xS2_ik0, 'g_xattn': g_xattn, 'g_ffn': g_ffn, 'L0_xattn_Wq': _L0_xattn_in['Wq'], 'L0_xattn_Wk': _L0_xattn_in['Wk'], 'L0_xattn_Wv': _L0_xattn_in['Wv'], 'L0_xattn_Wp': _L0_xattn_in['Wp'], 'L0_xattn_bp': _L0_xattn_in['bp'], 'L0_xattn_ln_g': _L0_xattn_in['ln_g'], 'L0_xattn_ln_b': _L0_xattn_in['ln_b'], 'L0_ffn_gate_weight': _L0_ffn_in['gate_weight'], 'L0_ffn_e_score_correction_bias': _L0_ffn_in['e_score_correction_bias'], 'L0_ffn_experts_gate_up': _L0_ffn_in['experts_gate_up'], 'L0_ffn_experts_down': _L0_ffn_in['experts_down'], 'L0_ffn_shared_gate_w': _L0_ffn_in['shared_gate_w'], 'L0_ffn_shared_up_w': _L0_ffn_in['shared_up_w'], 'L0_ffn_shared_down_w': _L0_ffn_in['shared_down_w'], 'L1_xattn_Wq': _L1_xattn_in['Wq'], 'L1_xattn_bq': _L1_xattn_in['bq'], 'L1_xattn_Wk': _L1_xattn_in['Wk'], 'L1_xattn_bk': _L1_xattn_in['bk'], 'L1_xattn_Wv': _L1_xattn_in['Wv'], 'L1_xattn_bv': _L1_xattn_in['bv'], 'L1_xattn_Wo': _L1_xattn_in['Wo'], 'L1_xattn_bo': _L1_xattn_in['bo'], 'L1_ffn_w_router': _L1_ffn_in['w_router'], 'L1_ffn_w_gate': _L1_ffn_in['w_gate'], 'L1_ffn_w_down': _L1_ffn_in['w_down']}

def reference(x, ctx_1024, mask_Bx1x1xS2_ik0, g_xattn, g_ffn, L0_xattn_Wq, L0_xattn_Wk, L0_xattn_Wv, L0_xattn_Wp, L0_xattn_bp, L0_xattn_ln_g, L0_xattn_ln_b, L0_ffn_gate_weight, L0_ffn_e_score_correction_bias, L0_ffn_experts_gate_up, L0_ffn_experts_down, L0_ffn_shared_gate_w, L0_ffn_shared_up_w, L0_ffn_shared_down_w, L1_xattn_Wq, L1_xattn_bq, L1_xattn_Wk, L1_xattn_bk, L1_xattn_Wv, L1_xattn_bv, L1_xattn_Wo, L1_xattn_bo, L1_ffn_w_router, L1_ffn_w_gate, L1_ffn_w_down):
    import jax
    import jax.numpy as jnp

    def _L0_xattn_ref(x1, x2, Wq, Wk, Wv, Wp, bp, ln_g, ln_b):
        import jax, jax.numpy as jnp
        import numpy as np
        NUM_HEADS = 16
        D_MODEL = 512
        HEAD_DIM = D_MODEL // NUM_HEADS
        SCALE = 8.0 / HEAD_DIM
        LN_EPS = 1e-05

        def _layernorm(x, g, b):
            mu = jnp.mean(x, axis=-1, keepdims=True)
            var = jnp.mean(jnp.square(x - mu), axis=-1, keepdims=True)
            return (x - mu) * jax.lax.rsqrt(var + LN_EPS) * g + b
        B, N, C = x1.shape
        M = x2.shape[1]
        H, D = (NUM_HEADS, HEAD_DIM)
        q = (x1 @ Wq.T).reshape(B, N, H, D).transpose(0, 2, 1, 3)
        k = (x2 @ Wk.T).reshape(B, M, H, D).transpose(0, 2, 1, 3)
        v = (x2 @ Wv.T).reshape(B, M, H, D).transpose(0, 2, 1, 3)
        q = _layernorm(q, ln_g, ln_b)
        k = _layernorm(k, ln_g, ln_b)
        q = q * SCALE
        attn = jnp.einsum('bhnd,bhmd->bhnm', q, k)
        attn = jax.nn.softmax(attn, axis=-1)
        out = jnp.einsum('bhnm,bhmd->bhnd', attn, v)
        out = out.transpose(0, 2, 1, 3).reshape(B, N, C)
        return out @ Wp.T + bp

    def _L0_ffn_ref(x, gate_weight, e_score_correction_bias, experts_gate_up, experts_down, shared_gate_w, shared_up_w, shared_down_w):
        import jax, jax.numpy as jnp
        import numpy as np
        H = 512
        I = 256
        E = 32
        TOP_K = 6
        N_GROUP = 8
        TOPK_GROUP = 4
        SCALE = 2.5
        N_SHARED = 2
        SI = I * N_SHARED
        B, S = (2, 512)
        b, s, h = x.shape
        xf = x.reshape(-1, h)
        T = xf.shape[0]
        logits = xf.astype(jnp.float32) @ gate_weight.astype(jnp.float32).T
        scores = jax.nn.sigmoid(logits)
        sfc = scores + e_score_correction_bias[None, :]
        gs = E // N_GROUP
        group_scores = sfc.reshape(T, N_GROUP, gs).max(axis=-1)
        _, gidx = jax.lax.top_k(group_scores, TOPK_GROUP)
        gmask = jnp.zeros((T, N_GROUP), bool).at[jnp.arange(T)[:, None], gidx].set(True)
        smask = jnp.repeat(gmask, gs, axis=1)
        masked = jnp.where(smask, sfc, 0.0)
        _, topk_idx = jax.lax.top_k(masked, TOP_K)
        tw = jnp.take_along_axis(scores, topk_idx, axis=1)
        tw = tw / (tw.sum(-1, keepdims=True) + 1e-20)
        tw = (tw * SCALE).astype(xf.dtype)
        combine = jnp.zeros((T, E), xf.dtype).at[jnp.arange(T)[:, None], topk_idx].add(tw)

        def expert_step(acc, inp):
            gu, dn, c = inp
            g = xf @ gu[:I].T
            u = xf @ gu[I:].T
            o = jax.nn.silu(g) * u @ dn.T
            return (acc + c[:, None] * o, None)
        routed, _ = jax.lax.scan(expert_step, jnp.zeros_like(xf), (experts_gate_up, experts_down, combine.T))
        sh = jax.nn.silu(xf @ shared_gate_w.T) * (xf @ shared_up_w.T)
        shared_out = sh @ shared_down_w.T
        return (routed + shared_out).reshape(b, s, h)

    def _L1_xattn_ref(q, k, v, mask, Wq, bq, Wk, bk, Wv, bv, Wo, bo):
        import jax, jax.numpy as jnp
        import numpy as np
        D_MODEL = 512
        NUM_HEADS = 16
        D_K = D_MODEL // NUM_HEADS
        B, S = (2, 1024)
        NEG = -1000000000.0

        def _split_heads(x):
            b, s, _ = x.shape
            return x.reshape(b, s, NUM_HEADS, D_K).transpose(0, 2, 1, 3)
        qh = _split_heads(q @ Wq.T + bq)
        kh = _split_heads(k @ Wk.T + bk)
        vh = _split_heads(v @ Wv.T + bv)
        scale = 1.0 / jnp.sqrt(jnp.float32(D_K))
        scores = jnp.einsum('bhqd,bhkd->bhqk', qh, kh) * scale
        scores = jnp.where(mask == 0, jnp.float32(NEG), scores)
        probs = jax.nn.softmax(scores, axis=-1)
        attn = jnp.einsum('bhqk,bhkd->bhqd', probs, vh)
        out = attn.transpose(0, 2, 1, 3).reshape(q.shape[0], q.shape[1], D_MODEL)
        return out @ Wo.T + bo

    def _L1_ffn_ref(x, w_router, w_gate, w_down):
        import math
        import jax, jax.numpy as jnp
        import numpy as np
        D_MODEL = 512
        D_HIDDEN = 1024
        N_EXPERTS = 8
        TOP_K = 2
        CAPACITY_FACTOR = 1.25

        def _moe_forward(x, w_router, w_gate, w_down):
            B, T, D = x.shape
            N = B * T
            xf = x.reshape(N, D)
            logits = xf.astype(jnp.float32) @ w_router.T
            gates = jax.nn.softmax(logits, axis=-1)
            topk_gates, topk_idx = jax.lax.top_k(gates, TOP_K)
            expert_mask = jax.nn.one_hot(topk_idx, N_EXPERTS, dtype=jnp.int32).sum(axis=1)
            capacity = math.ceil(N / N_EXPERTS * CAPACITY_FACTOR)
            position_in_expert = jnp.cumsum(expert_mask, axis=0) - 1
            expert_mask = expert_mask * (position_in_expert < capacity)
            keep = jnp.take_along_axis(expert_mask, topk_idx, axis=1) > 0
            topk_gates = topk_gates * keep
            topk_gates = topk_gates / (topk_gates.sum(axis=-1, keepdims=True) + 1e-06)
            hidden = jax.nn.silu(xf @ w_gate.T)
            combine = (topk_gates[:, :, None] * jax.nn.one_hot(topk_idx, N_EXPERTS, dtype=topk_gates.dtype)).sum(axis=1)
            y = jnp.zeros((N, D), dtype=x.dtype)
            for e in range(N_EXPERTS):
                y = y + combine[:, e:e + 1] * (hidden @ w_down[e].T)
            return y.reshape(B, T, D)
        return _moe_forward(x, w_router, w_gate, w_down)
    x = x + jnp.tanh(g_xattn[0]) * _L0_xattn_ref(_layernorm(x, axis=-1), ctx_1024, L0_xattn_Wq, L0_xattn_Wk, L0_xattn_Wv, L0_xattn_Wp, L0_xattn_bp, L0_xattn_ln_g, L0_xattn_ln_b)
    x = x + jnp.tanh(g_ffn[0]) * _L0_ffn_ref(_layernorm(x, axis=-1), L0_ffn_gate_weight, L0_ffn_e_score_correction_bias, L0_ffn_experts_gate_up, L0_ffn_experts_down, L0_ffn_shared_gate_w, L0_ffn_shared_up_w, L0_ffn_shared_down_w)
    x = x + jnp.tanh(g_xattn[1]) * _L1_xattn_ref(_layernorm(x, axis=-1), ctx_1024, ctx_1024, mask_Bx1x1xS2_ik0, L1_xattn_Wq, L1_xattn_bq, L1_xattn_Wk, L1_xattn_bk, L1_xattn_Wv, L1_xattn_bv, L1_xattn_Wo, L1_xattn_bo)
    x = x + jnp.tanh(g_ffn[1]) * _L1_ffn_ref(_layernorm(x, axis=-1), L1_ffn_w_router, L1_ffn_w_gate, L1_ffn_w_down)
    return x

_drawn_inputs = setup_inputs


def setup_inputs(seed=0):
    import zlib

    import numpy as np

    out = dict(_drawn_inputs(seed))
    spreads = {'g_ffn': (-1.0, 0.6),
     'L0_xattn_bp': (0.0, 0.1),
     'L0_xattn_ln_g': (1.0, 0.2),
     'L0_xattn_ln_b': (0.0, 0.399),
     'L1_xattn_bq': (0.0, 0.8),
     'L1_xattn_bk': (0.0, 2.0),
     'L1_xattn_bv': (0.0, 0.1),
     'L1_xattn_bo': (0.0, 0.1)}
    factors = {'L0_ffn_e_score_correction_bias': 13.549, 'L1_xattn_Wq': 4.205, 'L1_xattn_Wk': 3.81}
    for name, (base, spread) in spreads.items():
        noise = np.random.default_rng([zlib.crc32(name.encode()), seed]).standard_normal(out[name].shape)
        drawn = base * np.exp(spread * noise) if base else spread * noise
        out[name] = jnp.asarray(drawn.astype(out[name].dtype))
    for name, factor in factors.items():
        out[name] = (out[name] * factor).astype(out[name].dtype)
    return out
```

```python
from contextlib import ExitStack

import concourse.bass as bass
from concourse import mybir

F32 = mybir.dt.float32
F32R = mybir.dt.float32r
I32 = mybir.dt.int32
ALU = mybir.AluOpType
ACT = mybir.ActivationFunctionType
AX = mybir.AxisListType.X

P = 128
B, SQ, SK, D = 8, 100, 722, 512
NT = B * SQ
NK = D // P
H = 16
HD = D // H
GH = P // HD
NG = H // GH
KC = -(-SK // P)
KTAIL = SK - (KC - 1) * P
KHALF = (362, 360)
KOFF = 512 - KHALF[0]
LN_EPS = 1e-5
L0_SCALE = 8.0 / HD
L1_SCALE = float(1.0 / (HD ** 0.5))
NEG = 1e9
E0, I0, TOP0, GRP0, TOPG0 = 32, 256, 6, 8, 4
ES = E0 + 2
W0_SCALE = 2.5
E1, HID1, TOP1 = 8, 1024, 2
NI1 = HID1 // P
CAP1 = -(-NT * 5 // (E1 * 4))
C_LNG, C_LNB, C_BK, C_BQ, C_BV, C_GX, C_GF = 0, 1, 2, 6, 10, 14, 16
NCOLS = 18


PRIMED = 1


def prime(eng, *sems):
    for s in sems:
        eng.sem_inc(s, PRIMED)


class Chain:

    def __init__(self, eng, sem):
        self.eng, self.sem, self.n = eng, sem, 0

    def step(self, ins):
        self.n += 1
        ins.then_inc(self.sem, 1)
        self.eng.wait_ge(self.sem, self.n)


def key_halves():
    return ((0, KHALF[0], KOFF), (KHALF[0], KHALF[1], 512))


def chunk_rows(c):
    return P if c < KC - 1 else KTAIL


def project_context(nc, sem, A, S):
    with ExitStack() as ctx:
        sb = lambda name, shape, dt=F32: ctx.enter_context(nc.sbuf_tensor(name, shape, dt))
        ps = lambda name, shape: ctx.enter_context(nc.psum_tensor(name, shape, F32))
        w_names = ("k0", "k1", "v0", "v1")
        w_raw = sb("w_raw", [P, 2, NK, D])
        w_hi = {n: sb("w_hi_" + n, [P, NK, D], F32R) for n in w_names}
        w_lo = {n: sb("w_lo_" + n, [P, NK, D], F32R) for n in w_names}
        w_mean = sb("w_mean", [P, NK * H])
        ctx_raw = sb("ctx_raw", [P, NK, SK])
        ctx_hi = [sb(f"ctx_hi{i}", [P, NK, SK], F32R) for i in range(2)]
        ctx_lo = [sb(f"ctx_lo{i}", [P, NK, SK], F32R) for i in range(2)]
        mask_raw = sb("mask_raw", [P, SK], I32)
        keep = sb("keep", [P, SK])
        sq = sb("sq", [P, SK])
        lnv = sb("lnv", [P, SK])
        k0n = sb("k0n", [P, SK])
        k0f = sb("k0f", [P, SK])
        k1f = sb("k1f", [P, SK])
        kst = [[sb(f"kst{L}_{part}", [P, SK], F32R) for part in "hl"] for L in range(2)]
        vst = sb("vst", [P, 2, D])
        head_mean = S["head_mean"]
        psK = [ps(f"psK{L}", [P, 1024]) for L in range(2)]
        psR = ps("psR", [P, 1024])
        psV = [ps(f"psV{i}", [P, 512]) for i in range(2)]
        row = slice(KOFF, KOFF + SK)

        w_in = [sem(f"pc_w_in{i}") for i in range(2)]
        w_ready = sem("pc_w_ready")
        w_hid = sem("pc_w_hid")
        dch = sem("pc_dch")
        ctx_in = sem("pc_ctx_in")
        mask_in = sem("pc_mask_in")
        keep_done = sem("pc_keep_done")
        ctx_hid = sem("pc_ctx_hid")
        ctx_split = sem("pc_ctx_split")
        k0_done, k1_done = sem("pc_k0_done"), sem("pc_k1_done")
        sq_done, var_done, ln_done, rstd_done = sem("pc_sq"), sem("pc_var"), sem("pc_ln"), sem("pc_rstd")
        k0n_done, k0f_done, k1f_done = sem("pc_k0n"), sem("pc_k0f"), sem("pc_k1f")
        hi_done = [sem(f"pc_hi{L}") for L in range(2)]
        lo_done = [sem(f"pc_lo{L}") for L in range(2)]
        k_stored = [sem(f"pc_k_stored{L}") for L in range(2)]
        v_done = sem("pc_v_done")
        v_copied = [sem(f"pc_v_copied{i}") for i in range(2)]
        v_stored = [sem(f"pc_v_stored{i}") for i in range(2)]
        block = ctx.enter_context(nc.Block())

        v_order = [(L, c) for L in range(2) for c in range(KC)]

        @block.sync
        def _(sp):
            prime(sp, *k_stored, *v_stored)
            for i, n in enumerate(w_names):
                if i >= 2:
                    sp.wait_ge(w_ready, i - 1)
                sp.dma_start(w_raw[:, i % 2], A["wT_" + n].rearrange("(c p) n -> p c n", p=P)).then_inc(w_in[i % 2], 16)
                if i == 0:
                    sp.dma_start(ctx_raw[:], A["ctxT"][0]).then_inc(ctx_in, 16)
            with sp.Fori(0, B // 2) as it:
                for par in range(2):
                    n = it * 2 + par
                    sp.wait_ge(k1f_done, n * NK + PRIMED)
                    sp.dma_start(mask_raw[:], A["mask"][bass.ds(n, 1), :].broadcast_to([P, SK])).then_inc(mask_in, 16)
                    sp.wait_ge(ctx_split, (n + 1) * NK)
                    sp.dma_start(ctx_raw[:], A["ctxT"][n + 1]).then_inc(ctx_in, 16)
                    for m in range(NK):
                        r = n * NK + m
                        for q in (3 * m, 3 * m + 1, 3 * m + 2):
                            L, c = v_order[q]
                            w = chunk_rows(c)
                            sp.wait_ge(v_copied[q % 2], n * 6 + q // 2 + 1 + PRIMED)
                            sp.dma_start(S["V"][L][n, c * P:c * P + w, :], vst[0:w, q % 2]).then_inc(v_stored[q % 2], 16)
                        for L in range(2):
                            sp.wait_ge(hi_done[L], r + 1 + PRIMED)
                            sp.wait_ge(lo_done[L], r + 1 + PRIMED)
                            for part in range(2):
                                sp.dma_start(S["K"][L][part, m * P:(m + 1) * P, n, :], kst[L][part][:].bitcast(F32)).then_inc(k_stored[L], 16)
            for L in range(2):
                sp.wait_ge(k_stored[L], 2 * 16 * B * NK + PRIMED)
                sp.wait_ge(v_stored[L], 16 * B * KC + PRIMED)

        @block.tensor
        def _(pe):
            prime(pe, v_done)
            def product(out, wt, k, cols, first, last):
                wh, wl, xh, xl = wt
                nc.tensor.matmul(out, wh, xh, start=first, stop=False)
                nc.tensor.matmul(out, wh, xl, start=False, stop=False)
                return nc.tensor.matmul(out, wl, xh, start=False, stop=last)

            def k_chunk(L, m, par, done):
                name = f"k{L}"
                for col, w, at in key_halves():
                    for k in range(NK):
                        ws = slice(m * P, (m + 1) * P)
                        ins = product(psK[L][:, at:at + w],
                                      (w_hi[name][:, k, ws], w_lo[name][:, k, ws],
                                       ctx_hi[par][:, k, col:col + w], ctx_lo[par][:, k, col:col + w]),
                                      k, w, k == 0, k == NK - 1)
                ins.then_inc(done, 1)

            def v_chunk(n, q, par):
                L, c = v_order[q]
                w = chunk_rows(c)
                name = f"v{L}"
                pe.wait_ge(v_copied[q % 2], n * 6 + q // 2 + PRIMED)
                cs = slice(c * P, c * P + w)
                for k in range(NK):
                    ins = product(psV[q % 2][0:w, :],
                                  (ctx_hi[par][:, k, cs], ctx_lo[par][:, k, cs],
                                   w_hi[name][:, k, :], w_lo[name][:, k, :]), k, D, k == 0, k == NK - 1)
                ins.then_inc(v_done, 1)

            pe.wait_ge(w_ready, 4)
            with pe.Fori(0, B // 2) as it:
                for par in range(2):
                    n = it * 2 + par
                    pe.wait_ge(ctx_split, (n + 1) * NK)
                    for m in range(NK):
                        r = n * NK + m
                        pe.wait_ge(k0n_done, r + PRIMED)
                        k_chunk(0, m, par, k0_done)
                        v_chunk(n, 3 * m, par)
                        pe.wait_ge(sq_done, r + 1)
                        pe.wait_ge(ln_done, r + PRIMED)
                        for col, w, at in key_halves():
                            ins = nc.tensor.matmul(psR[:, at:at + w], head_mean[:], sq[:, col:col + w], start=True, stop=True)
                        ins.then_inc(var_done, 1)
                        v_chunk(n, 3 * m + 1, par)
                        pe.wait_ge(k1f_done, r + PRIMED)
                        k_chunk(1, m, par, k1_done)
                        v_chunk(n, 3 * m + 2, par)

        @block.scalar
        def _(act):
            prime(act, ln_done, *hi_done)
            for i, n in enumerate(w_names):
                if i == 0:
                    act.wait_ge(w_hid, 1)
                else:
                    act.wait_ge(w_in[i % 2], 16 * (i // 2 + 1))
                nc.scalar.copy(w_hi[n][:], w_raw[:, i % 2]).then_inc(w_hid, 1)
            act.wait_ge(ctx_in, 16)
            for k in range(NK):
                nc.scalar.copy(ctx_hi[0][:, k, :], ctx_raw[:, k, :]).then_inc(ctx_hid, 1)
            with act.Fori(0, B // 2) as it:
                for par in range(2):
                    n = it * 2 + par
                    act.wait_ge(ctx_in, 16 * (n + 2))
                    act.wait_ge(v_done, n * 12 + PRIMED)
                    for m in range(NK):
                        r = n * NK + m
                        act.wait_ge(k0_done, r + 1)
                        nc.scalar.activation(sq[:], psK[0][:, row], ACT.Square).then_inc(sq_done, 1)
                        nc.scalar.copy(ctx_hi[1 - par][:, m, :], ctx_raw[:, m, :]).then_inc(ctx_hid, 1)
                        act.wait_ge(var_done, r + 1)
                        act.wait_ge(k0n_done, r + PRIMED)
                        nc.scalar.activation(lnv[:], psR[:, row], ACT.Ln, bias=S["eps"][:, 0:1]).then_inc(ln_done, 1)
                        act.wait_ge(ln_done, r + 1 + PRIMED)
                        nc.scalar.activation(lnv[:], lnv[:], ACT.Exp, scale=-0.5).then_inc(rstd_done, 1)
                        for L, f_done, kf in ((0, k0f_done, k0f), (1, k1f_done, k1f)):
                            act.wait_ge(f_done, r + 1 + L * PRIMED)
                            act.wait_ge(k_stored[L], 32 * r + PRIMED)
                            nc.scalar.copy(kst[L][0][:], kf[:]).then_inc(hi_done[L], 1)

        @block.gpsimd
        def _(pool):
            prime(pool, *lo_done)
            for k in range(NK):
                pool.wait_ge(ctx_hid, k + 1)
                nc.gpsimd.tensor_tensor(ctx_lo[0][:, k, :], ctx_raw[:, k, :], ctx_hi[0][:, k, :], ALU.subtract).then_inc(ctx_split, 1)
            with pool.Fori(0, B // 2) as it:
                for par in range(2):
                    n = it * 2 + par
                    for m in range(NK):
                        r = n * NK + m
                        pool.wait_ge(ctx_hid, (n + 1) * NK + m + 1)
                        nc.gpsimd.tensor_tensor(ctx_lo[1 - par][:, m, :], ctx_raw[:, m, :], ctx_hi[1 - par][:, m, :],
                                                ALU.subtract).then_inc(ctx_split, 1)
                        for L, kf in ((0, k0f), (1, k1f)):
                            pool.wait_ge(hi_done[L], r + 1 + PRIMED)
                            pool.wait_ge(k_stored[L], 32 * r + PRIMED)
                            nc.gpsimd.tensor_tensor(kst[L][1][:], kf[:], kst[L][0][:], ALU.subtract).then_inc(lo_done[L], 1)

        @block.vector
        def _(dve):
            prime(dve, k0n_done, k1f_done, *v_copied)
            link = Chain(dve, dch).step
            dve.wait_ge(w_in[0], 16)
            heads = w_raw[:, 0].rearrange("p c (h d) -> p (c h) d", d=HD)
            link(nc.vector.tensor_reduce(w_mean[:], heads, axis=AX, op=ALU.add))
            link(nc.vector.tensor_scalar(w_mean[:], w_mean[:], 1.0 / HD, None, ALU.mult))
            nc.vector.tensor_tensor(heads, heads, w_mean[:].unsqueeze(2).broadcast_to([P, NK * H, HD]), ALU.subtract).then_inc(w_hid, 1)
            for i, n in enumerate(w_names):
                dve.wait_ge(w_hid, i + 2)
                nc.vector.tensor_tensor(w_lo[n][:], w_raw[:, i % 2], w_hi[n][:], ALU.subtract).then_inc(w_ready, 1)
            with dve.Fori(0, B // 2) as it:
                for par in range(2):
                    n = it * 2 + par
                    dve.wait_ge(mask_in, 16 * (n + 1))
                    nc.vector.tensor_scalar(keep[:], mask_raw[:], 0.0, None, ALU.not_equal).then_inc(keep_done, 1)
                    dve.wait_ge(keep_done, n + 1)
                    for m in range(NK):
                        r = n * NK + m

                        def v_out(q):
                            L, c = v_order[q]
                            w = chunk_rows(c)
                            dve.wait_ge(v_done, n * 12 + q + 1 + PRIMED)
                            dve.wait_ge(v_stored[q % 2], 16 * (n * 6 + q // 2) + PRIMED)
                            nc.vector.tensor_copy(vst[0:w, q % 2], psV[q % 2][0:w, :]).then_inc(v_copied[q % 2], 1)

                        v_out(3 * m)
                        dve.wait_ge(rstd_done, r + 1)
                        dve.wait_ge(k0f_done, r)
                        nc.vector.tensor_tensor(k0n[:], psK[0][:, row], lnv[:], ALU.mult).then_inc(k0n_done, 1)
                        v_out(3 * m + 1)
                        dve.wait_ge(k0n_done, r + 1 + PRIMED)
                        dve.wait_ge(lo_done[0], r + PRIMED)
                        nc.vector.tensor_scalar(k0f[:], k0n[:], S["cols"][:, C_LNG:C_LNG + 1], S["cols"][:, C_LNB:C_LNB + 1],
                                                ALU.mult, ALU.add).then_inc(k0f_done, 1)
                        dve.wait_ge(k1_done, r + 1)
                        dve.wait_ge(lo_done[1], r + PRIMED)
                        nc.vector.scalar_tensor_tensor(k1f[:], psK[1][:, row], S["cols"][:, C_BK + m:C_BK + m + 1], keep[:],
                                                       ALU.add, ALU.mult).then_inc(k1f_done, 1)
                        v_out(3 * m + 2)


def norm_and_transpose(nc, sem, tag, S, T, ps_t):
    mv_done, lny, y_done = sem(tag + "_mv"), sem(tag + "_lny"), sem(tag + "_y")
    xn_done, xt_done, xT_done = sem(tag + "_xn"), sem(tag + "_xt"), sem(tag + "_xT")
    x, xn, xT, st, mv, rs = S["x"], T["xn"], T["xT"], T["st"], T["mv"], T["rs"]
    nps = len(ps_t)

    def vector(dve, link):
        for b in range(B):
            ins = nc.vector.bn_stats(st[:, b, :], x[:, b, :])
        link(ins)
        for b in range(B):
            ins = nc.vector.bn_aggr(mv[:, b, :], st[:, b, :])
        link(ins)
        var = rs[:, 0:B]
        nc.vector.tensor_scalar(var, mv[:, :, 1], LN_EPS, None, ALU.add).then_inc(mv_done, 1)
        dve.wait_ge(mv_done, 1)
        y, t = rs[:, 2 * B:3 * B], rs[:, 3 * B:4 * B]
        dve.wait_ge(y_done, 1)
        link(nc.vector.tensor_tensor(t, y, y, ALU.mult))
        link(nc.vector.tensor_tensor(t, t, var, ALU.mult))
        link(nc.vector.tensor_scalar(t, t, -0.5, 1.5, ALU.mult, ALU.add))
        link(nc.vector.tensor_tensor(t, t, y, ALU.mult))
        for b in range(B):
            nc.vector.tensor_scalar(xn[:, b, :], x[:, b, :], mv[:, b, 0:1], t[:, b:b + 1], ALU.subtract, ALU.mult).then_inc(xn_done, 1)
        for b in range(1, B, 2):
            dve.wait_ge(xt_done, b + 1)
            nc.vector.tensor_copy(xT[:, :, b * SQ:(b + 1) * SQ], ps_t[b % nps][:, 0:NK * SQ].rearrange("p (c t) -> p c t", c=NK)).then_inc(xT_done, 1)

    def scalar(act):
        act.wait_ge(mv_done, 1)
        nc.scalar.activation(rs[:, B:2 * B], rs[:, 0:B], ACT.Ln).then_inc(lny, 1)
        act.wait_ge(lny, 1)
        nc.scalar.activation(rs[:, 2 * B:3 * B], rs[:, B:2 * B], ACT.Exp, scale=-0.5).then_inc(y_done, 1)
        for b in range(0, B, 2):
            act.wait_ge(xt_done, b + 1)
            nc.scalar.copy(xT[:, :, b * SQ:(b + 1) * SQ], ps_t[b % nps][:, 0:NK * SQ].rearrange("p (c t) -> p c t", c=NK)).then_inc(xT_done, 1)

    def tensor(pe):
        for b in range(B):
            pe.wait_ge(xn_done, b + 1)
            if b >= nps:
                pe.wait_ge(xT_done, b - nps + 2)
            for c in range(NK):
                ins = nc.tensor.transpose(ps_t[b % nps][:, c * SQ:(c + 1) * SQ], xn[:, b, c * P:(c + 1) * P], S["ident"][0:SQ, 0:SQ])
            ins.then_inc(xt_done, 1)

    return vector, scalar, tensor, xT_done


def norm_tiles(sb):
    return {"xn": sb("xn", [SQ, B, D]), "xT": sb("xT", [P, NK, NT]), "st": sb("bn_st", [SQ, B, 6]),
            "mv": sb("bn_mv", [SQ, B, 2]), "rs": sb("bn_rs", [SQ, 4 * B])}


def queries(nc, sem, L, A, S):
    HALF = NT // 2
    tag = f"q{L}"
    with ExitStack() as ctx:
        sb = lambda name, shape, dt=F32: ctx.enter_context(nc.sbuf_tensor(f"{tag}_{name}", shape, dt))
        ps = lambda name, shape: ctx.enter_context(nc.psum_tensor(f"{tag}_{name}", shape, F32))
        T = norm_tiles(sb)
        xT = T["xT"]
        wq = sb("wq", [P, NK, D])
        w_mean = sb("w_mean", [P, NK * H])
        gb = sb("gb", [P, 2])
        sq, lnv, qn, qf = (sb(n, [P, 2, HALF]) for n in ("sq", "lnv", "qn", "qf"))
        q_hi = [sb(f"q_hi{i}", [P, HALF], F32R) for i in range(2)]
        q_lo = [sb(f"q_lo{i}", [P, HALF], F32R) for i in range(2)]
        ps_t = [ps(f"t{i}", [P, 512]) for i in range(2)]
        ps_q = [ps(f"q{i}", [P, 512]) for i in range(2)]
        ps_r = [ps(f"r{i}", [P, 512]) for i in range(2)]
        w_in, w_done, dch = sem(tag + "_w_in"), sem(tag + "_w_done"), sem(tag + "_dch")
        q_done, sq_done, var_done = sem(tag + "_q_done"), sem(tag + "_sq"), sem(tag + "_var")
        ln_done, rstd_done, qf_done = sem(tag + "_ln"), sem(tag + "_rstd"), sem(tag + "_qf")
        hi_done, lo_done = sem(tag + "_hi"), sem(tag + "_lo")
        q_stored = [sem(f"{tag}_stored{i}") for i in range(2)]
        n_vector, n_scalar, n_tensor, xT_done = norm_and_transpose(nc, sem, tag, S, T, ps_t)
        block = ctx.enter_context(nc.Block())
        steps = [(m, h) for m in range(NK) for h in range(2)]

        @block.sync
        def _(sp):
            sp.dma_start(wq[:], A[f"wT_q{L}"].rearrange("(c p) n -> p c n", p=P)).then_inc(w_in, 16)
            for i, (m, h) in enumerate(steps):
                sp.wait_ge(lo_done, i + 1)
                sp.wait_ge(hi_done, i + 1)
                for part, t in enumerate((q_hi, q_lo)):
                    sp.dma_start(S["Q"][part, m * P:(m + 1) * P, h * HALF:(h + 1) * HALF], t[i % 2][:].bitcast(F32)).then_inc(q_stored[i % 2], 16)
            for i in range(2):
                sp.wait_ge(q_stored[i], 32 * len(steps) // 2)

        @block.tensor
        def _(pe):
            n_tensor(pe)
            pe.wait_ge(xT_done, B)
            pe.wait_ge(w_done, 1)

            def variance(i):
                pe.wait_ge(sq_done, i + 1)
                if i >= 2:
                    pe.wait_ge(ln_done, i - 1)
                nc.tensor.matmul(ps_r[i % 2][:, 0:HALF], S["head_mean"][:], sq[:, i % 2], start=True, stop=True).then_inc(var_done, 1)

            for i, (m, h) in enumerate(steps):
                if i >= 2:
                    pe.wait_ge(qf_done, i - 1)
                for k in range(NK):
                    ins = nc.tensor.matmul(ps_q[i % 2][:, 0:HALF], wq[:, k, m * P:(m + 1) * P],
                                           xT[:, k, h * HALF:(h + 1) * HALF], start=k == 0, stop=k == NK - 1)
                ins.then_inc(q_done, 1)
                if L == 0:
                    variance(i)

        @block.scalar
        def _(act):
            n_scalar(act)
            for i in range(len(steps)):
                if L == 0:
                    act.wait_ge(q_done, i + 1)
                    if i >= 2:
                        act.wait_ge(var_done, i - 1)
                    nc.scalar.activation(sq[:, i % 2], ps_q[i % 2][:, 0:HALF], ACT.Square).then_inc(sq_done, 1)
                    act.wait_ge(var_done, i + 1)
                    if i >= 2:
                        act.wait_ge(qf_done, i - 1)
                    nc.scalar.activation(lnv[:, i % 2], ps_r[i % 2][:, 0:HALF], ACT.Ln, bias=S["eps"][:, 0:1]).then_inc(ln_done, 1)
                    act.wait_ge(ln_done, i + 1)
                    nc.scalar.activation(lnv[:, i % 2], lnv[:, i % 2], ACT.Exp, scale=-0.5).then_inc(rstd_done, 1)
                act.wait_ge(qf_done, i + 1)
                if i >= 2:
                    act.wait_ge(q_stored[i % 2], 32 * (i // 2))
                nc.scalar.copy(q_hi[i % 2][:], qf[:, i % 2]).then_inc(hi_done, 1)

        @block.vector
        def _(dve):
            link = Chain(dve, dch).step
            dve.wait_ge(w_in, 16)
            if L == 0:
                heads = wq[:].rearrange("p c (h d) -> p (c h) d", d=HD)
                link(nc.vector.tensor_reduce(w_mean[:], heads, axis=AX, op=ALU.add))
                link(nc.vector.tensor_scalar(w_mean[:], w_mean[:], 1.0 / HD, None, ALU.mult))
                link(nc.vector.tensor_scalar(gb[:], S["cols"][:, C_LNG:C_LNB + 1], L0_SCALE, None, ALU.mult))
                nc.vector.tensor_tensor(heads, heads, w_mean[:].unsqueeze(2).broadcast_to([P, NK * H, HD]), ALU.subtract).then_inc(w_done, 1)
            else:
                nc.vector.memset(gb[:], 0.0).then_inc(w_done, 1)
            n_vector(dve, link)
            for i, (m, h) in enumerate(steps):
                if i >= 2:
                    dve.wait_ge(hi_done, i - 1)
                    dve.wait_ge(lo_done, i - 1)
                if L == 0:
                    dve.wait_ge(rstd_done, i + 1)
                    link(nc.vector.tensor_tensor(qn[:, i % 2], ps_q[i % 2][:, 0:HALF], lnv[:, i % 2], ALU.mult))
                    nc.vector.tensor_scalar(qf[:, i % 2], qn[:, i % 2], gb[:, 0:1], gb[:, 1:2], ALU.mult, ALU.add).then_inc(qf_done, 1)
                else:
                    dve.wait_ge(q_done, i + 1)
                    nc.vector.tensor_scalar(qf[:, i % 2], ps_q[i % 2][:, 0:HALF], S["cols"][:, C_BQ + m:C_BQ + m + 1], -L1_SCALE,
                                            ALU.add, ALU.mult).then_inc(qf_done, 1)
                dve.wait_ge(hi_done, i + 1)
                if i >= 2:
                    dve.wait_ge(q_stored[i % 2], 32 * (i // 2))
                nc.vector.tensor_tensor(q_lo[i % 2][:], qf[:, i % 2], q_hi[i % 2][:], ALU.subtract).then_inc(lo_done, 1)


def attention(nc, sem, L, A, S):
    tag = f"a{L}"
    with ExitStack() as ctx:
        sb = lambda name, shape, dt=F32: ctx.enter_context(nc.sbuf_tensor(f"{tag}_{name}", shape, dt))
        ps = lambda name, shape: ctx.enter_context(nc.psum_tensor(f"{tag}_{name}", shape, F32))
        k_st = [sb(f"k_st{i}", [P, GH, SK], F32R) for i in range(2)]
        q_st = [sb(f"q_st{i}", [P, GH, SQ], F32R) for i in range(2)]
        v_sb = [sb(f"v{i}", [P, KC, P]) for i in range(2)]
        prob = [sb(f"prob{i}", [SQ, KC * P]) for i in range(2)]
        probT = [sb(f"probT{i}", [P, KC * SQ]) for i in range(2)]
        scored = [sb(f"scored{i}", [SQ, SK]) for i in range(2)] if L else None
        mask_raw = sb("mask_raw", [SQ, SK], I32) if L else None
        masked = sb("masked", [SQ, SK]) if L else None
        nmax = sb("nmax", [SQ, 2])
        wait_here = sb("wait_here", [SQ, 2])
        rsum = sb("rsum", [SQ, 2, GH])
        rinv = sb("rinv", [SQ, GH])
        rep = sb("rep", [SQ, P])
        rinvT = sb("rinvT", [P, SQ])
        psS = [ps(f"s{i}", [P, 1024]) for i in range(2)]
        psT = [ps(f"t{i}", [P, 512]) for i in range(2)]
        psO = [ps(f"o{i}", [P, 512]) for i in range(2)]
        row = slice(KOFF, KOFF + SK)
        HC = KC // 2 * SQ
        loaded = [sem(f"{tag}_loaded{i}") for i in range(2)]
        mask_in, mask_done = sem(tag + "_mask_in"), sem(tag + "_mask_done")
        zeroed = sem(tag + "_zeroed")
        s_done, max_done, exp_done, t_done = sem(tag + "_s"), sem(tag + "_max"), sem(tag + "_exp"), sem(tag + "_t")
        ta_out, tb_out = sem(tag + "_ta"), sem(tag + "_tb")
        pv_done, rinv_done, rep_done = sem(tag + "_pv"), sem(tag + "_rinv"), sem(tag + "_rep")
        rt_done = [sem(f"{tag}_rt{i}") for i in range(2)]
        rinvT_done = sem(tag + "_rinvT")
        normed = [sem(f"{tag}_normed{i}") for i in range(2)]
        bv_done = sem(tag + "_bv")
        block = ctx.enter_context(nc.Block())
        LOADS = 8 + 2

        @block.sync
        def _(sp):
            with sp.Fori(0, B) as b:
                if L:
                    sp.wait_ge(mask_done, b + PRIMED)
                    sp.dma_start(mask_raw[:], A["mask"][bass.ds(b, 1), :].broadcast_to([SQ, SK])).then_inc(mask_in, 16)
                for g in range(NG):
                    i = g % 2
                    sp.wait_ge(rt_done[i], b * 2 + g // 2 + PRIMED)
                    for quad, (qp, kp) in enumerate(((0, 0), (0, 1), (1, 0), (1, 1))):
                        rows = slice(quad * HD, (quad + 1) * HD)
                        sp.dma_start(q_st[i][rows].bitcast(F32), S["Q"][qp, g * P:(g + 1) * P, bass.ds(b * SQ, SQ)]
                                     .rearrange("(h d) t -> d h t", d=HD)).then_inc(loaded[i], 16)
                        sp.dma_start(k_st[i][rows].bitcast(F32), S["K"][L][kp, g * P:(g + 1) * P, b, :]
                                     .rearrange("(h d) t -> d h t", d=HD)).then_inc(loaded[i], 16)
                    sp.dma_start(v_sb[i][:, 0:KC - 1, :], S["V"][L][b, 0:(KC - 1) * P, g * P:(g + 1) * P]
                                 .rearrange("(c p) d -> p c d", p=P)).then_inc(loaded[i], 16)
                    sp.dma_start(v_sb[i][0:KTAIL, KC - 1, :], S["V"][L][b, (KC - 1) * P:SK, g * P:(g + 1) * P]).then_inc(loaded[i], 16)

        @block.tensor
        def _(pe):
            prime(pe, *rt_done)
            with pe.Fori(0, B) as b:
                n0 = b * H

                def scores(i):
                    g = i // GH
                    if i % GH == 0:
                        pe.wait_ge(loaded[g % 2], (b * 2 + g // 2 + 1) * 16 * LOADS)
                    if i >= 2:
                        pe.wait_ge(max_done if L else exp_done, n0 + (i - 1))
                    for col, w, at in key_halves():
                        ins = nc.tensor.matmul(psS[i % 2][0:SQ, at:at + w], q_st[g % 2][:, i % GH, :],
                                               k_st[g % 2][:, i % GH, col:col + w], start=True, stop=True)
                    ins.then_inc(s_done, 1)

                def transposes(i):
                    pe.wait_ge(exp_done, n0 + (i + 1))
                    pe.wait_ge(ta_out, n0 + i + PRIMED)
                    pe.wait_ge(tb_out, n0 + i + PRIMED)
                    for c in range(KC):
                        at = c % (KC // 2) * SQ
                        ins = nc.tensor.transpose(psT[c // (KC // 2)][:, at:at + SQ], prob[i % 2][:, c * P:(c + 1) * P],
                                                  S["ident"][0:SQ, 0:SQ])
                    ins.then_inc(t_done, 1)

                def values(i):
                    g, j = divmod(i, GH)
                    pe.wait_ge(ta_out, n0 + (i + 1) + PRIMED)
                    pe.wait_ge(tb_out, n0 + (i + 1) + PRIMED)
                    if j == 0:
                        pe.wait_ge(normed[g % 2], b * 2 + g // 2 + PRIMED)
                    for c in range(KC):
                        w = chunk_rows(c)
                        ins = nc.tensor.matmul(psO[g % 2][j * HD:(j + 1) * HD, 0:SQ], v_sb[g % 2][0:w, c, j * HD:(j + 1) * HD],
                                               probT[i % 2][0:w, c * SQ:(c + 1) * SQ], start=c == 0, stop=c == KC - 1)
                    ins.then_inc(pv_done, 1)
                    if j == GH - 1:
                        pe.wait_ge(rep_done, b * NG + (g + 1))
                        nc.tensor.transpose(psO[g % 2][:, P:P + SQ], rep[:], S["ident"][0:SQ, 0:SQ]).then_inc(rt_done[g % 2], 1)

                pe.wait_ge(zeroed, 2)
                scores(0)
                for i in range(H):
                    if i + 1 < H:
                        scores(i + 1)
                    transposes(i)
                    if i:
                        values(i - 1)
                values(H - 1)

        @block.scalar
        def _(act):
            prime(act, tb_out)
            with act.Fori(0, B) as b:
                n0 = b * H

                def second_half(i):
                    act.wait_ge(t_done, n0 + (i + 1))
                    if i >= 2:
                        act.wait_ge(pv_done, n0 + (i - 1))
                    nc.scalar.copy(probT[i % 2][:, HC:], psT[1][:, 0:HC]).then_inc(tb_out, 1)

                for i in range(H):
                    g = i // GH
                    act.wait_ge(max_done, n0 + (i + 1))
                    if i >= 2:
                        act.wait_ge(t_done, n0 + (i - 1))
                    if g >= 2 and i % GH == 0:
                        act.wait_ge(rinv_done, b * NG + (g - 1))
                    if L:
                        nc.scalar.activation(prob[i % 2][:, 0:SK], scored[i % 2][:], ACT.Exp, bias=nmax[:, i % 2:i % 2 + 1], scale=-1.0,
                                             accum_out=rsum[:, g % 2, i % GH:i % GH + 1]).then_inc(exp_done, 1)
                    else:
                        nc.scalar.activation(prob[i % 2][:, 0:SK], psS[i % 2][0:SQ, row], ACT.Exp, bias=nmax[:, i % 2:i % 2 + 1],
                                             accum_out=rsum[:, g % 2, i % GH:i % GH + 1]).then_inc(exp_done, 1)
                    if i:
                        second_half(i - 1)
                second_half(H - 1)

        @block.vector
        def _(dve):
            prime(dve, mask_done, ta_out, *normed)
            for t in prob:
                nc.vector.memset(t[:, SK:], 0.0).then_inc(zeroed, 1)
            with dve.Fori(0, B) as b:
                n0 = b * H
                if L:
                    dve.wait_ge(mask_in, (b + 1) * 16)
                    nc.vector.tensor_scalar(masked[:], mask_raw[:], 0.0, NEG, ALU.is_equal, ALU.mult).then_inc(mask_done, 1)
                    dve.wait_ge(mask_done, b + 1 + PRIMED)

                def row_max(i):
                    dve.wait_ge(s_done, n0 + (i + 1))
                    if i >= 2:
                        dve.wait_ge(exp_done, n0 + (i - 1))
                    out = nmax[:, i % 2:i % 2 + 1]
                    if L:
                        nc.vector.memset(wait_here[:, i % 2:i % 2 + 1], 0.0)
                        nc.vector.tensor_tensor_reduce(out=scored[i % 2][:], in0=psS[i % 2][0:SQ, row], in1=masked[:], scale=1.0,
                                                       scalar=3.0e38, op0=ALU.add, op1=ALU.min, accum_out=out).then_inc(max_done, 1)
                    else:
                        nc.vector.tensor_reduce(out, psS[i % 2][0:SQ, row], axis=AX, op=ALU.max, negate=True).then_inc(max_done, 1)

                def first_half(i):
                    dve.wait_ge(t_done, n0 + (i + 1))
                    if i >= 2:
                        dve.wait_ge(pv_done, n0 + (i - 1))
                    nc.vector.tensor_copy(probT[i % 2][:, 0:HC], psT[0][:, 0:HC]).then_inc(ta_out, 1)

                def reciprocal_sums(g):
                    G = b * NG + g
                    dve.wait_ge(exp_done, n0 + (g + 1) * GH)
                    nc.vector.reciprocal(rinv[:], rsum[:, g % 2, :]).then_inc(rinv_done, 1)
                    dve.wait_ge(rinv_done, G + 1)
                    nc.vector.tensor_copy(rep[:].rearrange("p (h d) -> p h d", h=GH),
                                          rinv[:].unsqueeze(2).broadcast_to([SQ, GH, HD])).then_inc(rep_done, 1)

                def normalise(g):
                    G = b * NG + g
                    dve.wait_ge(rt_done[g % 2], b * 2 + (g // 2 + 1) + PRIMED)
                    nc.vector.tensor_copy(rinvT[:], psO[g % 2][:, P:P + SQ]).then_inc(rinvT_done, 1)
                    dve.wait_ge(rinvT_done, G + 1)
                    nc.vector.tensor_tensor(S["attnT"][:, g, bass.ds(b * SQ, SQ)], psO[g % 2][:, 0:SQ], rinvT[:], ALU.mult)\
                        .then_inc(normed[g % 2], 1)

                for i in range(H):
                    row_max(i)
                    if i:
                        first_half(i - 1)
                    if i and i % GH == 0:
                        reciprocal_sums(i // GH - 1)
                    if i > GH and i % GH == 2:
                        normalise(i // GH - 1)
                first_half(H - 1)
                reciprocal_sums(NG - 1)
                normalise(NG - 1)
            if L:
                for i in range(2):
                    dve.wait_ge(normed[i], B * NG // 2 + PRIMED)
                for k in range(NK):
                    nc.vector.tensor_scalar(S["attnT"][:, k, :], S["attnT"][:, k, :], S["cols"][:, C_BV + k:C_BV + k + 1], None, ALU.add)\
                        .then_inc(bv_done, 1)


def output(nc, sem, L, A, S):
    tag = f"o{L}"
    with ExitStack() as ctx:
        sb = lambda name, shape, dt=F32: ctx.enter_context(nc.sbuf_tensor(f"{tag}_{name}", shape, dt))
        wo, bias, t = sb("wo", [P, NK, D]), sb("bias", [SQ, D]), sb("t", [SQ, 2, D])
        psY = [ctx.enter_context(nc.psum_tensor(f"{tag}_y{i}", [P, 512], F32)) for i in range(B)]
        w_in, y_done, dch, x_done = sem(tag + "_w_in"), sem(tag + "_y"), sem(tag + "_dch"), sem(tag + "_x")
        block = ctx.enter_context(nc.Block())

        @block.sync
        def _(sp):
            sp.dma_start(wo[:], A[f"wT_o{L}"].rearrange("(c p) n -> p c n", p=P)).then_inc(w_in, 16)
            sp.dma_start(bias[:], A[f"bo{L}"].broadcast_to([SQ, D])).then_inc(w_in, 16)

        @block.tensor
        def _(pe):
            pe.wait_ge(w_in, 32)
            for b in range(B):
                for k in range(NK):
                    ins = nc.tensor.matmul(psY[b][0:SQ, :], S["attnT"][:, k, b * SQ:(b + 1) * SQ], wo[:, k, :], start=k == 0, stop=k == NK - 1)
                ins.then_inc(y_done, 1)

        @block.vector
        def _(dve):
            link = Chain(dve, dch).step
            dve.wait_ge(w_in, 32)
            for b in range(B):
                dve.wait_ge(y_done, b + 1)
                link(nc.vector.tensor_tensor(t[:, b % 2], psY[b][0:SQ, :], bias[:], ALU.add))
                nc.vector.scalar_tensor_tensor(S["x"][:, b, :], t[:, b % 2], S["gates"][0:SQ, L:L + 1], S["x"][:, b, :],
                                               ALU.mult, ALU.add).then_inc(x_done, 1)
            dve.wait_ge(x_done, B)


def top_k(nc, link, vals, n, k, mx, gt, eq, ca, cb, cnt, sel):
    for b in range(B):
        ins = nc.vector.max(mx[:, b, :], vals[:, b, :])
    link(ins)
    thr = mx[:, :, k - 1:k].broadcast_to([SQ, B, n])
    nc.vector.tensor_tensor(gt, vals, thr, ALU.is_gt)
    link(nc.vector.tensor_tensor(eq, vals, thr, ALU.is_equal))
    src, dst, d = eq, ca, 1
    while d < n:
        nc.vector.tensor_copy(dst[:, :, 0:d], src[:, :, 0:d])
        link(nc.vector.tensor_tensor(dst[:, :, d:n], src[:, :, d:n], src[:, :, 0:n - d], ALU.add))
        src, dst, d = dst, (cb if dst is ca else ca), 2 * d
    link(nc.vector.tensor_reduce(cnt, gt, axis=AX, op=ALU.add))
    link(nc.vector.tensor_tensor(dst, src, cnt.unsqueeze(2).broadcast_to([SQ, B, n]), ALU.add))
    link(nc.vector.scalar_tensor_tensor(dst, dst, float(k), eq, ALU.is_le, ALU.mult))
    link(nc.vector.tensor_tensor(sel, dst, gt, ALU.add))


def experts_0(nc, sem, A, S):
    tag = "f0"
    HALF = NT // 2
    with ExitStack() as ctx:
        sb = lambda name, shape, dt=F32: ctx.enter_context(nc.sbuf_tensor(f"{tag}_{name}", shape, dt))
        T = norm_tiles(sb)
        xT = T["xT"]
        gate_w, e_bias = sb("gate_w", [P, NK, E0]), sb("e_bias", [SQ, E0])
        big = [SQ, B, E0]
        sc, sfc, gt, eq, ca, cb, sel = (sb(n, big) for n in ("sc", "sfc", "gt", "eq", "ca", "cb", "sel"))
        small = [SQ, B, GRP0]
        gmx, gsc, gsel, mx = sb("gmx", small), sb("gsc", small), sb("gsel", small), sb("mx", [SQ, B, 8])
        cnt = sb("cnt", [SQ, B])
        comb = sb("comb", [SQ, B, ES])
        gu = [sb(f"gu{i}", [P, NK, 2 * I0]) for i in range(2)]
        dn = [sb(f"dn{i}", [P, I0 // P, D]) for i in range(2)]
        sg = sb("sg", [P, 2, HALF])
        hT = [sb(f"hT{i}", [P, I0 // P, NT]) for i in range(2)]
        acc = sb("acc", [SQ, B, D])
        ps = [ctx.enter_context(nc.psum_tensor(f"{tag}_p{i}", [P, 512], F32)) for i in range(8)]
        r_in, gu_in = sem(tag + "_r_in"), [sem(f"{tag}_w_in{i}") for i in range(2)]
        logit_done, e_done, comb_done, dch = sem(tag + "_logit"), sem(tag + "_e"), sem(tag + "_comb"), sem(tag + "_dch")
        gu_done, sg_done, h_done, acc_done = (sem(f"{tag}_{n}") for n in ("gu", "sg", "h", "acc"))
        y_done = [sem(f"{tag}_y{i}") for i in range(2)]
        x_done = sem(tag + "_x")
        n_vector, n_scalar, n_tensor, xT_done = norm_and_transpose(nc, sem, tag, S, T, ps[0:2])
        block = ctx.enter_context(nc.Block())
        units = [(h, j) for h in range(2) for j in range(I0 // P)]
        NU = len(units)

        @block.sync
        def _(sp):
            sp.dma_start(gate_w[:], A["gateT0"].rearrange("(c p) n -> p c n", p=P)).then_inc(r_in, 16)
            sp.dma_start(e_bias[:], A["e_bias"].broadcast_to([SQ, E0])).then_inc(r_in, 16)
            with sp.Fori(0, ES // 2) as it:
                for i in range(2):
                    e = it * 2 + i
                    sp.wait_ge(y_done[i], it * B + PRIMED)
                    sp.dma_start(gu[i][:], A["gu"][e]).then_inc(gu_in[i], 16)
                    sp.dma_start(dn[i][:], A["dn"][e]).then_inc(gu_in[i], 16)

        @block.tensor
        def _(pe):
            prime(pe, *y_done)
            n_tensor(pe)
            pe.wait_ge(xT_done, B)
            pe.wait_ge(r_in, 32)
            for b in range(B):
                for k in range(NK):
                    ins = nc.tensor.matmul(ps[2][0:SQ, b * E0:(b + 1) * E0], xT[:, k, b * SQ:(b + 1) * SQ], gate_w[:, k, :],
                                           start=k == 0, stop=k == NK - 1)
            ins.then_inc(logit_done, 1)
            pe.wait_ge(e_done, 1)
            with pe.Fori(0, ES // 2) as it:
                for i in range(2):
                    e = it * 2 + i
                    pe.wait_ge(gu_in[i], (it + 1) * 32)
                    for u, (h, j) in enumerate(units):
                        pe.wait_ge(h_done, PRIMED + (e * NU + (u - 2) + 1 if u >= 2 else e * NU))
                        for which in range(2):
                            bank = ps[(u % 2) * 2 + which]
                            for k in range(NK):
                                ins = nc.tensor.matmul(bank[:, 0:HALF], gu[i][:, k, which * I0 + j * P:which * I0 + (j + 1) * P],
                                                       xT[:, k, h * HALF:(h + 1) * HALF], start=k == 0, stop=k == NK - 1)
                            ins.then_inc(gu_done, 1)
                    for b in range(B):
                        if b == 0:
                            pe.wait_ge(h_done, e * NU + NU + PRIMED)
                        pe.wait_ge(acc_done, PRIMED + (e * B + (b - 4) + 1 if b >= 4 else e * B))
                        for j in range(I0 // P):
                            ins = nc.tensor.matmul(ps[4 + b % 4][0:SQ, :], hT[i][:, j, b * SQ:(b + 1) * SQ], dn[i][:, j, :],
                                                   start=j == 0, stop=j == I0 // P - 1)
                        ins.then_inc(y_done[i], 1)

        @block.scalar
        def _(act):
            n_scalar(act)
            act.wait_ge(logit_done, 1)
            nc.scalar.activation(sc[:], ps[2][0:SQ, 0:B * E0].rearrange("p (b e) -> p b e", b=B), ACT.Exp, scale=-1.0).then_inc(e_done, 1)
            with act.Fori(0, ES // 2) as it:
                for i in range(2):
                    e = it * 2 + i
                    for u, (h, j) in enumerate(units):
                        act.wait_ge(gu_done, (e * NU + u) * 2 + 1)
                        act.wait_ge(h_done, PRIMED + (e * NU + (u - 1) if u >= 1 else e * NU))
                        nc.scalar.activation(sg[:, u % 2], ps[(u % 2) * 2][:, 0:HALF], ACT.Silu).then_inc(sg_done, 1)

        @block.vector
        def _(dve):
            prime(dve, h_done, acc_done)
            link = Chain(dve, dch).step
            n_vector(dve, link)
            link(nc.vector.memset(acc[:], 0.0))
            dve.wait_ge(e_done, 1)
            dve.wait_ge(r_in, 32)
            link(nc.vector.tensor_scalar(sc[:], sc[:], 1.0, None, ALU.add))
            link(nc.vector.reciprocal(sc[:], sc[:]))
            link(nc.vector.tensor_tensor(sfc[:], sc[:], e_bias[:].unsqueeze(1).broadcast_to(big), ALU.add))
            gs = E0 // GRP0
            link(nc.vector.tensor_reduce(gsc[:], sfc[:].rearrange("p b (g s) -> p b g s", s=gs), axis=AX, op=ALU.max))
            g8 = lambda t: t[:, :, 0:GRP0]
            top_k(nc, link, gsc[:], GRP0, TOPG0, mx, g8(gt), g8(eq), g8(ca), g8(cb), cnt[:], gsel[:])
            link(nc.vector.tensor_tensor(sfc[:].rearrange("p b (g s) -> p (b g) s", s=gs), sfc[:].rearrange("p b (g s) -> p (b g) s", s=gs),
                                         gsel[:].rearrange("p b g -> p (b g)").unsqueeze(2).broadcast_to([SQ, B * GRP0, gs]), ALU.mult))
            top_k(nc, link, sfc[:], E0, TOP0, mx, gt[:], eq[:], ca[:], cb[:], cnt[:], sel[:])
            link(nc.vector.tensor_tensor(sel[:], sel[:], sc[:], ALU.mult))
            link(nc.vector.tensor_reduce(cnt[:], sel[:], axis=AX, op=ALU.add))
            link(nc.vector.tensor_scalar(cnt[:], cnt[:], 1e-20, None, ALU.add))
            link(nc.vector.reciprocal(cnt[:], cnt[:]))
            link(nc.vector.tensor_scalar(cnt[:], cnt[:], W0_SCALE, None, ALU.mult))
            nc.vector.memset(comb[:, :, E0:], 1.0)
            link(nc.vector.tensor_tensor(comb[:, :, 0:E0], sel[:], cnt[:].unsqueeze(2).broadcast_to(big), ALU.mult))
            with dve.Fori(0, ES // 2) as it:
                for i in range(2):
                    e = it * 2 + i
                    for u, (h, j) in enumerate(units):
                        dve.wait_ge(sg_done, e * NU + u + 1)
                        dve.wait_ge(gu_done, (e * NU + u) * 2 + 2)
                        nc.vector.tensor_tensor(hT[i][:, j, h * HALF:(h + 1) * HALF], sg[:, u % 2], ps[(u % 2) * 2 + 1][:, 0:HALF],
                                                ALU.mult).then_inc(h_done, 1)
                    for b in range(B):
                        dve.wait_ge(y_done[i], it * B + (b + 1) + PRIMED)
                        dve.wait_ge(acc_done, e * B + PRIMED)
                        nc.vector.scalar_tensor_tensor(acc[:, b, :], ps[4 + b % 4][0:SQ, :], comb[:, b, bass.ds(e, 1)], acc[:, b, :],
                                                       ALU.mult, ALU.add).then_inc(acc_done, 1)
            dve.wait_ge(acc_done, ES * B + PRIMED)
            for b in range(B):
                nc.vector.scalar_tensor_tensor(S["x"][:, b, :], acc[:, b, :], S["gates"][0:SQ, 2:3], S["x"][:, b, :],
                                               ALU.mult, ALU.add).then_inc(x_done, 1)
            dve.wait_ge(x_done, B)


def experts_1(nc, sem, A, S, out):
    tag = "f1"
    HALF = NT // 2
    with ExitStack() as ctx:
        sb = lambda name, shape, dt=F32: ctx.enter_context(nc.sbuf_tensor(f"{tag}_{name}", shape, dt))
        T = norm_tiles(sb)
        xT = T["xT"]
        gate_w = sb("gate_w", [P, NK, E1])
        wg = sb("wg", [P, NK, HID1])
        sh = [SQ, B, E1]
        lg, gt, eq, ca, cb, sel, mx, tot = (sb(n, sh) for n in ("lg", "gt", "eq", "ca", "cb", "sel", "mx", "tot"))
        cnt = sb("cnt", [SQ, B])
        hid = sb("hid", [P, NI1, NT])
        wd = [sb(f"wd{i}", [P, NI1, D]) for i in range(2)]
        acc = sb("acc", [SQ, B, D])
        ps = [ctx.enter_context(nc.psum_tensor(f"{tag}_p{i}", [P, 512], F32)) for i in range(8)]
        r_in, g_in, wd_in = sem(tag + "_r_in"), sem(tag + "_g_in"), [sem(f"{tag}_wd_in{i}") for i in range(2)]
        logit_done, l_out, sel_done, pos_done, dch = (sem(f"{tag}_{n}") for n in ("logit", "lout", "sel", "pos", "dch"))
        g_done, hid_done, acc_done, x_done, stored = (sem(f"{tag}_{n}") for n in ("g", "hid", "acc", "x", "stored"))
        y_done = [sem(f"{tag}_y{i}") for i in range(2)]
        lm_done, ex_done = sem(tag + "_lm"), sem(tag + "_ex")
        n_vector, n_scalar, n_tensor, xT_done = norm_and_transpose(nc, sem, tag, S, T, ps[0:2])
        block = ctx.enter_context(nc.Block())

        @block.sync
        def _(sp):
            sp.dma_start(gate_w[:], A["routerT1"].rearrange("(c p) n -> p c n", p=P)).then_inc(r_in, 16)
            sp.dma_start(wg[:], A["wgT1"].rearrange("(c p) n -> p c n", p=P)).then_inc(g_in, 16)
            with sp.Fori(0, E1 // 2) as it:
                for i in range(2):
                    sp.wait_ge(y_done[i], it * B + PRIMED)
                    sp.dma_start(wd[i][:], A["wd1"][it * 2 + i]).then_inc(wd_in[i], 16)
            for b in range(B):
                sp.wait_ge(x_done, b + 1)
                sp.dma_start(out[b], S["x"][:, b, :]).then_inc(stored, 16)
            sp.wait_ge(stored, 16 * B)

        @block.tensor
        def _(pe):
            prime(pe, *y_done)
            n_tensor(pe)
            pe.wait_ge(xT_done, B)
            pe.wait_ge(r_in, 16)
            for b in range(B):
                for k in range(NK):
                    ins = nc.tensor.matmul(ps[2][0:SQ, b * E1:(b + 1) * E1], xT[:, k, b * SQ:(b + 1) * SQ], gate_w[:, k, :],
                                           start=k == 0, stop=k == NK - 1)
            ins.then_inc(logit_done, 1)
            pe.wait_ge(g_in, 16)
            for u in range(2 * NI1):
                m, h = divmod(u, 2)
                if u >= 2:
                    pe.wait_ge(hid_done, u - 1)
                for k in range(NK):
                    ins = nc.tensor.matmul(ps[u % 2][:, 0:HALF], wg[:, k, m * P:(m + 1) * P], xT[:, k, h * HALF:(h + 1) * HALF],
                                           start=k == 0, stop=k == NK - 1)
                ins.then_inc(g_done, 1)
            pe.wait_ge(sel_done, 1)
            nc.tensor.matmul(ps[3][0:SQ, 0:B * E1], S["upto"][:], sel[:].rearrange("p b e -> p (b e)"), start=True, stop=True)
            nc.tensor.matmul(ps[2][0:SQ, 0:B * E1], S["ones"][:], sel[:].rearrange("p b e -> p (b e)"), start=True, stop=True).then_inc(pos_done, 1)
            pe.wait_ge(hid_done, 2 * NI1)
            with pe.Fori(0, E1 // 2) as it:
                for i in range(2):
                    e = it * 2 + i
                    pe.wait_ge(wd_in[i], (it + 1) * 16)
                    for b in range(B):
                        pe.wait_ge(acc_done, PRIMED + (e * B + (b - 4) + 1 if b >= 4 else e * B))
                        for j in range(NI1):
                            ins = nc.tensor.matmul(ps[4 + b % 4][0:SQ, :], hid[:, j, b * SQ:(b + 1) * SQ], wd[i][:, j, :],
                                                   start=j == 0, stop=j == NI1 - 1)
                        ins.then_inc(y_done[i], 1)

        @block.scalar
        def _(act):
            n_scalar(act)
            act.wait_ge(lm_done, 1)
            nc.scalar.activation(lg[:], lg[:], ACT.Exp).then_inc(ex_done, 1)
            for u in range(2 * NI1):
                m, h = divmod(u, 2)
                act.wait_ge(g_done, u + 1)
                nc.scalar.activation(hid[:, m, h * HALF:(h + 1) * HALF], ps[u % 2][:, 0:HALF], ACT.Silu).then_inc(hid_done, 1)

        @block.vector
        def _(dve):
            prime(dve, acc_done)
            link = Chain(dve, dch).step
            n_vector(dve, link)
            link(nc.vector.memset(acc[:], 0.0))
            dve.wait_ge(logit_done, 1)
            link(nc.vector.tensor_copy(lg[:], ps[2][0:SQ, 0:B * E1].rearrange("p (b e) -> p b e", b=B)))
            link(nc.vector.tensor_reduce(cnt[:], lg[:], axis=AX, op=ALU.max))
            nc.vector.tensor_tensor(lg[:], lg[:], cnt[:].unsqueeze(2).broadcast_to(sh), ALU.subtract).then_inc(lm_done, 1)
            dve.wait_ge(ex_done, 1)
            link(nc.vector.tensor_reduce(cnt[:], lg[:], axis=AX, op=ALU.add))
            link(nc.vector.reciprocal(cnt[:], cnt[:]))
            link(nc.vector.tensor_tensor(lg[:], lg[:], cnt[:].unsqueeze(2).broadcast_to(sh), ALU.mult))
            top_k(nc, link, lg[:], E1, TOP1, mx, gt[:], eq[:], ca[:], cb[:], cnt[:], sel[:])
            nc.vector.tensor_copy(gt[:], sel[:]).then_inc(sel_done, 1)
            dve.wait_ge(pos_done, 1)
            link(nc.vector.tensor_copy(ca[:], ps[3][0:SQ, 0:B * E1].rearrange("p (b e) -> p b e", b=B)))
            link(nc.vector.tensor_copy(tot[:], ps[2][0:SQ, 0:B * E1].rearrange("p (b e) -> p b e", b=B)))
            for b in range(1, B):
                link(nc.vector.tensor_tensor(ca[:, b:, :], ca[:, b:, :], tot[:, b - 1:b, :].broadcast_to([SQ, B - b, E1]), ALU.add))
            link(nc.vector.scalar_tensor_tensor(sel[:], ca[:], float(CAP1), sel[:], ALU.is_le, ALU.mult))
            link(nc.vector.tensor_tensor(sel[:], sel[:], lg[:], ALU.mult))
            link(nc.vector.tensor_reduce(cnt[:], sel[:], axis=AX, op=ALU.add))
            link(nc.vector.tensor_scalar(cnt[:], cnt[:], 1e-6, None, ALU.add))
            link(nc.vector.reciprocal(cnt[:], cnt[:]))
            link(nc.vector.tensor_tensor(sel[:], sel[:], cnt[:].unsqueeze(2).broadcast_to(sh), ALU.mult))
            with dve.Fori(0, E1 // 2) as it:
                for i in range(2):
                    e = it * 2 + i
                    for b in range(B):
                        dve.wait_ge(y_done[i], it * B + (b + 1) + PRIMED)
                        dve.wait_ge(acc_done, e * B + PRIMED)
                        nc.vector.scalar_tensor_tensor(acc[:, b, :], ps[4 + b % 4][0:SQ, :], sel[:, b, bass.ds(e, 1)], acc[:, b, :],
                                                       ALU.mult, ALU.add).then_inc(acc_done, 1)
            dve.wait_ge(acc_done, E1 * B + PRIMED)
            for b in range(B):
                nc.vector.scalar_tensor_tensor(S["x"][:, b, :], acc[:, b, :], S["gates"][0:SQ, 3:4], S["x"][:, b, :],
                                               ALU.mult, ALU.add).then_inc(x_done, 1)


def setup(nc, sem, A, S):
    x_in, c_in, g_done = sem("st_x_in"), sem("st_c_in"), sem("st_g")
    z_done, c_done = sem("st_z"), sem("st_c")
    with nc.Block() as block:
        @block.sync
        def _(sp):
            sp.dma_start(S["cols"][:], A["cols"]).then_inc(c_in, 16)
            sp.dma_start(S["x"][:], A["x"].rearrange("b t d -> t b d")).then_inc(x_in, 16)
            sp.wait_ge(x_in, 16)

        @block.scalar
        def _(act):
            act.wait_ge(c_in, 16)
            nc.scalar.activation(S["gates"][:], S["cols"][:, C_GX:C_GX + 4], ACT.Tanh).then_inc(g_done, 1)
            act.wait_ge(g_done, 1)

        @block.vector
        def _(dve):
            nc.vector.memset(S["eps"][:], LN_EPS).then_inc(z_done, 1)
            nc.vector.memset(S["ident"][:], 0.0).then_inc(z_done, 1)
            nc.vector.memset(S["ones"][:], 1.0).then_inc(z_done, 1)
            nc.vector.memset(S["upto"][:], 1.0).then_inc(z_done, 1)
            nc.vector.memset(S["head_mean"][:], 0.0).then_inc(z_done, 1)
            dve.wait_ge(z_done, 5)
            for j in range(GH):
                nc.vector.memset(S["head_mean"][j * HD:(j + 1) * HD, j * HD:(j + 1) * HD], 1.0 / HD).then_inc(c_done, 1)

        @block.gpsimd
        def _(pool):
            pool.wait_ge(z_done, 4)
            nc.gpsimd.affine_select(out=S["ident"][:], in_=S["ident"][:], compare_op=ALU.not_equal, fill=1.0, base=0,
                                    pattern=[[-1, P]], channel_multiplier=1).then_inc(c_done, 1)
            nc.gpsimd.affine_select(out=S["upto"][:], in_=S["upto"][:], compare_op=ALU.is_ge, fill=0.0, base=0,
                                    pattern=[[1, SQ]], channel_multiplier=-1).then_inc(c_done, 1)
            pool.wait_ge(c_done, 2 + GH)


def build(nc, A, out):
    with ExitStack() as ctx:
        sb = lambda name, shape, dt=F32: ctx.enter_context(nc.sbuf_tensor(name, shape, dt))
        layer_sems = []

        def sem(name):
            layer_sems.append(nc.alloc_semaphore(name=name))
            return layer_sems[-1]

        dram = lambda name, shape, dt: nc.dram_tensor(name, shape, dt, kind="Internal").ap()
        S = {
            "x": sb("x_sb", [SQ, B, D]), "cols": sb("cols_sb", [P, NCOLS]), "gates": sb("gates", [P, 4]),
            "ident": sb("ident", [P, P]), "head_mean": sb("head_mean", [P, P]), "eps": sb("eps", [P, 1]),
            "ones": sb("ones", [SQ, SQ]), "upto": sb("upto", [SQ, SQ]), "attnT": sb("attnT", [P, NK, NT]),
            "K": [dram(f"scr_k{L}", [2, D, B, SK], F32) for L in range(2)],
            "V": [dram(f"scr_v{L}", [B, SK, D], F32) for L in range(2)],
            "Q": dram("scr_q", [2, D, NT], F32),
        }
        setup(nc, sem, A, S)
        project_context(nc, sem, A, S)
        for L in range(2):
            queries(nc, sem, L, A, S)
            attention(nc, sem, L, A, S)
            output(nc, sem, L, A, S)
            if L == 0:
                experts_0(nc, sem, A, S)
                nc.clear_and_free_semaphores(layer_sems)
                layer_sems.clear()
                nc.all_engine_barrier()
            else:
                experts_1(nc, sem, A, S, out)


def lay_out(i):
    import numpy as np
    i = {k: np.asarray(v) for k, v in i.items()}
    a = {}
    ctxT = i["ctx_1024"].reshape(B, SK, NK, P).transpose(0, 3, 2, 1)
    a["ctxT"] = np.concatenate([ctxT, np.zeros((1, P, NK, SK), ctxT.dtype)])
    a["x"] = i["x"]
    a["mask"] = i["mask_Bx1x1xS2_ik0"].reshape(B, SK)
    for L in range(2):
        for n in "qkv":
            a[f"wT_{n}{L}"] = i[f"L{L}_xattn_W{n}"].T
    a["wT_o0"], a["wT_o1"] = i["L0_xattn_Wp"].T, i["L1_xattn_Wo"].T
    a["bo0"], a["bo1"] = i["L0_xattn_bp"].reshape(1, D), i["L1_xattn_bo"].reshape(1, D)
    col = lambda v: v.reshape(NK, P).T
    a["cols"] = np.concatenate([np.tile(i["L0_xattn_ln_g"], GH)[:, None], np.tile(i["L0_xattn_ln_b"], GH)[:, None],
                                col(i["L1_xattn_bk"]), col(i["L1_xattn_bq"]), col(i["L1_xattn_bv"]),
                                np.tile(i["g_xattn"], (P, 1)), np.tile(i["g_ffn"], (P, 1))], axis=1)
    a["gateT0"] = i["L0_ffn_gate_weight"].T
    a["e_bias"] = i["L0_ffn_e_score_correction_bias"].reshape(1, E0)
    shared_gu = np.concatenate([i["L0_ffn_shared_gate_w"].reshape(2, I0, D), i["L0_ffn_shared_up_w"].reshape(2, I0, D)], axis=1)
    gu = np.concatenate([i["L0_ffn_experts_gate_up"], shared_gu])
    a["gu"] = gu.reshape(ES, 2 * I0, NK, P).transpose(0, 3, 2, 1)
    dn = np.concatenate([i["L0_ffn_experts_down"], i["L0_ffn_shared_down_w"].reshape(D, 2, I0).transpose(1, 0, 2)])
    a["dn"] = dn.reshape(ES, D, I0 // P, P).transpose(0, 3, 2, 1)
    a["routerT1"] = i["L1_ffn_w_router"].T
    a["wgT1"] = i["L1_ffn_w_gate"].T
    a["wd1"] = i["L1_ffn_w_down"].reshape(E1, D, NI1, P).transpose(0, 3, 2, 1)
    return {k: np.ascontiguousarray(v) for k, v in a.items()}


def kernel(**inputs):
    import concourse.bacc as bacc
    from concourse.bass_utils import run_bass_kernel_spmd
    arrays = lay_out(inputs)
    nc = bacc.Bacc("TRN2", target_bir_lowering=False, num_devices=1)
    A = {k: nc.dram_tensor(f"in_{k}", list(v.shape), mybir.dt.from_np(v.dtype), kind="ExternalInput").ap() for k, v in arrays.items()}
    out = nc.dram_tensor("out_0", [B, SQ, D], F32, kind="ExternalOutput").ap()
    build(nc, A, out)
    r = run_bass_kernel_spmd(nc, [{f"in_{k}": v for k, v in arrays.items()}], core_ids=[0])
    return r.results[0]["out_0"]
```

```python
from contextlib import ExitStack

import concourse.bass as bass
from concourse import mybir

F32 = mybir.dt.float32
F32R = mybir.dt.float32r
I32 = mybir.dt.int32
ALU = mybir.AluOpType
ACT = mybir.ActivationFunctionType
AX = mybir.AxisListType.X

P = 128
B, SQ, SK, D = 8, 100, 722, 512
NT = B * SQ
NK = D // P
H = 16
HD = D // H
GH = P // HD
NG = H // GH
KC = -(-SK // P)
KTAIL = SK - (KC - 1) * P
KHALF = (362, 360)
KOFF = 512 - KHALF[0]
LN_EPS = 1e-5
L0_SCALE = 8.0 / HD
L1_SCALE = float(1.0 / (HD ** 0.5))
NEG = 1e9
E0, I0, TOP0, GRP0, TOPG0 = 32, 256, 6, 8, 4
MB0 = (NT * TOP0 + E0 * (P - 1)) // P
W0_SCALE = 2.5
E1, HID1, TOP1 = 8, 1024, 2
NI1 = HID1 // P
CAP1 = -(-NT * 5 // (E1 * 4))
C_LNG, C_LNB, C_BK, C_BQ, C_BV, C_GX, C_GF = 0, 1, 2, 6, 10, 14, 16
NCOLS = 18


PRIMED = 1


def prime(eng, *sems):
    for s in sems:
        eng.sem_inc(s, PRIMED)


class Chain:

    def __init__(self, eng, sem):
        self.eng, self.sem, self.n = eng, sem, 0

    def step(self, ins):
        self.n += 1
        ins.then_inc(self.sem, 1)
        self.eng.wait_ge(self.sem, self.n)


def key_halves():
    return ((0, KHALF[0], KOFF), (KHALF[0], KHALF[1], 512))


def chunk_rows(c):
    return P if c < KC - 1 else KTAIL


def project_context(nc, sem, A, S):
    with ExitStack() as ctx:
        sb = lambda name, shape, dt=F32: ctx.enter_context(nc.sbuf_tensor(name, shape, dt))
        ps = lambda name, shape: ctx.enter_context(nc.psum_tensor(name, shape, F32))
        w_names = ("k0", "k1", "v0", "v1")
        w_raw = sb("w_raw", [P, 2, NK, D])
        w_hi = {n: sb("w_hi_" + n, [P, NK, D], F32R) for n in w_names}
        w_lo = {n: sb("w_lo_" + n, [P, NK, D], F32R) for n in w_names}
        w_mean = sb("w_mean", [P, NK * H])
        ctx_raw = sb("ctx_raw", [P, NK, SK])
        ctx_hi = [sb(f"ctx_hi{i}", [P, NK, SK], F32R) for i in range(2)]
        ctx_lo = [sb(f"ctx_lo{i}", [P, NK, SK], F32R) for i in range(2)]
        mask_raw = sb("mask_raw", [P, SK], I32)
        keep = sb("keep", [P, SK])
        sq = sb("sq", [P, SK])
        lnv = sb("lnv", [P, SK])
        k0n = sb("k0n", [P, SK])
        k0f = sb("k0f", [P, SK])
        k1f = sb("k1f", [P, SK])
        kst = [[sb(f"kst{L}_{part}", [P, SK], F32R) for part in "hl"] for L in range(2)]
        vst = sb("vst", [P, 2, D])
        head_mean = S["head_mean"]
        psK = [ps(f"psK{L}", [P, 1024]) for L in range(2)]
        psR = ps("psR", [P, 1024])
        psV = [ps(f"psV{i}", [P, 512]) for i in range(2)]
        row = slice(KOFF, KOFF + SK)

        w_in = [sem(f"pc_w_in{i}") for i in range(2)]
        w_ready = sem("pc_w_ready")
        w_hid = sem("pc_w_hid")
        dch = sem("pc_dch")
        ctx_in = sem("pc_ctx_in")
        mask_in = sem("pc_mask_in")
        keep_done = sem("pc_keep_done")
        ctx_hid = sem("pc_ctx_hid")
        ctx_split = sem("pc_ctx_split")
        k0_done, k1_done = sem("pc_k0_done"), sem("pc_k1_done")
        sq_done, var_done, ln_done, rstd_done = sem("pc_sq"), sem("pc_var"), sem("pc_ln"), sem("pc_rstd")
        k0n_done, k0f_done, k1f_done = sem("pc_k0n"), sem("pc_k0f"), sem("pc_k1f")
        hi_done = [sem(f"pc_hi{L}") for L in range(2)]
        lo_done = [sem(f"pc_lo{L}") for L in range(2)]
        k_stored = [sem(f"pc_k_stored{L}") for L in range(2)]
        v_done = sem("pc_v_done")
        v_copied = [sem(f"pc_v_copied{i}") for i in range(2)]
        v_stored = [sem(f"pc_v_stored{i}") for i in range(2)]
        block = ctx.enter_context(nc.Block())

        v_order = [(L, c) for L in range(2) for c in range(KC)]

        @block.sync
        def _(sp):
            prime(sp, *k_stored, *v_stored)
            for i, n in enumerate(w_names):
                if i >= 2:
                    sp.wait_ge(w_ready, i - 1)
                sp.dma_start(w_raw[:, i % 2], A["wT_" + n].rearrange("(c p) n -> p c n", p=P)).then_inc(w_in[i % 2], 16)
                if i == 0:
                    sp.dma_start(ctx_raw[:], A["ctxT"][0]).then_inc(ctx_in, 16)
            with sp.Fori(0, B // 2) as it:
                for par in range(2):
                    n = it * 2 + par
                    sp.wait_ge(k1f_done, n * NK + PRIMED)
                    sp.dma_start(mask_raw[:], A["mask"][bass.ds(n, 1), :].broadcast_to([P, SK])).then_inc(mask_in, 16)
                    sp.wait_ge(ctx_split, (n + 1) * NK)
                    sp.dma_start(ctx_raw[:], A["ctxT"][n + 1]).then_inc(ctx_in, 16)
                    for m in range(NK):
                        r = n * NK + m
                        for q in (3 * m, 3 * m + 1, 3 * m + 2):
                            L, c = v_order[q]
                            w = chunk_rows(c)
                            sp.wait_ge(v_copied[q % 2], n * 6 + q // 2 + 1 + PRIMED)
                            sp.dma_start(S["V"][L][n, c * P:c * P + w, :], vst[0:w, q % 2]).then_inc(v_stored[q % 2], 16)
                        for L in range(2):
                            sp.wait_ge(hi_done[L], r + 1 + PRIMED)
                            sp.wait_ge(lo_done[L], r + 1 + PRIMED)
                            for part in range(2):
                                sp.dma_start(S["K"][L][part, m * P:(m + 1) * P, n, :], kst[L][part][:].bitcast(F32)).then_inc(k_stored[L], 16)
            for L in range(2):
                sp.wait_ge(k_stored[L], 2 * 16 * B * NK + PRIMED)
                sp.wait_ge(v_stored[L], 16 * B * KC + PRIMED)

        @block.tensor
        def _(pe):
            prime(pe, v_done)
            def product(out, wt, k, cols, first, last):
                wh, wl, xh, xl = wt
                nc.tensor.matmul(out, wh, xh, start=first, stop=False)
                nc.tensor.matmul(out, wh, xl, start=False, stop=False)
                return nc.tensor.matmul(out, wl, xh, start=False, stop=last)

            def k_chunk(L, m, par, done):
                name = f"k{L}"
                for col, w, at in key_halves():
                    for k in range(NK):
                        ws = slice(m * P, (m + 1) * P)
                        ins = product(psK[L][:, at:at + w],
                                      (w_hi[name][:, k, ws], w_lo[name][:, k, ws],
                                       ctx_hi[par][:, k, col:col + w], ctx_lo[par][:, k, col:col + w]),
                                      k, w, k == 0, k == NK - 1)
                ins.then_inc(done, 1)

            def v_chunk(n, q, par):
                L, c = v_order[q]
                w = chunk_rows(c)
                name = f"v{L}"
                pe.wait_ge(v_copied[q % 2], n * 6 + q // 2 + PRIMED)
                cs = slice(c * P, c * P + w)
                for k in range(NK):
                    ins = product(psV[q % 2][0:w, :],
                                  (ctx_hi[par][:, k, cs], ctx_lo[par][:, k, cs],
                                   w_hi[name][:, k, :], w_lo[name][:, k, :]), k, D, k == 0, k == NK - 1)
                ins.then_inc(v_done, 1)

            pe.wait_ge(w_ready, 4)
            with pe.Fori(0, B // 2) as it:
                for par in range(2):
                    n = it * 2 + par
                    pe.wait_ge(ctx_split, (n + 1) * NK)
                    for m in range(NK):
                        r = n * NK + m
                        pe.wait_ge(k0n_done, r + PRIMED)
                        k_chunk(0, m, par, k0_done)
                        v_chunk(n, 3 * m, par)
                        pe.wait_ge(sq_done, r + 1)
                        pe.wait_ge(ln_done, r + PRIMED)
                        for col, w, at in key_halves():
                            ins = nc.tensor.matmul(psR[:, at:at + w], head_mean[:], sq[:, col:col + w], start=True, stop=True)
                        ins.then_inc(var_done, 1)
                        v_chunk(n, 3 * m + 1, par)
                        pe.wait_ge(k1f_done, r + PRIMED)
                        k_chunk(1, m, par, k1_done)
                        v_chunk(n, 3 * m + 2, par)

        @block.scalar
        def _(act):
            prime(act, ln_done, *hi_done)
            for i, n in enumerate(w_names):
                if i == 0:
                    act.wait_ge(w_hid, 1)
                else:
                    act.wait_ge(w_in[i % 2], 16 * (i // 2 + 1))
                nc.scalar.copy(w_hi[n][:], w_raw[:, i % 2]).then_inc(w_hid, 1)
            act.wait_ge(ctx_in, 16)
            for k in range(NK):
                nc.scalar.copy(ctx_hi[0][:, k, :], ctx_raw[:, k, :]).then_inc(ctx_hid, 1)
            with act.Fori(0, B // 2) as it:
                for par in range(2):
                    n = it * 2 + par
                    act.wait_ge(ctx_in, 16 * (n + 2))
                    act.wait_ge(v_done, n * 12 + PRIMED)
                    for m in range(NK):
                        r = n * NK + m
                        act.wait_ge(k0_done, r + 1)
                        nc.scalar.activation(sq[:], psK[0][:, row], ACT.Square).then_inc(sq_done, 1)
                        nc.scalar.copy(ctx_hi[1 - par][:, m, :], ctx_raw[:, m, :]).then_inc(ctx_hid, 1)
                        act.wait_ge(var_done, r + 1)
                        act.wait_ge(k0n_done, r + PRIMED)
                        nc.scalar.activation(lnv[:], psR[:, row], ACT.Ln, bias=S["eps"][:, 0:1]).then_inc(ln_done, 1)
                        act.wait_ge(ln_done, r + 1 + PRIMED)
                        nc.scalar.activation(lnv[:], lnv[:], ACT.Exp, scale=-0.5).then_inc(rstd_done, 1)
                        for L, f_done, kf in ((0, k0f_done, k0f), (1, k1f_done, k1f)):
                            act.wait_ge(f_done, r + 1 + L * PRIMED)
                            act.wait_ge(k_stored[L], 32 * r + PRIMED)
                            nc.scalar.copy(kst[L][0][:], kf[:]).then_inc(hi_done[L], 1)

        @block.gpsimd
        def _(pool):
            prime(pool, *lo_done)
            for k in range(NK):
                pool.wait_ge(ctx_hid, k + 1)
                nc.gpsimd.tensor_tensor(ctx_lo[0][:, k, :], ctx_raw[:, k, :], ctx_hi[0][:, k, :], ALU.subtract).then_inc(ctx_split, 1)
            with pool.Fori(0, B // 2) as it:
                for par in range(2):
                    n = it * 2 + par
                    for m in range(NK):
                        r = n * NK + m
                        pool.wait_ge(ctx_hid, (n + 1) * NK + m + 1)
                        nc.gpsimd.tensor_tensor(ctx_lo[1 - par][:, m, :], ctx_raw[:, m, :], ctx_hi[1 - par][:, m, :],
                                                ALU.subtract).then_inc(ctx_split, 1)
                        for L, kf in ((0, k0f), (1, k1f)):
                            pool.wait_ge(hi_done[L], r + 1 + PRIMED)
                            pool.wait_ge(k_stored[L], 32 * r + PRIMED)
                            nc.gpsimd.tensor_tensor(kst[L][1][:], kf[:], kst[L][0][:], ALU.subtract).then_inc(lo_done[L], 1)

        @block.vector
        def _(dve):
            prime(dve, k0n_done, k1f_done, *v_copied)
            link = Chain(dve, dch).step
            dve.wait_ge(w_in[0], 16)
            heads = w_raw[:, 0].rearrange("p c (h d) -> p (c h) d", d=HD)
            link(nc.vector.tensor_reduce(w_mean[:], heads, axis=AX, op=ALU.add))
            link(nc.vector.tensor_scalar(w_mean[:], w_mean[:], 1.0 / HD, None, ALU.mult))
            nc.vector.tensor_tensor(heads, heads, w_mean[:].unsqueeze(2).broadcast_to([P, NK * H, HD]), ALU.subtract).then_inc(w_hid, 1)
            for i, n in enumerate(w_names):
                dve.wait_ge(w_hid, i + 2)
                nc.vector.tensor_tensor(w_lo[n][:], w_raw[:, i % 2], w_hi[n][:], ALU.subtract).then_inc(w_ready, 1)
            with dve.Fori(0, B // 2) as it:
                for par in range(2):
                    n = it * 2 + par
                    dve.wait_ge(mask_in, 16 * (n + 1))
                    nc.vector.tensor_scalar(keep[:], mask_raw[:], 0.0, None, ALU.not_equal).then_inc(keep_done, 1)
                    dve.wait_ge(keep_done, n + 1)
                    for m in range(NK):
                        r = n * NK + m

                        def v_out(q):
                            L, c = v_order[q]
                            w = chunk_rows(c)
                            dve.wait_ge(v_done, n * 12 + q + 1 + PRIMED)
                            dve.wait_ge(v_stored[q % 2], 16 * (n * 6 + q // 2) + PRIMED)
                            nc.vector.tensor_copy(vst[0:w, q % 2], psV[q % 2][0:w, :]).then_inc(v_copied[q % 2], 1)

                        v_out(3 * m)
                        dve.wait_ge(rstd_done, r + 1)
                        dve.wait_ge(k0f_done, r)
                        nc.vector.tensor_tensor(k0n[:], psK[0][:, row], lnv[:], ALU.mult).then_inc(k0n_done, 1)
                        v_out(3 * m + 1)
                        dve.wait_ge(k0n_done, r + 1 + PRIMED)
                        dve.wait_ge(lo_done[0], r + PRIMED)
                        nc.vector.tensor_scalar(k0f[:], k0n[:], S["cols"][:, C_LNG:C_LNG + 1], S["cols"][:, C_LNB:C_LNB + 1],
                                                ALU.mult, ALU.add).then_inc(k0f_done, 1)
                        dve.wait_ge(k1_done, r + 1)
                        dve.wait_ge(lo_done[1], r + PRIMED)
                        nc.vector.scalar_tensor_tensor(k1f[:], psK[1][:, row], S["cols"][:, C_BK + m:C_BK + m + 1], keep[:],
                                                       ALU.add, ALU.mult).then_inc(k1f_done, 1)
                        v_out(3 * m + 2)


def norm_and_transpose(nc, sem, tag, S, T, ps_t):
    mv_done, lny, y_done = sem(tag + "_mv"), sem(tag + "_lny"), sem(tag + "_y")
    xn_done, xt_done, xT_done = sem(tag + "_xn"), sem(tag + "_xt"), sem(tag + "_xT")
    T["xn_done"] = xn_done
    x, xn, xT, st, mv, rs = S["x"], T["xn"], T["xT"], T["st"], T["mv"], T["rs"]
    nps = len(ps_t)

    def vector(dve, link):
        for b in range(B):
            ins = nc.vector.bn_stats(st[:, b, :], x[:, b, :])
        link(ins)
        for b in range(B):
            ins = nc.vector.bn_aggr(mv[:, b, :], st[:, b, :])
        link(ins)
        var = rs[:, 0:B]
        nc.vector.tensor_scalar(var, mv[:, :, 1], LN_EPS, None, ALU.add).then_inc(mv_done, 1)
        dve.wait_ge(mv_done, 1)
        y, t = rs[:, 2 * B:3 * B], rs[:, 3 * B:4 * B]
        dve.wait_ge(y_done, 1)
        link(nc.vector.tensor_tensor(t, y, y, ALU.mult))
        link(nc.vector.tensor_tensor(t, t, var, ALU.mult))
        link(nc.vector.tensor_scalar(t, t, -0.5, 1.5, ALU.mult, ALU.add))
        link(nc.vector.tensor_tensor(t, t, y, ALU.mult))
        for b in range(B):
            nc.vector.tensor_scalar(xn[:, b, :], x[:, b, :], mv[:, b, 0:1], t[:, b:b + 1], ALU.subtract, ALU.mult).then_inc(xn_done, 1)
        for b in range(1, B, 2):
            dve.wait_ge(xt_done, b + 1)
            nc.vector.tensor_copy(xT[:, :, b * SQ:(b + 1) * SQ], ps_t[b % nps][:, 0:NK * SQ].rearrange("p (c t) -> p c t", c=NK)).then_inc(xT_done, 1)

    def scalar(act):
        act.wait_ge(mv_done, 1)
        nc.scalar.activation(rs[:, B:2 * B], rs[:, 0:B], ACT.Ln).then_inc(lny, 1)
        act.wait_ge(lny, 1)
        nc.scalar.activation(rs[:, 2 * B:3 * B], rs[:, B:2 * B], ACT.Exp, scale=-0.5).then_inc(y_done, 1)
        for b in range(0, B, 2):
            act.wait_ge(xt_done, b + 1)
            nc.scalar.copy(xT[:, :, b * SQ:(b + 1) * SQ], ps_t[b % nps][:, 0:NK * SQ].rearrange("p (c t) -> p c t", c=NK)).then_inc(xT_done, 1)

    def tensor(pe):
        for b in range(B):
            pe.wait_ge(xn_done, b + 1)
            if b >= nps:
                pe.wait_ge(xT_done, b - nps + 2)
            for c in range(NK):
                ins = nc.tensor.transpose(ps_t[b % nps][:, c * SQ:(c + 1) * SQ], xn[:, b, c * P:(c + 1) * P], S["ident"][0:SQ, 0:SQ])
            ins.then_inc(xt_done, 1)

    return vector, scalar, tensor, xT_done


def norm_tiles(sb):
    return {"xn": sb("xn", [SQ, B, D]), "xT": sb("xT", [P, NK, NT]), "st": sb("bn_st", [SQ, B, 6]),
            "mv": sb("bn_mv", [SQ, B, 2]), "rs": sb("bn_rs", [SQ, 4 * B])}


def queries(nc, sem, L, A, S):
    HALF = NT // 2
    tag = f"q{L}"
    with ExitStack() as ctx:
        sb = lambda name, shape, dt=F32: ctx.enter_context(nc.sbuf_tensor(f"{tag}_{name}", shape, dt))
        ps = lambda name, shape: ctx.enter_context(nc.psum_tensor(f"{tag}_{name}", shape, F32))
        T = norm_tiles(sb)
        xT = T["xT"]
        wq = sb("wq", [P, NK, D])
        w_mean = sb("w_mean", [P, NK * H])
        gb = sb("gb", [P, 2])
        sq, lnv, qn, qf = (sb(n, [P, 2, HALF]) for n in ("sq", "lnv", "qn", "qf"))
        q_hi = [sb(f"q_hi{i}", [P, HALF], F32R) for i in range(2)]
        q_lo = [sb(f"q_lo{i}", [P, HALF], F32R) for i in range(2)]
        ps_t = [ps(f"t{i}", [P, 512]) for i in range(2)]
        ps_q = [ps(f"q{i}", [P, 512]) for i in range(2)]
        ps_r = [ps(f"r{i}", [P, 512]) for i in range(2)]
        w_in, w_done, dch = sem(tag + "_w_in"), sem(tag + "_w_done"), sem(tag + "_dch")
        q_done, sq_done, var_done = sem(tag + "_q_done"), sem(tag + "_sq"), sem(tag + "_var")
        ln_done, rstd_done, qf_done = sem(tag + "_ln"), sem(tag + "_rstd"), sem(tag + "_qf")
        hi_done, lo_done = sem(tag + "_hi"), sem(tag + "_lo")
        q_stored = [sem(f"{tag}_stored{i}") for i in range(2)]
        n_vector, n_scalar, n_tensor, xT_done = norm_and_transpose(nc, sem, tag, S, T, ps_t)
        block = ctx.enter_context(nc.Block())
        steps = [(m, h) for m in range(NK) for h in range(2)]

        @block.sync
        def _(sp):
            sp.dma_start(wq[:], A[f"wT_q{L}"].rearrange("(c p) n -> p c n", p=P)).then_inc(w_in, 16)
            for i, (m, h) in enumerate(steps):
                sp.wait_ge(lo_done, i + 1)
                sp.wait_ge(hi_done, i + 1)
                for part, t in enumerate((q_hi, q_lo)):
                    sp.dma_start(S["Q"][part, m * P:(m + 1) * P, h * HALF:(h + 1) * HALF], t[i % 2][:].bitcast(F32)).then_inc(q_stored[i % 2], 16)
            for i in range(2):
                sp.wait_ge(q_stored[i], 32 * len(steps) // 2)

        @block.tensor
        def _(pe):
            n_tensor(pe)
            pe.wait_ge(xT_done, B)
            pe.wait_ge(w_done, 1)

            def variance(i):
                pe.wait_ge(sq_done, i + 1)
                if i >= 2:
                    pe.wait_ge(ln_done, i - 1)
                nc.tensor.matmul(ps_r[i % 2][:, 0:HALF], S["head_mean"][:], sq[:, i % 2], start=True, stop=True).then_inc(var_done, 1)

            for i, (m, h) in enumerate(steps):
                if i >= 2:
                    pe.wait_ge(qf_done, i - 1)
                for k in range(NK):
                    ins = nc.tensor.matmul(ps_q[i % 2][:, 0:HALF], wq[:, k, m * P:(m + 1) * P],
                                           xT[:, k, h * HALF:(h + 1) * HALF], start=k == 0, stop=k == NK - 1)
                ins.then_inc(q_done, 1)
                if L == 0:
                    variance(i)

        @block.scalar
        def _(act):
            n_scalar(act)
            for i in range(len(steps)):
                if L == 0:
                    act.wait_ge(q_done, i + 1)
                    if i >= 2:
                        act.wait_ge(var_done, i - 1)
                    nc.scalar.activation(sq[:, i % 2], ps_q[i % 2][:, 0:HALF], ACT.Square).then_inc(sq_done, 1)
                    act.wait_ge(var_done, i + 1)
                    if i >= 2:
                        act.wait_ge(qf_done, i - 1)
                    nc.scalar.activation(lnv[:, i % 2], ps_r[i % 2][:, 0:HALF], ACT.Ln, bias=S["eps"][:, 0:1]).then_inc(ln_done, 1)
                    act.wait_ge(ln_done, i + 1)
                    nc.scalar.activation(lnv[:, i % 2], lnv[:, i % 2], ACT.Exp, scale=-0.5).then_inc(rstd_done, 1)
                act.wait_ge(qf_done, i + 1)
                if i >= 2:
                    act.wait_ge(q_stored[i % 2], 32 * (i // 2))
                nc.scalar.copy(q_hi[i % 2][:], qf[:, i % 2]).then_inc(hi_done, 1)

        @block.vector
        def _(dve):
            link = Chain(dve, dch).step
            dve.wait_ge(w_in, 16)
            if L == 0:
                heads = wq[:].rearrange("p c (h d) -> p (c h) d", d=HD)
                link(nc.vector.tensor_reduce(w_mean[:], heads, axis=AX, op=ALU.add))
                link(nc.vector.tensor_scalar(w_mean[:], w_mean[:], 1.0 / HD, None, ALU.mult))
                link(nc.vector.tensor_scalar(gb[:], S["cols"][:, C_LNG:C_LNB + 1], L0_SCALE, None, ALU.mult))
                nc.vector.tensor_tensor(heads, heads, w_mean[:].unsqueeze(2).broadcast_to([P, NK * H, HD]), ALU.subtract).then_inc(w_done, 1)
            else:
                nc.vector.memset(gb[:], 0.0).then_inc(w_done, 1)
            n_vector(dve, link)
            for i, (m, h) in enumerate(steps):
                if i >= 2:
                    dve.wait_ge(hi_done, i - 1)
                    dve.wait_ge(lo_done, i - 1)
                if L == 0:
                    dve.wait_ge(rstd_done, i + 1)
                    link(nc.vector.tensor_tensor(qn[:, i % 2], ps_q[i % 2][:, 0:HALF], lnv[:, i % 2], ALU.mult))
                    nc.vector.tensor_scalar(qf[:, i % 2], qn[:, i % 2], gb[:, 0:1], gb[:, 1:2], ALU.mult, ALU.add).then_inc(qf_done, 1)
                else:
                    dve.wait_ge(q_done, i + 1)
                    nc.vector.tensor_scalar(qf[:, i % 2], ps_q[i % 2][:, 0:HALF], S["cols"][:, C_BQ + m:C_BQ + m + 1], -L1_SCALE,
                                            ALU.add, ALU.mult).then_inc(qf_done, 1)
                dve.wait_ge(hi_done, i + 1)
                if i >= 2:
                    dve.wait_ge(q_stored[i % 2], 32 * (i // 2))
                nc.vector.tensor_tensor(q_lo[i % 2][:], qf[:, i % 2], q_hi[i % 2][:], ALU.subtract).then_inc(lo_done, 1)


def attention(nc, sem, L, A, S):
    tag = f"a{L}"
    with ExitStack() as ctx:
        sb = lambda name, shape, dt=F32: ctx.enter_context(nc.sbuf_tensor(f"{tag}_{name}", shape, dt))
        ps = lambda name, shape: ctx.enter_context(nc.psum_tensor(f"{tag}_{name}", shape, F32))
        k_st = [sb(f"k_st{i}", [3 * HD, GH, SK], F32R) for i in range(NG)]
        q_st = [sb(f"q_st{i}", [3 * HD, GH, SQ], F32R) for i in range(NG)]
        v_sb = [sb(f"v{i}", [P, KC, P]) for i in range(NG)]
        prob = [sb(f"prob{i}", [SQ, KC * P]) for i in range(2)]
        probT = [sb(f"probT{i}", [P, KC * SQ]) for i in range(2)]
        scored = [sb(f"scored{i}", [SQ, SK]) for i in range(4)] if L else None
        mask_raw = sb("mask_raw", [SQ, SK], I32) if L else None
        masked = sb("masked", [SQ, SK]) if L else None
        nmax = sb("nmax", [SQ, 4])
        wait_here = sb("wait_here", [SQ, 2])
        rsum = sb("rsum", [SQ, 2, GH])
        rinv = sb("rinv", [SQ, GH])
        rep = sb("rep", [SQ, P])
        rinvT = sb("rinvT", [P, SQ])
        psS = [ps(f"s{i}", [P, 1024]) for i in range(2)]
        psT = [ps(f"t{i}", [P, 512]) for i in range(2)]
        psO = [ps(f"o{i}", [P, 512]) for i in range(2)]
        row = slice(KOFF, KOFF + SK)
        CV = 2
        loaded = [sem(f"{tag}_loaded{i}") for i in range(NG)]
        mask_in, mask_done = sem(tag + "_mask_in"), sem(tag + "_mask_done")
        zeroed = sem(tag + "_zeroed")
        s_done, max_done, exp_done, t_done = sem(tag + "_s"), sem(tag + "_max"), sem(tag + "_exp"), sem(tag + "_t")
        tv_out, ts_out = sem(tag + "_tv"), sem(tag + "_ts")
        pv_done, rinv_done, rep_done = sem(tag + "_pv"), sem(tag + "_rinv"), sem(tag + "_rep")
        rt_done = [sem(f"{tag}_rt{i}") for i in range(NG)]
        rinvT_done = sem(tag + "_rinvT")
        normed = sem(tag + "_normed")
        bv_done = sem(tag + "_bv")
        block = ctx.enter_context(nc.Block())
        LOADS = 6 + 2

        def bodies(eng, body):
            body(0, first=True)
            with eng.Fori(1, B - 1) as b:
                body(b)
            body(B - 1, last=True)

        @block.sync
        def _(sp):
            with sp.Fori(0, B) as b:
                if L:
                    sp.wait_ge(mask_done, b + PRIMED)
                    sp.dma_start(mask_raw[:], A["mask"][bass.ds(b, 1), :].broadcast_to([SQ, SK])).then_inc(mask_in, 16)
                for g in range(NG):
                    sp.wait_ge(rt_done[g], b + PRIMED)
                    for quad, (qp, kp) in enumerate(((0, 0), (0, 1), (1, 0))):
                        rows = slice(quad * HD, (quad + 1) * HD)
                        sp.dma_start(q_st[g][rows].bitcast(F32), S["Q"][qp, g * P:(g + 1) * P, bass.ds(b * SQ, SQ)]
                                     .rearrange("(h d) t -> d h t", d=HD)).then_inc(loaded[g], 16)
                        sp.dma_start(k_st[g][rows].bitcast(F32), S["K"][L][kp, g * P:(g + 1) * P, b, :]
                                     .rearrange("(h d) t -> d h t", d=HD)).then_inc(loaded[g], 16)
                    sp.dma_start(v_sb[g][:, 0:KC - 1, :], S["V"][L][b, 0:(KC - 1) * P, g * P:(g + 1) * P]
                                 .rearrange("(c p) d -> p c d", p=P)).then_inc(loaded[g], 16)
                    sp.dma_start(v_sb[g][0:KTAIL, KC - 1, :], S["V"][L][b, (KC - 1) * P:SK, g * P:(g + 1) * P]).then_inc(loaded[g], 16)

        @block.tensor
        def _(pe):
            prime(pe, *rt_done)

            def body(b, first=False, last=False):
                def scores(i):
                    n, g = b * H + i, i % H // GH
                    if i % GH == 0:
                        pe.wait_ge(loaded[g], (b + i // H + 1) * 16 * LOADS)
                    if not (first and i < 2):
                        pe.wait_ge(max_done if L else exp_done, n - 1)
                    for col, w, at in key_halves():
                        ins = nc.tensor.matmul(psS[i % 2][0:SQ, at:at + w], q_st[g][:, i % GH, :],
                                               k_st[g][:, i % GH, col:col + w], start=True, stop=True)
                    ins.then_inc(s_done, 1)

                def transposes(i):
                    n = b * H + i
                    pe.wait_ge(exp_done, n + 1)
                    pe.wait_ge(tv_out, n + PRIMED)
                    pe.wait_ge(ts_out, n + PRIMED)
                    for c in range(KC):
                        half, at = (0, c * SQ) if c < CV else (1, (c - CV) * SQ)
                        ins = nc.tensor.transpose(psT[half][:, at:at + SQ], prob[i % 2][:, c * P:(c + 1) * P], S["ident"][0:SQ, 0:SQ])
                    ins.then_inc(t_done, 1)

                def values(i):
                    n, g, j = b * H + i, i % H // GH, i % GH
                    pe.wait_ge(tv_out, n + 1 + PRIMED)
                    pe.wait_ge(ts_out, n + 1 + PRIMED)
                    if j == 0 and not (first and g < 2):
                        pe.wait_ge(normed, b * NG + (i // GH - 1))
                    for c in range(KC):
                        w = chunk_rows(c)
                        ins = nc.tensor.matmul(psO[g % 2][j * HD:(j + 1) * HD, 0:SQ], v_sb[g][0:w, c, j * HD:(j + 1) * HD],
                                               probT[i % 2][0:w, c * SQ:(c + 1) * SQ], start=c == 0, stop=c == KC - 1)
                    ins.then_inc(pv_done, 1)

                def sums_transpose(g):
                    pe.wait_ge(rep_done, b * NG + (g + 1))
                    nc.tensor.transpose(psO[g % 2][:, P:P + SQ], rep[:], S["ident"][0:SQ, 0:SQ]).then_inc(rt_done[g % NG], 1)

                if first:
                    scores(0)
                    scores(1)
                for i in range(H):
                    if not (last and i + 2 >= H):
                        scores(i + 2)
                    transposes(i)
                    if not (first and i == 0):
                        values(i - 1)
                    if i % GH == 1 and not (first and i == 1):
                        sums_transpose(i // GH - 1)
                if last:
                    values(H - 1)
                    sums_transpose(NG - 1)

            pe.wait_ge(zeroed, 2)
            bodies(pe, body)

        @block.scalar
        def _(act):
            prime(act, ts_out)

            def body(b, first=False, last=False):
                def second_part(i):
                    n = b * H + i
                    act.wait_ge(t_done, n + 1)
                    if not (first and i < 2):
                        act.wait_ge(pv_done, n - 1)
                    nc.scalar.copy(probT[i % 2][:, CV * SQ:], psT[1][:, 0:(KC - CV) * SQ]).then_inc(ts_out, 1)

                for i in range(H):
                    n, g = b * H + i, i // GH
                    act.wait_ge(max_done, n + 1)
                    if not (first and i < 2):
                        act.wait_ge(t_done, n - 1)
                    if i % GH == 0 and not (first and g < 2):
                        act.wait_ge(rinv_done, b * NG + (g - 1))
                    src = scored[i % 4][:] if L else psS[i % 2][0:SQ, row]
                    nc.scalar.activation(prob[i % 2][:, 0:SK], src, ACT.Exp, bias=nmax[:, i % 4:i % 4 + 1], scale=-1.0 if L else 1.0,
                                         accum_out=rsum[:, g % 2, i % GH:i % GH + 1]).then_inc(exp_done, 1)
                    if not (first and i == 0):
                        second_part(i - 1)
                if last:
                    second_part(H - 1)

            bodies(act, body)

        @block.vector
        def _(dve):
            prime(dve, mask_done, tv_out)
            for t in prob:
                nc.vector.memset(t[:, SK:], 0.0).then_inc(zeroed, 1)

            def body(b, first=False, last=False):
                def mask(after):
                    dve.wait_ge(mask_in, (b + after + 1) * 16)
                    if after:
                        dve.wait_ge(max_done, b * H + H)
                    nc.vector.tensor_scalar(masked[:], mask_raw[:], 0.0, NEG, ALU.is_equal, ALU.mult).then_inc(mask_done, 1)
                    dve.wait_ge(mask_done, b + (after + 1 + PRIMED))

                def row_max(i):
                    n = b * H + i
                    dve.wait_ge(s_done, n + 1)
                    if not (first and i < 4):
                        dve.wait_ge(exp_done, n - 3)
                    out = nmax[:, i % 4:i % 4 + 1]
                    if L:
                        nc.vector.memset(wait_here[:, i % 2:i % 2 + 1], 0.0)
                        nc.vector.tensor_tensor_reduce(out=scored[i % 4][:], in0=psS[i % 2][0:SQ, row], in1=masked[:], scale=1.0,
                                                       scalar=3.0e38, op0=ALU.add, op1=ALU.min, accum_out=out).then_inc(max_done, 1)
                    else:
                        nc.vector.tensor_reduce(out, psS[i % 2][0:SQ, row], axis=AX, op=ALU.max, negate=True).then_inc(max_done, 1)

                def first_part(i):
                    n = b * H + i
                    dve.wait_ge(t_done, n + 1)
                    if not (first and i < 2):
                        dve.wait_ge(pv_done, n - 1)
                    nc.vector.tensor_copy(probT[i % 2][:, 0:CV * SQ], psT[0][:, 0:CV * SQ]).then_inc(tv_out, 1)

                def reciprocal_sums(g):
                    G = b * NG + g
                    dve.wait_ge(exp_done, b * H + (g + 1) * GH)
                    nc.vector.reciprocal(rinv[:], rsum[:, g % 2, :]).then_inc(rinv_done, 1)
                    dve.wait_ge(rinv_done, G + 1)
                    nc.vector.tensor_copy(rep[:].rearrange("p (h d) -> p h d", h=GH),
                                          rinv[:].unsqueeze(2).broadcast_to([SQ, GH, HD])).then_inc(rep_done, 1)

                def normalise(g):
                    G = b * NG + g
                    dve.wait_ge(rt_done[g % NG], b + (g // NG + 1 + PRIMED))
                    nc.vector.tensor_copy(rinvT[:], psO[g % 2][:, P:P + SQ]).then_inc(rinvT_done, 1)
                    dve.wait_ge(rinvT_done, G + 1)
                    out = S["attnT"][:, g % NG, bass.ds(b * SQ + g // NG * SQ, SQ)]
                    nc.vector.tensor_tensor(out, psO[g % 2][:, 0:SQ], rinvT[:], ALU.mult).then_inc(normed, 1)

                if first:
                    if L:
                        mask(0)
                    row_max(0)
                    row_max(1)
                for i in range(H):
                    if not (last and i + 2 >= H):
                        if L and i + 2 == H:
                            mask(1)
                        row_max(i + 2)
                    first_part(i)
                    if i % GH == GH - 1:
                        reciprocal_sums(i // GH)
                    if i % GH == 2 and not (first and i == 2):
                        normalise(i // GH - 1)
                if last:
                    normalise(NG - 1)

            bodies(dve, body)
            if L:
                dve.wait_ge(normed, B * NG)
                for k in range(NK):
                    nc.vector.tensor_scalar(S["attnT"][:, k, :], S["attnT"][:, k, :], S["cols"][:, C_BV + k:C_BV + k + 1], None, ALU.add)\
                        .then_inc(bv_done, 1)


def output(nc, sem, L, A, S):
    tag = f"o{L}"
    with ExitStack() as ctx:
        sb = lambda name, shape, dt=F32: ctx.enter_context(nc.sbuf_tensor(f"{tag}_{name}", shape, dt))
        wo, bias, t = sb("wo", [P, NK, D]), sb("bias", [SQ, D]), sb("t", [SQ, 2, D])
        psY = [ctx.enter_context(nc.psum_tensor(f"{tag}_y{i}", [P, 512], F32)) for i in range(B)]
        w_in, y_done, dch, x_done = sem(tag + "_w_in"), sem(tag + "_y"), sem(tag + "_dch"), sem(tag + "_x")
        block = ctx.enter_context(nc.Block())

        @block.sync
        def _(sp):
            sp.dma_start(wo[:], A[f"wT_o{L}"].rearrange("(c p) n -> p c n", p=P)).then_inc(w_in, 16)
            sp.dma_start(bias[:], A[f"bo{L}"].broadcast_to([SQ, D])).then_inc(w_in, 16)

        @block.tensor
        def _(pe):
            pe.wait_ge(w_in, 32)
            for b in range(B):
                for k in range(NK):
                    ins = nc.tensor.matmul(psY[b][0:SQ, :], S["attnT"][:, k, b * SQ:(b + 1) * SQ], wo[:, k, :], start=k == 0, stop=k == NK - 1)
                ins.then_inc(y_done, 1)

        @block.vector
        def _(dve):
            link = Chain(dve, dch).step
            dve.wait_ge(w_in, 32)
            for b in range(B):
                dve.wait_ge(y_done, b + 1)
                link(nc.vector.tensor_tensor(t[:, b % 2], psY[b][0:SQ, :], bias[:], ALU.add))
                nc.vector.scalar_tensor_tensor(S["x"][:, b, :], t[:, b % 2], S["gates"][0:SQ, L:L + 1], S["x"][:, b, :],
                                               ALU.mult, ALU.add).then_inc(x_done, 1)
            dve.wait_ge(x_done, B)


def top_k(nc, link, vals, n, k, mx, gt, eq, ca, cb, cnt, sel):
    for b in range(B):
        ins = nc.vector.max(mx[:, b, :], vals[:, b, :])
    link(ins)
    thr = mx[:, :, k - 1:k].broadcast_to([SQ, B, n])
    nc.vector.tensor_tensor(gt, vals, thr, ALU.is_gt)
    link(nc.vector.tensor_tensor(eq, vals, thr, ALU.is_equal))
    src, dst, d = eq, ca, 1
    while d < n:
        nc.vector.tensor_copy(dst[:, :, 0:d], src[:, :, 0:d])
        link(nc.vector.tensor_tensor(dst[:, :, d:n], src[:, :, d:n], src[:, :, 0:n - d], ALU.add))
        src, dst, d = dst, (cb if dst is ca else ca), 2 * d
    link(nc.vector.tensor_reduce(cnt, gt, axis=AX, op=ALU.add))
    link(nc.vector.tensor_tensor(dst, src, cnt.unsqueeze(2).broadcast_to([SQ, B, n]), ALU.add))
    link(nc.vector.scalar_tensor_tensor(dst, dst, float(k), eq, ALU.is_le, ALU.mult))
    link(nc.vector.tensor_tensor(sel, dst, gt, ALU.add))


def positions(nc, dve, link, sh, pos, tot, cnt_e, ps_pos, ps_tot):
    view = lambda t: t[0:SQ, 0:B * sh[2]].rearrange("p (b e) -> p b e", b=B)
    link(nc.vector.tensor_copy(pos, view(ps_pos)))
    link(nc.vector.tensor_copy(tot, view(ps_tot)))
    for b in range(1, B):
        link(nc.vector.tensor_tensor(pos[:, b:, :], pos[:, b:, :], tot[:, b - 1:b, :].broadcast_to([SQ, B - b, sh[2]]), ALU.add))
    link(nc.vector.tensor_reduce(cnt_e, tot.rearrange("p b e -> p e b"), axis=AX, op=ALU.add))


def blocks(eng, first, end, step):
    n = end - first
    with eng.Fori(0, n // 2) as it:
        for i in range(2):
            step(it * 2 + (first + i), it + (first + i) // 2, (first + i) % 2)
    if n % 2:
        step(end - 1, (end - 1) // 2, (end - 1) % 2)


def experts(nc, sem, L, A, S, out):
    tag = f"f{L}"
    HALF = NT // 2
    E = (E0, E1)[L]
    NB = (MB0, E1)[L]
    HC = (I0 // P, NI1)[L]
    UB = (1, 2)[L]
    sh = [SQ, B, E]
    with ExitStack() as ctx:
        sb = lambda name, shape, dt=F32: ctx.enter_context(nc.sbuf_tensor(f"{tag}_{name}", shape, dt))
        bank = lambda name: ctx.enter_context(nc.psum_tensor(f"{tag}_{name}", [P, 512], F32))
        T = norm_tiles(sb)
        xT, xn = T["xT"], T["xn"]
        gate_w = sb("gate_w", [P, NK, E])
        sc, gt, eq, ca, cb, sel, pos, tot = (sb(n, sh) for n in ("sc", "gt", "eq", "ca", "cb", "sel", "pos", "tot"))
        mx, cnt = sb("mx", [SQ, B, 8]), sb("cnt", [SQ, B])
        cnt_e, nblk, base, base2 = (sb(n, [SQ, E]) for n in ("cnt_e", "nblk", "base", "base2"))
        block_no, oh, oh2 = sb("block_no", [SQ, NB]), sb("oh", [SQ, NB, E]), sb("oh2", [SQ, NB, E])
        block_at = sb("block_at", [SQ, NB])
        expert_f, expert_i = sb("expert_f", [SQ, NB]), sb("expert_i", [SQ, NB], I32)
        slot_w = sb("slot_w", [SQ, B, 2, E])
        picked = sb("picked", [SQ, B * 2, E])
        tok = [sb(f"tok{i}", [SQ, B, 4]) for i in range(2)]
        onehot = [sb(f"onehot{i}", [SQ, B, P]) for i in range(2)]
        info = sb("info", [P, NB, 3])
        row_f, row_i = sb("row_f", [P, 1]), sb("row_i", [P, NB], I32)
        g_row, s_row = ([sb(f"{n}{i}", [P, 1], I32) for i in range(2)] for n in ("g_row", "s_row"))
        xg = [sb(f"xg{i}", [P, D]) for i in range(2)]
        xgT = [sb(f"xgT{i}", [P, NK, P]) for i in range(2)]
        up_w = [sb(f"up_w{i}", [P, NK, UB * 512]) for i in range(2 - L)]
        dn_w = [sb(f"dn_w{i}", [P, HC, D]) for i in range(2)]
        sg = sb("sg", [P, I0]) if L == 0 else None
        hid = [sb(f"hid{i}", [P, HC * P]) for i in range(2)]
        hidT = [sb(f"hidT{i}", [P, HC, P]) for i in range(2)]
        yw = [sb(f"yw{i}", [P, D]) for i in range(2)]
        acc = sb("acc", [SQ, B, D])
        zero, wait_here = sb("zero", [P, D]), sb("wait_here", [1, 2])
        if L == 0:
            e_bias = sb("e_bias", [SQ, E0])
            sfc = sb("sfc", sh)
            gsc, gsel = sb("gsc", [SQ, B, GRP0]), sb("gsel", [SQ, B, GRP0])
            sh_up, sh_dn = sb("sh_up", [P, NK, 4 * I0]), sb("sh_dn", [P, NK, D])
            sh_g, sh_u = sb("sh_g", [P, 2, HALF]), sb("sh_u", [P, 2, HALF])
            sh_h = sb("sh_h", [P, NK, NT])
        x_rows, acc_rows = S["x_rows"], S["acc_rows"]

        psX, psI, psY = bank("x"), bank("i"), bank("y")
        psU, psH = [bank(f"u{i}") for i in range(2)], [bank(f"h{i}") for i in range(2)]
        ps8 = bank("r")
        r_in, dch = sem(tag + "_r_in"), sem(tag + "_dch")
        logit_done, exp_done, sel_done, pos_done, lm_done, base_done = (sem(f"{tag}_{n}") for n in ("logit", "exp", "sel", "pos", "lm", "base"))
        up_in, dn_in = ([sem(f"{tag}_{n}{i}") for i in range(2)] for n in ("up_in", "dn_in"))
        x_stored, acc_set, zeroed = sem(tag + "_x_stored"), sem(tag + "_acc_set"), sem(tag + "_zeroed")
        picked_done, tok_done, onehot_done = sem(tag + "_picked"), sem(tag + "_tok"), sem(tag + "_onehot")
        ids_done, info_done, row_done, idx_done = (sem(f"{tag}_{n}") for n in ("ids", "info", "row", "idx"))
        gathered, scattered = [sem(f"{tag}_gath{i}") for i in range(2)], sem(tag + "_scat")
        xtr_done, xT_out, up_done, silu_done, h_done = (sem(f"{tag}_{n}") for n in ("xtr", "xTo", "up", "silu", "h"))
        htr_done, hT_out, dn_done, yw_done = (sem(f"{tag}_{n}") for n in ("htr", "hTo", "dn", "yw"))
        hT_half, waited = sem(tag + "_hT_half"), sem(tag + "_waited")
        added = sem(tag + "_added")
        acc_in, x_done, stored = sem(tag + "_acc_in"), sem(tag + "_x"), sem(tag + "_stored")
        if L == 0:
            sh_in, sg_done, su_done, sh_done, shg_out, shy_done, shy_out = \
                (sem(f"{tag}_sh{n}") for n in ("in", "g", "u", "h", "go", "y", "yo"))
        n_vector, n_scalar, n_tensor, xT_done = norm_and_transpose(nc, sem, tag, S, T, [psX, psY])
        block = ctx.enter_context(nc.Block())
        sh_units = [(j, h) for j in range(NK) for h in range(2)]

        @block.sync
        def _(sp):
            sp.dma_start(gate_w[:], A[f"routerT{L}"].rearrange("(c p) n -> p c n", p=P)).then_inc(r_in, 16)
            if L == 0:
                sp.dma_start(e_bias[:], A["e_bias"].broadcast_to([SQ, E0])).then_inc(r_in, 16)
                sp.dma_start(sh_up[:], A["sh_up"]).then_inc(sh_in, 16)
                sp.dma_start(sh_dn[:], A["sh_dn"]).then_inc(sh_in, 16)
            else:
                sp.dma_start(up_w[0][:], A["wgT1"].rearrange("(c p) n -> p c n", p=P)).then_inc(up_in[0], 16)
            sp.wait_ge(zeroed, 1)
            sp.dma_start(x_rows[NT:NT + P, :], zero[:]).then_inc(x_stored, 16)
            sp.dma_start(acc_rows[NT:NT + P, :], zero[:]).then_inc(acc_set, 16)
            sp.wait_ge(T["xn_done"], B)
            sp.dma_start(x_rows[0:NT, :].rearrange("(b t) d -> t b d", t=SQ), xn[:]).then_inc(x_stored, 16)
            if L:
                for b in range(B):
                    sp.dma_start(acc_rows[b * SQ:(b + 1) * SQ, :], zero[0:SQ, :]).then_inc(acc_set, 16)

            def expert(t):
                return sp.value_load(expert_i[0:1, bass.ds(t, 1)], min_val=0, max_val=E0 - 1) if L == 0 else t

            def load_up(e, i):
                sp.dma_start(up_w[i][:], A["gu"][e]).then_inc(up_in[i], 16)

            def load_dn(e, i):
                sp.dma_start(dn_w[i][:], A[("dn", "wd1")[L]][e]).then_inc(dn_in[i], 16)

            if L == 0:
                sp.wait_ge(base_done, 1)
                for t in range(2):
                    e = expert(t)
                    load_up(e, t)
                    load_dn(e, t)
                for b in range(B):
                    sp.wait_ge(shy_out, b + 1)
                    sp.dma_start(acc_rows[b * SQ:(b + 1) * SQ, :], acc[:, b, :]).then_inc(acc_set, 16)
            else:
                for t in range(2):
                    load_dn(t, t)

            def load(t, c, i):
                e = expert(t)
                if L == 0:
                    sp.wait_ge(up_done, t - 1)
                    load_up(e, i)
                sp.wait_ge(dn_done, t - 1)
                load_dn(e, i)

            blocks(sp, 2, NB, load)
            sp.wait_ge(scattered, 16 * NB)
            sp.dma_start(acc[:], acc_rows[0:NT, :].rearrange("(b t) d -> t b d", t=SQ)).then_inc(acc_in, 16)
            if L:
                for b in range(B):
                    sp.wait_ge(x_done, b + 1)
                    sp.dma_start(out[b], S["x"][:, b, :]).then_inc(stored, 16)
                sp.wait_ge(stored, 16 * B)

        @block.tensor
        def _(pe):
            n_tensor(pe)
            pe.wait_ge(xT_done, B)
            pe.wait_ge(r_in, (32, 16)[L])
            for b in range(B):
                for k in range(NK):
                    ins = nc.tensor.matmul(ps8[0:SQ, b * E:(b + 1) * E], xT[:, k, b * SQ:(b + 1) * SQ], gate_w[:, k, :],
                                           start=k == 0, stop=k == NK - 1)
            ins.then_inc(logit_done, 1)
            if L == 0:
                pe.wait_ge(sh_in, 32)
                for u, (j, h) in enumerate(sh_units):
                    if u >= 2:
                        pe.wait_ge(shg_out, u - 1)
                    for which, banks, done in ((0, psU, sg_done), (1, psH, su_done)):
                        for k in range(NK):
                            at = which * 2 * I0 + j * P
                            ins = nc.tensor.matmul(banks[u % 2][:, 0:HALF], sh_up[:, k, at:at + P], xT[:, k, h * HALF:(h + 1) * HALF],
                                                   start=k == 0, stop=k == NK - 1)
                        ins.then_inc(done, 1)
            pe.wait_ge(sel_done, 1)
            flat = gt[:].rearrange("p b e -> p (b e)")
            nc.tensor.matmul(psX[0:SQ, 0:B * E], S["upto"][:], flat, start=True, stop=True)
            nc.tensor.matmul(psY[0:SQ, 0:B * E], S["ones"][:], flat, start=True, stop=True).then_inc(pos_done, 1)
            if L == 0:
                pe.wait_ge(sh_done, len(sh_units))
                for b in range(B):
                    if b >= 2:
                        pe.wait_ge(shy_out, b - 1)
                    for j in range(NK):
                        ins = nc.tensor.matmul(psU[b % 2][0:SQ, :], sh_h[:, j, b * SQ:(b + 1) * SQ], sh_dn[:, j, :],
                                               start=j == 0, stop=j == NK - 1)
                    ins.then_inc(shy_done, 1)
                pe.wait_ge(shy_out, B)

            def ids(t, c, i):
                pe.wait_ge(onehot_done, t + 1)
                pe.wait_ge(info_done, t + PRIMED)
                for b in range(B):
                    ins = nc.tensor.matmul(psI[:, 0:3], onehot[i][:, b, :], tok[i][:, b, 1:4], start=b == 0, stop=b == B - 1)
                ins.then_inc(ids_done, 1)

            def x_transpose(t, c, i):
                pe.wait_ge(gathered[i], (c + 1) * 16)
                pe.wait_ge(xT_out, t + PRIMED)
                for k in range(NK):
                    ins = nc.tensor.transpose(psX[:, k * P:(k + 1) * P], xg[i][:, k * P:(k + 1) * P], S["ident"][:])
                ins.then_inc(xtr_done, 1)

            def up(t, c, i):
                pe.wait_ge(xT_out, t + 1 + PRIMED)
                if L == 0:
                    pe.wait_ge(up_in[i], (c + 1) * 16)
                pe.wait_ge((h_done, silu_done)[L], t + PRIMED)
                for u in range(UB):
                    for k in range(NK):
                        ins = nc.tensor.matmul(psU[u][:], xgT[i][:, k, :], up_w[i * (1 - L)][:, k, u * 512:(u + 1) * 512],
                                               start=k == 0, stop=k == NK - 1)
                ins.then_inc(up_done, 1)

            def h_transpose(t, c, i):
                pe.wait_ge((h_done, silu_done)[L], t + 1 + PRIMED)
                pe.wait_ge(hT_out, t + PRIMED)
                for j in range(HC):
                    ins = nc.tensor.transpose(psH[j // 4][:, j % 4 * P:(j % 4 + 1) * P], hid[i][:, j * P:(j + 1) * P], S["ident"][:])
                ins.then_inc(htr_done, 1)

            def down(t, c, i):
                pe.wait_ge(hT_out, t + 1 + PRIMED)
                pe.wait_ge(dn_in[i], (c + 1) * 16)
                pe.wait_ge(yw_done, t + PRIMED)
                for j in range(HC):
                    ins = nc.tensor.matmul(psY[:], hidT[i][:, j, :], dn_w[i][:, j, :], start=j == 0, stop=j == HC - 1)
                ins.then_inc(dn_done, 1)

            def step(t, c, i, first=False, ids_too=True, x_too=True):
                up(t, c, i)
                if ids_too:
                    ids(t + 2, c + 1, i)
                if not first:
                    down(t - 1, c + i - 1, 1 - i)
                if x_too:
                    x_transpose(t + 1, c + i, 1 - i)
                h_transpose(t, c, i)

            if L:
                pe.wait_ge(up_in[0], 16)
            ids(0, 0, 0)
            ids(1, 0, 1)
            x_transpose(0, 0, 0)
            step(0, 0, 0, first=True)
            blocks(pe, 1, NB - 2, step)
            step(NB - 2, (NB - 2) // 2, NB % 2, ids_too=False)
            step(NB - 1, (NB - 1) // 2, (NB - 1) % 2, ids_too=False, x_too=False)
            down(NB - 1, (NB - 1) // 2, (NB - 1) % 2)

        @block.scalar
        def _(act):
            prime(act, xT_out, hT_out, silu_done)
            n_scalar(act)
            act.wait_ge((logit_done, lm_done)[L], 1)
            if L == 0:
                nc.scalar.activation(sc[:], ps8[0:SQ, 0:B * E0].rearrange("p (b e) -> p b e", b=B), ACT.Exp, scale=-1.0).then_inc(exp_done, 1)
                for u, (j, h) in enumerate(sh_units):
                    act.wait_ge(sg_done, u + 1)
                    if u >= 2:
                        act.wait_ge(sh_done, u - 1)
                    nc.scalar.activation(sh_g[:, u % 2], psU[u % 2][:, 0:HALF], ACT.Silu).then_inc(lm_done, 1)
                    act.wait_ge(su_done, u + 1)
                    nc.scalar.copy(sh_u[:, u % 2], psH[u % 2][:, 0:HALF]).then_inc(shg_out, 1)
                for b in range(B):
                    act.wait_ge(shy_done, b + 1)
                    nc.scalar.copy(acc[:, b, :], psU[b % 2][0:SQ, :]).then_inc(shy_out, 1)
            else:
                nc.scalar.activation(sc[:], sc[:], ACT.Exp).then_inc(exp_done, 1)

            def x_out(t, c, i):
                act.wait_ge(xtr_done, t + 1)
                nc.scalar.copy(xgT[i][:].rearrange("p c t -> p (c t)"), psX[:]).then_inc(xT_out, 1)

            def step(t, c, i, x_too=True):
                act.wait_ge(up_done, t + 1)
                if L == 0:
                    act.wait_ge(h_done, t + PRIMED)
                    nc.scalar.activation(sg[:], psU[0][:, 0:I0], ACT.Silu).then_inc(silu_done, 1)
                else:
                    nc.scalar.activation(hid[i][:, 0:512], psU[0][:], ACT.Silu).then_inc(h_done, 1)
                    nc.scalar.activation(hid[i][:, 512:1024], psU[1][:], ACT.Silu).then_inc(silu_done, 1)
                if x_too:
                    x_out(t + 1, c + i, 1 - i)
                act.wait_ge(htr_done, t + 1)
                hT = hidT[i][:].rearrange("p c t -> p (c t)")
                if L == 0:
                    nc.scalar.copy(hT, psH[0][:, 0:HC * P]).then_inc(hT_out, 1)
                else:
                    nc.scalar.copy(hT[:, 0:512], psH[0][:]).then_inc(hT_half, 1)
                    nc.scalar.copy(hT[:, 512:1024], psH[1][:]).then_inc(hT_out, 1)

            x_out(0, 0, 0)
            blocks(act, 0, NB - 1, step)
            step(NB - 1, (NB - 1) // 2, (NB - 1) % 2, x_too=False)

        @block.gpsimd
        def _(pool):
            prime(pool, added, waited)
            nc.gpsimd.memset(zero[:], 0.0).then_inc(zeroed, 1)
            if L == 0:
                for u, (j, h) in enumerate(sh_units):
                    pool.wait_ge(shg_out, u + 1)
                    pool.wait_ge(lm_done, u + 1)
                    nc.gpsimd.tensor_tensor(sh_h[:, j, h * HALF:(h + 1) * HALF], sh_g[:, u % 2], sh_u[:, u % 2], ALU.mult).then_inc(sh_done, 1)
            pool.wait_ge(x_stored, 32)
            pool.wait_ge(acc_set, 16 * (B + 1))

            def gather(t, c, i):
                pool.wait_ge(idx_done, t + 1)
                if not isinstance(t, int):
                    pool.wait_ge(xtr_done, t - 1)
                pool.wait_ge(waited, t + PRIMED)
                nc.gpsimd.tensor_tensor(wait_here[:, 0:1], zero[0:1, 0:1], zero[0:1, 0:1], ALU.add).then_inc(waited, 1)
                nc.gpsimd.indirect_dma_start(xg[i][:], None, x_rows[:, :], bass.IndirectOffsetOnAxis(ap=g_row[i][:, 0:1], axis=0))\
                    .then_inc(gathered[i], 16)

            def scatter(t, c, i):
                pool.wait_ge(yw_done, t + 1 + PRIMED)
                if not isinstance(t, int) or t:
                    pool.wait_ge(scattered, t * 16)
                pool.wait_ge(added, t + PRIMED)
                nc.gpsimd.tensor_tensor(wait_here[:, 1:2], zero[0:1, 0:1], zero[0:1, 0:1], ALU.add).then_inc(added, 1)
                nc.gpsimd.indirect_dma_start(acc_rows[:, :], bass.IndirectOffsetOnAxis(ap=s_row[i][:, 0:1], axis=0), yw[i][:], None,
                                             compute_op=ALU.add).then_inc(scattered, 16)

            def step(t, c, i, gather_too=True):
                if gather_too:
                    gather(t + 2, c + 1, i)
                scatter(t, c, i)

            gather(0, 0, 0)
            gather(1, 0, 1)
            step(0, 0, 0)
            blocks(pool, 1, NB - 2, step)
            for t in (NB - 2, NB - 1):
                scatter(t, t // 2, t % 2)

        @block.vector
        def _(dve):
            prime(dve, info_done, yw_done, h_done)
            link = Chain(dve, dch).step
            n_vector(dve, link)
            link(nc.vector.tensor_copy(block_no[:], S["iota"][0:SQ, 0:NB]))
            nc.vector.tensor_scalar(block_at[:], block_no[:], float(P), None, ALU.mult)
            for t in tok:
                nc.vector.tensor_copy(t[:, :, 2:3], S["token"][:].unsqueeze(2))
                ins = nc.vector.memset(t[:, :, 3:4], 1.0)
            link(ins)
            if L == 0:
                dve.wait_ge(exp_done, 1)
                dve.wait_ge(r_in, 32)
                link(nc.vector.tensor_scalar(sc[:], sc[:], 1.0, None, ALU.add))
                link(nc.vector.reciprocal(sc[:], sc[:]))
                link(nc.vector.tensor_tensor(sfc[:], sc[:], e_bias[:].unsqueeze(1).broadcast_to(sh), ALU.add))
                gs = E0 // GRP0
                link(nc.vector.tensor_reduce(gsc[:], sfc[:].rearrange("p b (g s) -> p b g s", s=gs), axis=AX, op=ALU.max))
                g8 = lambda t: t[:, :, 0:GRP0]
                top_k(nc, link, gsc[:], GRP0, TOPG0, mx, g8(gt), g8(eq), g8(ca), g8(cb), cnt[:], gsel[:])
                by_group = sfc[:].rearrange("p b (g s) -> p (b g) s", s=gs)
                link(nc.vector.tensor_tensor(by_group, by_group, gsel[:].rearrange("p b g -> p (b g)").unsqueeze(2)
                                             .broadcast_to([SQ, B * GRP0, gs]), ALU.mult))
                top_k(nc, link, sfc[:], E0, TOP0, mx, gt[:], eq[:], ca[:], cb[:], cnt[:], sel[:])
            else:
                dve.wait_ge(logit_done, 1)
                link(nc.vector.tensor_copy(sc[:], ps8[0:SQ, 0:B * E1].rearrange("p (b e) -> p b e", b=B)))
                link(nc.vector.tensor_reduce(cnt[:], sc[:], axis=AX, op=ALU.max))
                nc.vector.tensor_tensor(sc[:], sc[:], cnt[:].unsqueeze(2).broadcast_to(sh), ALU.subtract).then_inc(lm_done, 1)
                dve.wait_ge(exp_done, 1)
                link(nc.vector.tensor_reduce(cnt[:], sc[:], axis=AX, op=ALU.add))
                link(nc.vector.reciprocal(cnt[:], cnt[:]))
                link(nc.vector.tensor_tensor(sc[:], sc[:], cnt[:].unsqueeze(2).broadcast_to(sh), ALU.mult))
                top_k(nc, link, sc[:], E1, TOP1, mx, gt[:], eq[:], ca[:], cb[:], cnt[:], sel[:])
            nc.vector.tensor_copy(gt[:], sel[:]).then_inc(sel_done, 1)
            dve.wait_ge(pos_done, 1)
            positions(nc, dve, link, sh, pos[:], tot[:], cnt_e[:], psX, psY)
            if L:
                link(nc.vector.scalar_tensor_tensor(sel[:], pos[:], float(CAP1), sel[:], ALU.is_le, ALU.mult))
            weight = slot_w[:, :, 1, :]
            link(nc.vector.tensor_tensor(sc[:], sel[:], sc[:], ALU.mult))
            link(nc.vector.tensor_reduce(cnt[:], sc[:], axis=AX, op=ALU.add))
            link(nc.vector.tensor_scalar(cnt[:], cnt[:], (1e-20, 1e-6)[L], None, ALU.add))
            link(nc.vector.reciprocal(cnt[:], cnt[:]))
            if L == 0:
                link(nc.vector.tensor_scalar(cnt[:], cnt[:], W0_SCALE, None, ALU.mult))
            link(nc.vector.tensor_tensor(weight, sc[:], cnt[:].unsqueeze(2).broadcast_to(sh), ALU.mult))
            ones_b = lambda t: t.unsqueeze(1).broadcast_to([SQ, NB, E])
            bno = block_no[:].unsqueeze(2).broadcast_to([SQ, NB, E])
            if L == 0:
                link(nc.vector.tensor_scalar(nblk[:], cnt_e[:], 0.0, None, ALU.is_gt))
                for j in range(1, -(-NT // P)):
                    link(nc.vector.scalar_tensor_tensor(nblk[:], cnt_e[:], float(j * P), nblk[:], ALU.is_gt, ALU.add))
                src, dst, d = nblk, base, 1
                while d < E:
                    nc.vector.tensor_copy(dst[:, 0:d], src[:, 0:d])
                    link(nc.vector.tensor_tensor(dst[:, d:], src[:, d:], src[:, 0:E - d], ALU.add))
                    src, dst, d = dst, (base2 if dst is base else base), 2 * d
                first = dst
                link(nc.vector.tensor_tensor(oh2[:], bno, ones_b(src[:]), ALU.is_ge))
                link(nc.vector.tensor_tensor(first[:], src[:], nblk[:], ALU.subtract))
                link(nc.vector.tensor_tensor(oh[:], bno, ones_b(first[:]), ALU.is_ge))
                link(nc.vector.tensor_tensor(oh[:], oh[:], oh2[:], ALU.subtract))
                link(nc.vector.tensor_tensor(oh2[:], oh[:], ones_b(S["iota"][0:SQ, 0:E]), ALU.mult))
                link(nc.vector.tensor_reduce(expert_f[:], oh2[:], axis=AX, op=ALU.add))
                nc.vector.tensor_copy(expert_i[:], expert_f[:]).then_inc(base_done, 1)
            else:
                first = base
                link(nc.vector.tensor_copy(first[:], S["iota"][0:SQ, 0:E]))
                link(nc.vector.tensor_tensor(oh[:], bno, ones_b(first[:]), ALU.is_equal))
            link(nc.vector.scalar_tensor_tensor(pos[:], first[:].unsqueeze(1).broadcast_to(sh), float(P), pos[:], ALU.mult, ALU.add))
            link(nc.vector.tensor_tensor(slot_w[:, :, 0, :], pos[:], sel[:], ALU.mult))

            def slots(t, c, i):
                nc.vector.tensor_tensor(picked[:], slot_w[:].rearrange("p b s e -> p (b s) e"),
                                        oh[:, bass.ds(t, 1), :].broadcast_to([SQ, B * 2, E]), ALU.mult).then_inc(picked_done, 1)
                dve.wait_ge(picked_done, t + 1)
                nc.vector.tensor_reduce(tok[i][:, :, 0:2], picked[:].rearrange("p (b s) e -> p b s e", s=2), axis=AX, op=ALU.add)\
                    .then_inc(tok_done, 1)
                dve.wait_ge(tok_done, t + 1)
                nc.vector.scalar_tensor_tensor(onehot[i][:], S["iota1"][0:SQ, :].unsqueeze(1).broadcast_to([SQ, B, P]),
                                               block_at[:, bass.ds(t, 1)], tok[i][:, :, 0:1].broadcast_to([SQ, B, P]),
                                               ALU.add, ALU.is_equal).then_inc(onehot_done, 1)

            def rows(t, c, i):
                dve.wait_ge(ids_done, t + 1)
                nc.vector.tensor_copy(info[:, bass.ds(t, 1), :], psI[:, 0:3].unsqueeze(1)).then_inc(info_done, 1)
                dve.wait_ge(info_done, t + 1 + PRIMED)
                nc.vector.scalar_tensor_tensor(row_f[:], info[:, bass.ds(t, 1), 2], S["spare"][:, 1:2], info[:, bass.ds(t, 1), 1],
                                               ALU.mult, ALU.add).then_inc(row_done, 1)
                dve.wait_ge(row_done, t + 1)
                nc.vector.tensor_scalar(row_i[:, bass.ds(t, 1)], row_f[:], S["spare"][:, 0:1], None, ALU.add)
                nc.vector.tensor_scalar(g_row[i][:], row_f[:], S["spare"][:, 0:1], None, ALU.add).then_inc(idx_done, 1)

            def hidden(t, c, i):
                dve.wait_ge(silu_done, t + 1 + PRIMED)
                nc.vector.tensor_tensor(hid[i][:], sg[:], psU[0][:, I0:2 * I0], ALU.mult).then_inc(h_done, 1)

            def weighted(t, c, i):
                dve.wait_ge(dn_done, t + 1)
                dve.wait_ge(added, t + PRIMED)
                nc.vector.tensor_copy(s_row[i][:], row_i[:, bass.ds(t, 1)])
                nc.vector.tensor_scalar(yw[i][:], psY[:], info[:, bass.ds(t, 1), 0], None, ALU.mult).then_inc(yw_done, 1)

            def step(t, c, i, first=False, rows_too=True, slots_too=True):
                if L == 0:
                    hidden(t, c, i)
                if rows_too:
                    rows(t + 2, c + 1, i)
                if not first:
                    weighted(t - 1, c + i - 1, 1 - i)
                if slots_too:
                    slots(t + 3, c + 1 + i, 1 - i)

            slots(0, 0, 0)
            rows(0, 0, 0)
            slots(1, 0, 1)
            rows(1, 0, 1)
            slots(2, 1, 0)
            step(0, 0, 0, first=True)
            blocks(dve, 1, NB - 3, step)
            for t in (NB - 3, NB - 2, NB - 1):
                step(t, t // 2, t % 2, rows_too=t < NB - 2, slots_too=False)
            weighted(NB - 1, (NB - 1) // 2, (NB - 1) % 2)
            dve.wait_ge(acc_in, 16)
            for b in range(B):
                nc.vector.scalar_tensor_tensor(S["x"][:, b, :], acc[:, b, :], S["gates"][0:SQ, 2 + L:3 + L], S["x"][:, b, :],
                                               ALU.mult, ALU.add).then_inc(x_done, 1)
            dve.wait_ge(x_done, B)


def setup(nc, sem, A, S):
    x_in, c_in, g_done = sem("st_x_in"), sem("st_c_in"), sem("st_g")
    z_done, c_done, i_done = sem("st_z"), sem("st_c"), sem("st_i")
    with (nc.sbuf_tensor("iota_i", [P, 2, P], I32) as iota_i, nc.sbuf_tensor("token_i", [P, B], I32) as token_i,
          nc.sbuf_tensor("spare_i", [P, 1], I32) as spare_i, nc.Block() as block):
        @block.sync
        def _(sp):
            sp.dma_start(S["cols"][:], A["cols"]).then_inc(c_in, 16)
            sp.dma_start(S["x"][:], A["x"].rearrange("b t d -> t b d")).then_inc(x_in, 16)
            sp.wait_ge(x_in, 16)

        @block.scalar
        def _(act):
            act.wait_ge(c_in, 16)
            nc.scalar.activation(S["gates"][:], S["cols"][:, C_GX:C_GX + 4], ACT.Tanh).then_inc(g_done, 1)
            act.wait_ge(g_done, 1)

        @block.vector
        def _(dve):
            nc.vector.memset(S["eps"][:], LN_EPS).then_inc(z_done, 1)
            nc.vector.memset(S["ident"][:], 0.0).then_inc(z_done, 1)
            nc.vector.memset(S["ones"][:], 1.0).then_inc(z_done, 1)
            nc.vector.memset(S["upto"][:], 1.0).then_inc(z_done, 1)
            nc.vector.memset(S["head_mean"][:], 0.0).then_inc(z_done, 1)
            dve.wait_ge(z_done, 5)
            for j in range(GH):
                nc.vector.memset(S["head_mean"][j * HD:(j + 1) * HD, j * HD:(j + 1) * HD], 1.0 / HD).then_inc(c_done, 1)

        @block.gpsimd
        def _(pool):
            pool.wait_ge(z_done, 4)
            nc.gpsimd.affine_select(out=S["ident"][:], in_=S["ident"][:], compare_op=ALU.not_equal, fill=1.0, base=0,
                                    pattern=[[-1, P]], channel_multiplier=1).then_inc(c_done, 1)
            nc.gpsimd.affine_select(out=S["upto"][:], in_=S["upto"][:], compare_op=ALU.is_ge, fill=0.0, base=0,
                                    pattern=[[1, SQ]], channel_multiplier=-1).then_inc(c_done, 1)
            nc.gpsimd.iota(iota_i[:, 0, :], pattern=[[1, P]], base=0, channel_multiplier=0).then_inc(i_done, 1)
            nc.gpsimd.iota(iota_i[:, 1, :], pattern=[[1, P]], base=1, channel_multiplier=0).then_inc(i_done, 1)
            nc.gpsimd.iota(token_i[:], pattern=[[SQ, B]], base=0, channel_multiplier=1).then_inc(i_done, 1)
            nc.gpsimd.iota(spare_i[:], pattern=[[1, 1]], base=NT, channel_multiplier=1).then_inc(i_done, 1)
            pool.wait_ge(i_done, 4)
            nc.gpsimd.tensor_copy(S["iota"][:], iota_i[:, 0, :]).then_inc(c_done, 1)
            nc.gpsimd.tensor_copy(S["iota1"][:], iota_i[:, 1, :]).then_inc(c_done, 1)
            nc.gpsimd.tensor_copy(S["token"][:], token_i[0:SQ, :]).then_inc(c_done, 1)
            nc.gpsimd.tensor_copy(S["spare"][:, 0:1], spare_i[:]).then_inc(i_done, 1)
            pool.wait_ge(i_done, 5)
            nc.gpsimd.tensor_scalar(S["spare"][:, 1:2], S["spare"][:, 0:1], -1.0, 0.0, ALU.mult, ALU.add).then_inc(c_done, 1)
            pool.wait_ge(c_done, 6 + GH)


def build(nc, A, out):
    with ExitStack() as ctx:
        sb = lambda name, shape, dt=F32: ctx.enter_context(nc.sbuf_tensor(name, shape, dt))
        layer_sems = []

        def sem(name):
            layer_sems.append(nc.alloc_semaphore(name=name))
            return layer_sems[-1]

        dram = lambda name, shape, dt: nc.dram_tensor(name, shape, dt, kind="Internal").ap()
        S = {
            "x": sb("x_sb", [SQ, B, D]), "cols": sb("cols_sb", [P, NCOLS]), "gates": sb("gates", [P, 4]),
            "ident": sb("ident", [P, P]), "head_mean": sb("head_mean", [P, P]), "eps": sb("eps", [P, 1]),
            "ones": sb("ones", [SQ, SQ]), "upto": sb("upto", [SQ, SQ]), "attnT": sb("attnT", [P, NK, NT]),
            "K": [dram(f"scr_k{L}", [2, D, B, SK], F32) for L in range(2)],
            "V": [dram(f"scr_v{L}", [B, SK, D], F32) for L in range(2)],
            "Q": dram("scr_q", [2, D, NT], F32),
            "x_rows": dram("scr_x", [NT + P, D], F32), "acc_rows": dram("scr_acc", [NT + P, D], F32),
            "iota": sb("iota", [P, P]), "iota1": sb("iota1", [P, P]), "token": sb("token", [SQ, B]), "spare": sb("spare", [P, 2]),
        }
        setup(nc, sem, A, S)
        project_context(nc, sem, A, S)
        for L in range(2):
            queries(nc, sem, L, A, S)
            attention(nc, sem, L, A, S)
            output(nc, sem, L, A, S)
            experts(nc, sem, L, A, S, out)
            if L == 0:
                nc.clear_and_free_semaphores(layer_sems)
                layer_sems.clear()
                nc.all_engine_barrier()


def lay_out(i):
    import numpy as np
    i = {k: np.asarray(v) for k, v in i.items()}
    a = {}
    ctxT = i["ctx_1024"].reshape(B, SK, NK, P).transpose(0, 3, 2, 1)
    a["ctxT"] = np.concatenate([ctxT, np.zeros((1, P, NK, SK), ctxT.dtype)])
    a["x"] = i["x"]
    a["mask"] = i["mask_Bx1x1xS2_ik0"].reshape(B, SK)
    for L in range(2):
        for n in "qkv":
            a[f"wT_{n}{L}"] = i[f"L{L}_xattn_W{n}"].T
    a["wT_o0"], a["wT_o1"] = i["L0_xattn_Wp"].T, i["L1_xattn_Wo"].T
    a["bo0"], a["bo1"] = i["L0_xattn_bp"].reshape(1, D), i["L1_xattn_bo"].reshape(1, D)
    col = lambda v: v.reshape(NK, P).T
    a["cols"] = np.concatenate([np.tile(i["L0_xattn_ln_g"], GH)[:, None], np.tile(i["L0_xattn_ln_b"], GH)[:, None],
                                col(i["L1_xattn_bk"]), col(i["L1_xattn_bq"]), col(i["L1_xattn_bv"]),
                                np.tile(i["g_xattn"], (P, 1)), np.tile(i["g_ffn"], (P, 1))], axis=1)
    a["routerT0"] = i["L0_ffn_gate_weight"].T
    a["e_bias"] = i["L0_ffn_e_score_correction_bias"].reshape(1, E0)
    a["sh_up"] = np.concatenate([i["L0_ffn_shared_gate_w"], i["L0_ffn_shared_up_w"]]).reshape(4 * I0, NK, P).transpose(2, 1, 0)
    a["sh_dn"] = i["L0_ffn_shared_down_w"].reshape(D, NK, P).transpose(2, 1, 0)
    a["gu"] = i["L0_ffn_experts_gate_up"].reshape(E0, 2 * I0, NK, P).transpose(0, 3, 2, 1)
    a["dn"] = i["L0_ffn_experts_down"].reshape(E0, D, I0 // P, P).transpose(0, 3, 2, 1)
    a["routerT1"] = i["L1_ffn_w_router"].T
    a["wgT1"] = i["L1_ffn_w_gate"].T
    a["wd1"] = i["L1_ffn_w_down"].reshape(E1, D, NI1, P).transpose(0, 3, 2, 1)
    return {k: np.ascontiguousarray(v) for k, v in a.items()}


def kernel(**inputs):
    import concourse.bacc as bacc
    from concourse.bass_utils import run_bass_kernel_spmd
    arrays = lay_out(inputs)
    nc = bacc.Bacc("TRN2", target_bir_lowering=False, num_devices=1)
    A = {k: nc.dram_tensor(f"in_{k}", list(v.shape), mybir.dt.from_np(v.dtype), kind="ExternalInput").ap() for k, v in arrays.items()}
    out = nc.dram_tensor("out_0", [B, SQ, D], F32, kind="ExternalOutput").ap()
    build(nc, A, out)
    r = run_bass_kernel_spmd(nc, [{f"in_{k}": v for k, v in arrays.items()}], core_ids=[0])
    return r.results[0]["out_0"]
```

```python
from contextlib import ExitStack

import concourse.bass as bass
from concourse import mybir

F32 = mybir.dt.float32
F32R = mybir.dt.float32r
I32 = mybir.dt.int32
ALU = mybir.AluOpType
ACT = mybir.ActivationFunctionType
AX = mybir.AxisListType.X

P = 128
B, SQ, SK, D = 8, 100, 722, 512
NT = B * SQ
NK = D // P
H = 16
HD = D // H
GH = P // HD
NG = H // GH
KC = -(-SK // P)
KTAIL = SK - (KC - 1) * P
KHALF = (362, 360)
KOFF = 512 - KHALF[0]
LN_EPS = 1e-5
L0_SCALE = 8.0 / HD
L1_SCALE = float(1.0 / (HD ** 0.5))
NEG = 1e9
E0, I0, TOP0, GRP0, TOPG0 = 32, 256, 6, 8, 4
MB0 = (NT * TOP0 + E0 * (P - 1)) // P
W0_SCALE = 2.5
E1, HID1, TOP1 = 8, 1024, 2
NI1 = HID1 // P
CAP1 = -(-NT * 5 // (E1 * 4))
C_LNG, C_LNB, C_BK, C_BQ, C_BV, C_GX, C_GF = 0, 1, 2, 6, 10, 14, 16
NCOLS = 18


PRIMED = 1


def prime(eng, *sems):
    for s in sems:
        eng.sem_inc(s, PRIMED)


class Chain:

    def __init__(self, eng, sem):
        self.eng, self.sem, self.n = eng, sem, 0

    def step(self, ins):
        self.n += 1
        ins.then_inc(self.sem, 1)
        self.eng.wait_ge(self.sem, self.n)


def key_halves():
    return ((0, KHALF[0], KOFF), (KHALF[0], KHALF[1], 512))


def chunk_rows(c):
    return P if c < KC - 1 else KTAIL


def project_context(nc, sem, A, S):
    with ExitStack() as ctx:
        sb = lambda name, shape, dt=F32: ctx.enter_context(nc.sbuf_tensor(name, shape, dt))
        ps = lambda name, shape: ctx.enter_context(nc.psum_tensor(name, shape, F32))
        w_names = ("k0", "v0", "k1", "v1")
        w_raw = sb("w_raw", [P, 3, NK, D])
        w_hi = {n: sb("w_hi_" + n, [P, NK, D], F32R) for n in w_names}
        w_lo = {n: sb("w_lo_" + n, [P, NK, D], F32R) for n in w_names}
        w_mean = sb("w_mean", [P, NK * H])
        ctx_raw = sb("ctx_raw", [P, NK, SK])
        ctx_hi = [sb(f"ctx_hi{i}", [P, NK, SK], F32R) for i in range(2)]
        ctx_lo = [sb(f"ctx_lo{i}", [P, NK, SK], F32R) for i in range(2)]
        mask_raw = sb("mask_raw", [P, SK], I32)
        keep = sb("keep", [P, SK])
        sq = sb("sq", [P, SK])
        sq_hi, sq_lo = sb("sq_hi", [P, SK], F32R), sb("sq_lo", [P, SK], F32R)
        head_mean = sb("head_mean_r", [P, P], F32R)
        rstd = sb("rstd", [P, SK])
        k0n = sb("k0n", [P, SK])
        k0f = sb("k0f", [P, SK])
        k1f = sb("k1f", [P, SK])
        kst = [[sb(f"kst{L}_{part}", [P, SK], F32R) for part in "hl"] for L in range(2)]
        vst = sb("vst", [P, 2, D])
        psK = [ps(f"psK{L}", [P, 1024]) for L in range(2)]
        psR = ps("psR", [P, 1024])
        psV = [ps(f"psV{i}", [P, 512]) for i in range(2)]
        row = slice(KOFF, KOFF + SK)

        w_in = [sem(f"pc_w_in{i}") for i in range(3)]
        w_ready = sem("pc_w_ready")
        w_hid = sem("pc_w_hid")
        dch = sem("pc_dch")
        ctx_in, x_in, stats_done = sem("pc_ctx_in"), sem("pc_x_in"), sem("pc_stats")
        mask_in = sem("pc_mask_in")
        keep_done = sem("pc_keep_done")
        ctx_hid = sem("pc_ctx_hid")
        ctx_split = sem("pc_ctx_split")
        k0_done, k1_done = sem("pc_k0_done"), sem("pc_k1_done")
        sq_done, var_done, ln_done, rstd_done = sem("pc_sq"), sem("pc_var"), sem("pc_ln"), sem("pc_rstd")
        sq_hid, sq_split, mean_ready = sem("pc_sq_hid"), sem("pc_sq_split"), sem("pc_mean_ready")
        k0n_done, k0f_done, k1f_done = sem("pc_k0n"), sem("pc_k0f"), sem("pc_k1f")
        hi_done = [sem(f"pc_hi{L}") for L in range(2)]
        lo_done = [sem(f"pc_lo{L}") for L in range(2)]
        k_stored = [sem(f"pc_k_stored{L}") for L in range(2)]
        v_done = sem("pc_v_done")
        v_copied = [sem(f"pc_v_copied{i}") for i in range(2)]
        v_stored = [sem(f"pc_v_stored{i}") for i in range(2)]
        block = ctx.enter_context(nc.Block())

        v_order = [(L, c) for L in range(2) for c in range(KC)]

        @block.sync
        def _(sp):
            prime(sp, *k_stored, *v_stored)
            for i, n in enumerate(w_names):
                if i == 3:
                    sp.wait_ge(w_ready, 1)
                sp.dma_start(w_raw[:, i % 3], A["wT_" + n].rearrange("(c p) n -> p c n", p=P)).then_inc(w_in[i % 3], 16)
                if i == 0:
                    sp.dma_start(ctx_raw[:], A["ctxT"][0]).then_inc(ctx_in, 16)
                    sp.dma_start(mask_raw[:], A["mask"][0:1, :].broadcast_to([P, SK])).then_inc(mask_in, 16)
            sp.dma_start(S["x"][:], A["x"].rearrange("b t d -> t b d")).then_inc(x_in, 16)
            sp.wait_ge(ctx_split, NK)
            sp.dma_start(ctx_raw[:], A["ctxT"][1]).then_inc(ctx_in, 16)
            with sp.Fori(0, B // 2) as it:
                for par in range(2):
                    n = it * 2 + par
                    for m in range(NK):
                        if m == 1:
                            sp.wait_ge(keep_done, n + 1)
                            sp.dma_start(mask_raw[:], A["mask"][bass.ds(n + 1, 1), :].broadcast_to([P, SK])).then_inc(mask_in, 16)
                        if m == NK - 1:
                            sp.wait_ge(ctx_split, (n + 2) * NK)
                            sp.dma_start(ctx_raw[:], A["ctxT"][n + 2]).then_inc(ctx_in, 16)
                        r = n * NK + m
                        for q in (3 * m, 3 * m + 1, 3 * m + 2):
                            L, c = v_order[q]
                            w = chunk_rows(c)
                            sp.wait_ge(v_copied[q % 2], n * 6 + q // 2 + 1 + PRIMED)
                            sp.dma_start(S["V"][L][n, c * P:c * P + w, :], vst[0:w, q % 2]).then_inc(v_stored[q % 2], 16)
                        for L in range(2):
                            sp.wait_ge(hi_done[L], r + 1 + PRIMED)
                            sp.wait_ge(lo_done[L], r + 1 + PRIMED)
                            for part in range(2):
                                sp.dma_start(S["K"][L][part, m * P:(m + 1) * P, n, :], kst[L][part][:].bitcast(F32)).then_inc(k_stored[L], 16)
            for L in range(2):
                sp.wait_ge(k_stored[L], 2 * 16 * B * NK + PRIMED)
                sp.wait_ge(v_stored[L], 16 * B * KC + PRIMED)
            sp.wait_ge(ctx_in, 16 * (B + 2))
            sp.wait_ge(mask_in, 16 * (B + 1))
            sp.wait_ge(x_in, 16)

        @block.tensor
        def _(pe):
            prime(pe, v_done)

            def product(out, wt, k, cols, first, last):
                wh, wl, xh, xl = wt
                nc.tensor.matmul(out, wh, xh, start=first, stop=False)
                nc.tensor.matmul(out, wh, xl, start=False, stop=False)
                return nc.tensor.matmul(out, wl, xh, start=False, stop=last)

            def k_chunk(L, m, par, done):
                name = f"k{L}"
                for col, w, at in key_halves():
                    for k in range(NK):
                        ws = slice(m * P, (m + 1) * P)
                        ins = product(psK[L][:, at:at + w],
                                      (w_hi[name][:, k, ws], w_lo[name][:, k, ws],
                                       ctx_hi[par][:, k, col:col + w], ctx_lo[par][:, k, col:col + w]),
                                      k, w, k == 0, k == NK - 1)
                ins.then_inc(done, 1)

            def v_chunk(n, q, par):
                L, c = v_order[q]
                w = chunk_rows(c)
                name = f"v{L}"
                pe.wait_ge(v_copied[q % 2], n * 6 + q // 2 + PRIMED)
                cs = slice(c * P, c * P + w)
                for k in range(NK):
                    ins = product(psV[q % 2][0:w, :],
                                  (ctx_hi[par][:, k, cs], ctx_lo[par][:, k, cs],
                                   w_hi[name][:, k, :], w_lo[name][:, k, :]), k, D, k == 0, k == NK - 1)
                ins.then_inc(v_done, 1)

            with pe.Fori(0, B // 2) as it:
                for par in range(2):
                    n = it * 2 + par
                    pe.wait_ge(ctx_split, (n + 1) * NK)
                    for m in range(NK):
                        r = n * NK + m
                        if m == 0:
                            pe.wait_ge(mean_ready, 1)
                        if m in (0, 2):
                            pe.wait_ge(w_ready, 1 if m == 0 else 4)
                        pe.wait_ge(k0n_done, r + PRIMED)
                        k_chunk(0, m, par, k0_done)
                        if m == 0:
                            pe.wait_ge(w_ready, 2)
                        v_chunk(n, 3 * m, par)
                        v_chunk(n, 3 * m + 1, par)
                        pe.wait_ge(sq_split, r + 1)
                        pe.wait_ge(ln_done, r + PRIMED)
                        for col, w, at in key_halves():
                            nc.tensor.matmul(psR[:, at:at + w], head_mean[:], sq_hi[:, col:col + w], start=True, stop=False)
                            ins = nc.tensor.matmul(psR[:, at:at + w], head_mean[:], sq_lo[:, col:col + w], start=False, stop=True)
                        ins.then_inc(var_done, 1)
                        if m == 0:
                            pe.wait_ge(w_ready, 3)
                        pe.wait_ge(k1f_done, r + PRIMED)
                        k_chunk(1, m, par, k1_done)
                        v_chunk(n, 3 * m + 2, par)

        @block.scalar
        def _(act):
            prime(act, ln_done, *hi_done)
            for i, n in enumerate(w_names):
                if i == 0:
                    act.wait_ge(w_hid, 1)
                else:
                    act.wait_ge(w_in[i % 3], 16 * (i // 3 + 1))
                nc.scalar.copy(w_hi[n][:], w_raw[:, i % 3]).then_inc(w_hid, 1)
                if i == 0:
                    act.wait_ge(ctx_in, 16)
                    for k in range(NK):
                        nc.scalar.copy(ctx_hi[0][:, k, :], ctx_raw[:, k, :]).then_inc(ctx_hid, 1)
            with act.Fori(0, B // 2) as it:
                for par in range(2):
                    n = it * 2 + par
                    act.wait_ge(ctx_in, 16 * (n + 2))
                    act.wait_ge(v_done, n * 12 + PRIMED)
                    for m in range(NK):
                        r = n * NK + m
                        act.wait_ge(k0_done, r + 1)
                        nc.scalar.activation(sq[:], psK[0][:, row], ACT.Square).then_inc(sq_done, 1)
                        act.wait_ge(sq_done, r + 1)
                        nc.scalar.copy(sq_hi[:], sq[:]).then_inc(sq_hid, 1)
                        nc.scalar.copy(ctx_hi[1 - par][:, m, :], ctx_raw[:, m, :]).then_inc(ctx_hid, 1)
                        act.wait_ge(var_done, r + 1)
                        act.wait_ge(k0n_done, r + PRIMED)
                        nc.scalar.activation(rstd[:], psR[:, row], ACT.Ln, bias=S["eps"][:, 0:1]).then_inc(ln_done, 1)
                        act.wait_ge(ln_done, r + 1 + PRIMED)
                        nc.scalar.activation(rstd[:], rstd[:], ACT.Exp, scale=-0.5).then_inc(rstd_done, 1)
                        for L, f_done, kf in ((0, k0f_done, k0f), (1, k1f_done, k1f)):
                            act.wait_ge(f_done, r + 1 + PRIMED)
                            act.wait_ge(k_stored[L], 32 * r + PRIMED)
                            nc.scalar.copy(kst[L][0][:], kf[:]).then_inc(hi_done[L], 1)

        @block.gpsimd
        def _(pool):
            prime(pool, *lo_done)
            for k in range(NK // 2):
                pool.wait_ge(ctx_hid, k + 1)
                nc.gpsimd.tensor_tensor(ctx_lo[0][:, k, :], ctx_raw[:, k, :], ctx_hi[0][:, k, :], ALU.subtract).then_inc(ctx_split, 1)
            with pool.Fori(0, B // 2) as it:
                for par in range(2):
                    n = it * 2 + par
                    for m in range(NK):
                        r = n * NK + m
                        pool.wait_ge(ctx_hid, (n + 1) * NK + m + 1)
                        nc.gpsimd.tensor_tensor(ctx_lo[1 - par][:, m, :], ctx_raw[:, m, :], ctx_hi[1 - par][:, m, :],
                                                ALU.subtract).then_inc(ctx_split, 1)
                        for L, kf in ((0, k0f), (1, k1f)):
                            pool.wait_ge(hi_done[L], r + 1 + PRIMED)
                            pool.wait_ge(k_stored[L], 32 * r + PRIMED)
                            nc.gpsimd.tensor_tensor(kst[L][1][:], kf[:], kst[L][0][:], ALU.subtract).then_inc(lo_done[L], 1)

        @block.vector
        def _(dve):
            prime(dve, k0n_done, k0f_done, k1f_done, *v_copied)
            link = Chain(dve, dch).step
            nc.vector.tensor_copy(head_mean[:], S["head_mean"][:]).then_inc(mean_ready, 1)
            dve.wait_ge(w_in[0], 16)
            heads = w_raw[:, 0].rearrange("p c (h d) -> p (c h) d", d=HD)
            link(nc.vector.tensor_reduce(w_mean[:], heads, axis=AX, op=ALU.add))
            link(nc.vector.tensor_scalar(w_mean[:], w_mean[:], 1.0 / HD, None, ALU.mult))
            nc.vector.tensor_tensor(heads, heads, w_mean[:].unsqueeze(2).broadcast_to([P, NK * H, HD]), ALU.subtract).then_inc(w_hid, 1)
            for i, n in enumerate(w_names):
                dve.wait_ge(w_hid, i + 2)
                nc.vector.tensor_tensor(w_lo[n][:], w_raw[:, i % 3], w_hi[n][:], ALU.subtract).then_inc(w_ready, 1)
                if i == 0:
                    for k in range(NK // 2, NK):
                        dve.wait_ge(ctx_hid, k + 1)
                        nc.vector.tensor_tensor(ctx_lo[0][:, k, :], ctx_raw[:, k, :], ctx_hi[0][:, k, :], ALU.subtract).then_inc(ctx_split, 1)
            with dve.Fori(0, B // 2) as it:
                for par in range(2):
                    n = it * 2 + par
                    dve.wait_ge(mask_in, 16 * (n + 1))
                    dve.wait_ge(k1f_done, n * NK + PRIMED)
                    nc.vector.tensor_scalar(keep[:], mask_raw[:], 0.0, None, ALU.not_equal).then_inc(keep_done, 1)
                    dve.wait_ge(keep_done, n + 1)
                    for m in range(NK):
                        r = n * NK + m

                        def v_out(q):
                            L, c = v_order[q]
                            w = chunk_rows(c)
                            dve.wait_ge(v_done, n * 12 + q + 1 + PRIMED)
                            dve.wait_ge(v_stored[q % 2], 16 * (n * 6 + q // 2) + PRIMED)
                            nc.vector.tensor_copy(vst[0:w, q % 2], psV[q % 2][0:w, :]).then_inc(v_copied[q % 2], 1)

                        dve.wait_ge(sq_hid, r + 1)
                        nc.vector.tensor_tensor(sq_lo[:], sq[:], sq_hi[:], ALU.subtract).then_inc(sq_split, 1)
                        v_out(3 * m)
                        v_out(3 * m + 1)
                        dve.wait_ge(rstd_done, r + 1)
                        dve.wait_ge(k0f_done, r + PRIMED)
                        nc.vector.tensor_tensor(k0n[:], psK[0][:, row], rstd[:], ALU.mult).then_inc(k0n_done, 1)
                        dve.wait_ge(k0n_done, r + 1 + PRIMED)
                        dve.wait_ge(lo_done[0], r + PRIMED)
                        nc.vector.tensor_scalar(k0f[:], k0n[:], S["cols"][:, C_LNG:C_LNG + 1], S["cols"][:, C_LNB:C_LNB + 1],
                                                ALU.mult, ALU.add).then_inc(k0f_done, 1)
                        dve.wait_ge(k1_done, r + 1)
                        dve.wait_ge(lo_done[1], r + PRIMED)
                        nc.vector.scalar_tensor_tensor(k1f[:], psK[1][:, row], S["cols"][:, C_BK + m:C_BK + m + 1], keep[:],
                                                       ALU.add, ALU.mult).then_inc(k1f_done, 1)
                        v_out(3 * m + 2)
            dve.wait_ge(x_in, 16)
            for b in range(B):
                nc.vector.bn_stats(S["stats"][:, b, :], S["x"][:, b, :]).then_inc(stats_done, 1)
            dve.wait_ge(stats_done, B)


def norm_and_transpose(nc, sem, tag, S, T, ps_t):
    mv_done, lny, y_done = sem(tag + "_mv"), sem(tag + "_lny"), sem(tag + "_y")
    xn_done, xt_done, xT_done = sem(tag + "_xn"), sem(tag + "_xt"), sem(tag + "_xT")
    T["xn_done"] = xn_done
    x, xn, xT, st, mv, rs = S["x"], T["xn"], T["xT"], S["stats"], T["mv"], T["rs"]

    def vector(dve, link, between=None):
        for b in range(B):
            ins = nc.vector.bn_aggr(mv[:, b, :], st[:, b, :])
        link(ins)
        var = rs[:, 0:B]
        nc.vector.tensor_scalar(var, mv[:, :, 1], LN_EPS, None, ALU.add).then_inc(mv_done, 1)
        dve.wait_ge(mv_done, 1)
        y, t = rs[:, 2 * B:3 * B], rs[:, 3 * B:4 * B]
        dve.wait_ge(y_done, 1)
        link(nc.vector.tensor_tensor(t, y, y, ALU.mult))
        link(nc.vector.tensor_tensor(t, t, var, ALU.mult))
        link(nc.vector.tensor_scalar(t, t, -0.5, 1.5, ALU.mult, ALU.add))
        link(nc.vector.tensor_tensor(t, t, y, ALU.mult))
        for b in range(B):
            nc.vector.tensor_scalar(xn[:, b, :], x[:, b, :], mv[:, b, 0:1], t[:, b:b + 1], ALU.subtract, ALU.mult).then_inc(xn_done, 1)
        if between:
            between()
        for b in range(1, B, 2):
            dve.wait_ge(xt_done, b + 1)
            nc.vector.tensor_copy(xT[:, :, b * SQ:(b + 1) * SQ], ps_t[b][:, 0:NK * SQ].rearrange("p (c t) -> p c t", c=NK)).then_inc(xT_done, 1)

    def scalar(act):
        act.wait_ge(mv_done, 1)
        nc.scalar.activation(rs[:, B:2 * B], rs[:, 0:B], ACT.Ln).then_inc(lny, 1)
        act.wait_ge(lny, 1)
        nc.scalar.activation(rs[:, 2 * B:3 * B], rs[:, B:2 * B], ACT.Exp, scale=-0.5).then_inc(y_done, 1)
        for b in range(0, B, 2):
            act.wait_ge(xt_done, b + 1)
            nc.scalar.copy(xT[:, :, b * SQ:(b + 1) * SQ], ps_t[b][:, 0:NK * SQ].rearrange("p (c t) -> p c t", c=NK)).then_inc(xT_done, 1)

    def tensor(pe):
        for b in range(B):
            pe.wait_ge(xn_done, b + 1)
            for c in range(NK):
                ins = nc.tensor.transpose(ps_t[b][:, c * SQ:(c + 1) * SQ], xn[:, b, c * P:(c + 1) * P], S["ident"][0:SQ, 0:SQ])
            ins.then_inc(xt_done, 1)

    return vector, scalar, tensor, xT_done


def norm_tiles(sb):
    return {"xn": sb("xn", [SQ, B, D]), "xT": sb("xT", [P, NK, NT]), 
            "mv": sb("bn_mv", [SQ, B, 2]), "rs": sb("bn_rs", [SQ, 4 * B])}


def queries(nc, sem, L, A, S, KV):
    HALF = NT // 2
    tag = f"q{L}"
    with ExitStack() as ctx:
        sb = lambda name, shape, dt=F32: ctx.enter_context(nc.sbuf_tensor(f"{tag}_{name}", shape, dt))
        ps = lambda name, shape: ctx.enter_context(nc.psum_tensor(f"{tag}_{name}", shape, F32))
        T = norm_tiles(sb)
        xT = T["xT"]
        wq = sb("wq", [P, NK, D])
        w_mean = sb("w_mean", [P, NK * H])
        gb = sb("gb", [P, 2])
        sq, rstd = sb("sq", [P, 4, HALF]), sb("rstd", [P, 4, HALF])
        qn, qf = sb("qn", [P, 2, HALF]), sb("qf", [P, 2, HALF])
        q_hi = [sb(f"q_hi{i}", [P, HALF], F32R) for i in range(2)]
        q_lo = [sb(f"q_lo{i}", [P, HALF], F32R) for i in range(2)]
        ps_q = [ps(f"q{i}", [P, 512]) for i in range(4)]
        ps_r = [ps(f"r{i}", [P, 512]) for i in range(4)]
        w_in, w_done, dch = sem(tag + "_w_in"), sem(tag + "_w_done"), sem(tag + "_dch")
        q_done, sq_done, var_done = sem(tag + "_q_done"), sem(tag + "_sq"), sem(tag + "_var")
        ln_done, rstd_done, qf_done = sem(tag + "_ln"), sem(tag + "_rstd"), sem(tag + "_qf")
        hi_done, lo_done = sem(tag + "_hi"), sem(tag + "_lo")
        q_stored = [sem(f"{tag}_stored{i}") for i in range(2)]
        n_vector, n_scalar, n_tensor, xT_done = norm_and_transpose(nc, sem, tag, S, T, ps_q + ps_r)
        block = ctx.enter_context(nc.Block())
        steps = [(m, h) for m in range(NK) for h in range(2)]

        @block.sync
        def _(sp):
            sp.dma_start(wq[:], A[f"wT_q{L}"].rearrange("(c p) n -> p c n", p=P)).then_inc(w_in, 16)
            for g in range(NG):
                load_kv(sp, A, S, KV, L, 0, g)
            for i, (m, h) in enumerate(steps):
                sp.wait_ge(lo_done, i + 1)
                sp.wait_ge(hi_done, i + 1)
                for part, t in enumerate((q_hi, q_lo)):
                    sp.dma_start(S["Q"][part, m * P:(m + 1) * P, h * HALF:(h + 1) * HALF], t[i % 2][:].bitcast(F32)).then_inc(q_stored[i % 2], 16)
            for i in range(2):
                sp.wait_ge(q_stored[i], 32 * len(steps) // 2)
            for loaded in KV["loaded"]:
                sp.wait_ge(loaded, 5 * 16)

        @block.tensor
        def _(pe):
            n_tensor(pe)
            pe.wait_ge(xT_done, B)
            if L == 0:
                pe.wait_ge(w_done, 1)
            else:
                pe.wait_ge(w_in, 16)

            def variance(i):
                pe.wait_ge(sq_done, i + 1)
                if i >= 4:
                    pe.wait_ge(ln_done, i - 3)
                nc.tensor.matmul(ps_r[i % 4][:, 0:HALF], S["head_mean"][:], sq[:, i % 4], start=True, stop=True).then_inc(var_done, 1)

            for i, (m, h) in enumerate(steps):
                if i >= 4:
                    pe.wait_ge(qf_done, i - 3)
                for k in range(NK):
                    ins = nc.tensor.matmul(ps_q[i % 4][:, 0:HALF], wq[:, k, m * P:(m + 1) * P],
                                           xT[:, k, h * HALF:(h + 1) * HALF], start=k == 0, stop=k == NK - 1)
                ins.then_inc(q_done, 1)
                if L == 0 and i % 2:
                    variance(i - 1)
                    variance(i)

        @block.scalar
        def _(act):
            n_scalar(act)

            def squares(pair):
                for i in (2 * pair, 2 * pair + 1):
                    act.wait_ge(q_done, i + 1)
                    if i >= 4:
                        act.wait_ge(var_done, i - 3)
                    nc.scalar.activation(sq[:, i % 4], ps_q[i % 4][:, 0:HALF], ACT.Square).then_inc(sq_done, 1)

            if L == 0:
                for pair in range(len(steps) // 2):
                    squares(pair)
                    for i in (2 * pair, 2 * pair + 1):
                        act.wait_ge(var_done, i + 1)
                        if i >= 4:
                            act.wait_ge(qf_done, i - 3)
                        nc.scalar.activation(rstd[:, i % 4], ps_r[i % 4][:, 0:HALF], ACT.Ln, bias=S["eps"][:, 0:1]).then_inc(ln_done, 1)
                    for i in (2 * pair, 2 * pair + 1):
                        act.wait_ge(ln_done, i + 1)
                        nc.scalar.activation(rstd[:, i % 4], rstd[:, i % 4], ACT.Exp, scale=-0.5).then_inc(rstd_done, 1)

        @block.vector
        def _(dve):
            link = Chain(dve, dch).step

            def centre_weights():
                heads = wq[:].rearrange("p c (h d) -> p (c h) d", d=HD)
                dve.wait_ge(w_in, 16)
                link(nc.vector.tensor_reduce(w_mean[:], heads, axis=AX, op=ALU.add))
                link(nc.vector.tensor_scalar(w_mean[:], w_mean[:], 1.0 / HD, None, ALU.mult))
                link(nc.vector.tensor_scalar(gb[:], S["cols"][:, C_LNG:C_LNB + 1], L0_SCALE, None, ALU.mult))
                nc.vector.tensor_tensor(heads, heads, w_mean[:].unsqueeze(2).broadcast_to([P, NK * H, HD]), ALU.subtract).then_inc(w_done, 1)

            n_vector(dve, link, centre_weights if L == 0 else None)
            for i, (m, h) in enumerate(steps):
                if i >= 2:
                    dve.wait_ge(lo_done, i - 1)
                if L == 0:
                    dve.wait_ge(rstd_done, i + 1)
                    link(nc.vector.tensor_tensor(qn[:, i % 2], ps_q[i % 4][:, 0:HALF], rstd[:, i % 4], ALU.mult))
                    nc.vector.tensor_scalar(qf[:, i % 2], qn[:, i % 2], gb[:, 0:1], gb[:, 1:2], ALU.mult, ALU.add).then_inc(qf_done, 1)
                else:
                    dve.wait_ge(q_done, i + 1)
                    nc.vector.tensor_scalar(qf[:, i % 2], ps_q[i % 4][:, 0:HALF], S["cols"][:, C_BQ + m:C_BQ + m + 1], -L1_SCALE,
                                            ALU.add, ALU.mult).then_inc(qf_done, 1)
                dve.wait_ge(qf_done, i + 1)
                if i >= 2:
                    dve.wait_ge(q_stored[i % 2], 32 * (i // 2))
                nc.vector.tensor_copy(q_hi[i % 2][:], qf[:, i % 2]).then_inc(hi_done, 1)
                dve.wait_ge(hi_done, i + 1)
                nc.vector.tensor_tensor(q_lo[i % 2][:], qf[:, i % 2], q_hi[i % 2][:], ALU.subtract).then_inc(lo_done, 1)


def kv_tiles(nc, ctx, sem, L):
    sb = lambda name, shape, dt: [ctx.enter_context(nc.sbuf_tensor(f"a{L}_{name}{i}", shape, dt)) for i in range(NG)]
    return {"k_st": sb("k_st", [3 * HD, GH, SK], F32R), "q_st": sb("q_st", [3 * HD, GH, SQ], F32R), "v": sb("v", [P, KC, P], F32),
            "loaded": [sem(f"a{L}_loaded{i}") for i in range(NG)]}


STACK = ((0, 0), (0, 1), (1, 0))


def load_kv(sp, A, S, T, L, b, g):
    for quad, (_, part) in enumerate(STACK):
        sp.dma_start(T["k_st"][g][quad * HD:(quad + 1) * HD].bitcast(F32), S["K"][L][part, g * P:(g + 1) * P, b, :]
                     .rearrange("(h d) t -> d h t", d=HD)).then_inc(T["loaded"][g], 16)
    sp.dma_start(T["v"][g][:, 0:KC - 1, :], S["V"][L][b, 0:(KC - 1) * P, g * P:(g + 1) * P]
                 .rearrange("(c p) d -> p c d", p=P)).then_inc(T["loaded"][g], 16)
    sp.dma_start(T["v"][g][0:KTAIL, KC - 1, :], S["V"][L][b, (KC - 1) * P:SK, g * P:(g + 1) * P]).then_inc(T["loaded"][g], 16)


def load_q(sp, S, T, b, g):
    for quad, (part, _) in enumerate(STACK):
        sp.dma_start(T["q_st"][g][quad * HD:(quad + 1) * HD].bitcast(F32), S["Q"][part, g * P:(g + 1) * P, bass.ds(b * SQ, SQ)]
                     .rearrange("(h d) t -> d h t", d=HD)).then_inc(T["loaded"][g], 16)


LOADS = 5 + 3


def attention(nc, sem, L, A, S, T, W):
    tag = f"a{L}"
    with ExitStack() as ctx:
        sb = lambda name, shape, dt=F32: ctx.enter_context(nc.sbuf_tensor(f"{tag}_{name}", shape, dt))
        ps = lambda name, shape: ctx.enter_context(nc.psum_tensor(f"{tag}_{name}", shape, F32))
        k_st, q_st, v_sb, loaded = T["k_st"], T["q_st"], T["v"], T["loaded"]
        prob = [sb(f"prob{i}", [SQ, KC * P]) for i in range(2)]
        probT = [sb(f"probT{i}", [P, KC * SQ]) for i in range(2)]
        scored = [sb(f"scored{i}", [SQ, SK]) for i in range(4)] if L else None
        mask_raw = sb("mask_raw", [SQ, SK], I32) if L else None
        masked = sb("masked", [SQ, SK]) if L else None
        nmax = sb("nmax", [SQ, 4])
        wait_here = sb("wait_here", [SQ, 2])
        rsum = sb("rsum", [SQ, 2, GH])
        rinv = sb("rinv", [SQ, GH])
        rep = sb("rep", [SQ, P])
        rinvT = sb("rinvT", [P, SQ])
        psS = [ps(f"s{i}", [P, 1024]) for i in range(2)]
        psT = [ps(f"t{i}", [P, 512]) for i in range(2)]
        psO = [ps(f"o{i}", [P, 512]) for i in range(2)]
        row = slice(KOFF, KOFF + SK)
        CV = 1
        mask_in, mask_done = sem(tag + "_mask_in"), sem(tag + "_mask_done")
        zeroed = sem(tag + "_zeroed")
        s_done, max_done, exp_done = sem(tag + "_s"), sem(tag + "_max"), sem(tag + "_exp")
        tv_done, ts_done = sem(tag + "_tvd"), sem(tag + "_tsd")
        tv_out, ts_out = sem(tag + "_tv"), sem(tag + "_ts")
        pv_done, rinv_done, rep_done = sem(tag + "_pv"), sem(tag + "_rinv"), sem(tag + "_rep")
        rt_done = [sem(f"{tag}_rt{i}") for i in range(NG)]
        rinvT_done = sem(tag + "_rinvT")
        normed = sem(tag + "_normed")
        bv_done = sem(tag + "_bv")
        block = ctx.enter_context(nc.Block())

        def bodies(eng, body):
            body(0, first=True)
            with eng.Fori(1, B - 1) as b:
                body(b)
            body(B - 1, last=True)

        @block.sync
        def _(sp):
            def load(b, kv=True):
                if L:
                    sp.wait_ge(mask_done, b + PRIMED)
                    sp.dma_start(mask_raw[:], A["mask"][bass.ds(b, 1), :].broadcast_to([SQ, SK])).then_inc(mask_in, 16)
                for g in range(NG):
                    if kv:
                        sp.wait_ge(rt_done[g], b + PRIMED)
                    load_q(sp, S, T, b, g)
                    if kv:
                        load_kv(sp, A, S, T, L, b, g)

            load(0, kv=False)
            load_output_weights(sp, A, S, W, L)
            with sp.Fori(1, B) as b:
                load(b)
            sp.wait_ge(W["in"], 32)

        @block.tensor
        def _(pe):
            prime(pe, *rt_done)

            def body(b, first=False, last=False):
                def scores(i):
                    n, g = b * H + i, i % H // GH
                    if i % GH == 0:
                        pe.wait_ge(loaded[g], (b + i // H + 1) * 16 * LOADS)
                    if not (first and i < 2):
                        pe.wait_ge(max_done if L else exp_done, n - 1)
                    for col, w, at in key_halves():
                        ins = nc.tensor.matmul(psS[i % 2][0:SQ, at:at + w], q_st[g][:, i % GH, :],
                                               k_st[g][:, i % GH, col:col + w], start=True, stop=True)
                    ins.then_inc(s_done, 1)

                def transposes(i):
                    n = b * H + i
                    pe.wait_ge(exp_done, n + 1)
                    for part, chunks, out_done, done in ((0, range(CV), tv_out, tv_done), (1, range(CV, KC), ts_out, ts_done)):
                        pe.wait_ge(out_done, n + PRIMED)
                        for c in chunks:
                            at = (c - chunks[0]) * SQ
                            ins = nc.tensor.transpose(psT[part][:, at:at + SQ], prob[i % 2][:, c * P:(c + 1) * P], S["ident"][0:SQ, 0:SQ])
                        ins.then_inc(done, 1)

                def values(i):
                    n, g, j = b * H + i, i % H // GH, i % GH
                    pe.wait_ge(tv_out, n + 1 + PRIMED)
                    pe.wait_ge(ts_out, n + 1 + PRIMED)
                    if j == 0 and not (first and g < 2):
                        pe.wait_ge(normed, b * NG + (i // GH - 1))
                    for c in range(KC):
                        w = chunk_rows(c)
                        ins = nc.tensor.matmul(psO[g % 2][j * HD:(j + 1) * HD, 0:SQ], v_sb[g][0:w, c, j * HD:(j + 1) * HD],
                                               probT[i % 2][0:w, c * SQ:(c + 1) * SQ], start=c == 0, stop=c == KC - 1)
                    ins.then_inc(pv_done, 1)

                def sums_transpose(g):
                    pe.wait_ge(rep_done, b * NG + (g + 1) + PRIMED)
                    nc.tensor.transpose(psO[g % 2][:, P:P + SQ], rep[:], S["ident"][0:SQ, 0:SQ]).then_inc(rt_done[g % NG], 1)

                if first:
                    scores(0)
                    scores(1)
                for i in range(H):
                    if not (last and i + 2 >= H):
                        scores(i + 2)
                    transposes(i)
                    if not (first and i == 0):
                        values(i - 1)
                    if i % GH == 1 and not (first and i == 1):
                        sums_transpose(i // GH - 1)
                if last:
                    values(H - 1)
                    sums_transpose(NG - 1)

            pe.wait_ge(zeroed, 2)
            bodies(pe, body)

        @block.scalar
        def _(act):
            prime(act, ts_out)

            def body(b, first=False, last=False):
                def second_part(i):
                    n = b * H + i
                    act.wait_ge(ts_done, n + 1)
                    if not (first and i < 2):
                        act.wait_ge(pv_done, n - 1)
                    nc.scalar.copy(probT[i % 2][:, CV * SQ:], psT[1][:, 0:(KC - CV) * SQ]).then_inc(ts_out, 1)

                for i in range(H):
                    n, g = b * H + i, i // GH
                    act.wait_ge(max_done, n + 1)
                    if not (first and i < 2):
                        act.wait_ge(ts_done, n - 1)
                    if i % GH == 0 and not (first and g < 2):
                        act.wait_ge(rinv_done, b * NG + (g - 1))
                    src = scored[i % 4][:] if L else psS[i % 2][0:SQ, row]
                    nc.scalar.activation(prob[i % 2][:, 0:SK], src, ACT.Exp, bias=nmax[:, i % 4:i % 4 + 1], scale=-1.0 if L else 1.0,
                                         accum_out=rsum[:, g % 2, i % GH:i % GH + 1]).then_inc(exp_done, 1)
                    if not (first and i == 0):
                        second_part(i - 1)
                if last:
                    second_part(H - 1)

            bodies(act, body)

        @block.gpsimd
        def _(pool):
            prime(pool, rep_done)
            with pool.Fori(0, B) as b:
                for g in range(NG):
                    pool.wait_ge(rinv_done, b * NG + (g + 1))
                    pool.wait_ge(rt_done[(g - 1) % NG], b + (1 if g else 0) + PRIMED)
                    by_head = lambda t: t.rearrange("p (h d) -> p h d", h=GH)
                    nc.gpsimd.tensor_tensor(by_head(rep[:]), rinv[:].unsqueeze(2).broadcast_to([SQ, GH, HD]), by_head(S["ones"][:]),
                                            ALU.mult).then_inc(rep_done, 1)

        @block.vector
        def _(dve):
            prime(dve, mask_done, tv_out)
            for t in prob:
                nc.vector.memset(t[:, SK:], 0.0).then_inc(zeroed, 1)

            def body(b, first=False, last=False):
                def mask(after):
                    dve.wait_ge(mask_in, (b + after + 1) * 16)
                    if after:
                        dve.wait_ge(max_done, b * H + H)
                    nc.vector.tensor_scalar(masked[:], mask_raw[:], 0.0, NEG, ALU.is_equal, ALU.mult).then_inc(mask_done, 1)
                    dve.wait_ge(mask_done, b + (after + 1 + PRIMED))

                def row_max(i):
                    n = b * H + i
                    dve.wait_ge(s_done, n + 1)
                    if not (first and i < 4):
                        dve.wait_ge(exp_done, n - 3)
                    out = nmax[:, i % 4:i % 4 + 1]
                    if L:
                        nc.vector.memset(wait_here[:, i % 2:i % 2 + 1], 0.0)
                        nc.vector.tensor_tensor_reduce(out=scored[i % 4][:], in0=psS[i % 2][0:SQ, row], in1=masked[:], scale=1.0,
                                                       scalar=3.0e38, op0=ALU.add, op1=ALU.min, accum_out=out).then_inc(max_done, 1)
                    else:
                        nc.vector.tensor_reduce(out, psS[i % 2][0:SQ, row], axis=AX, op=ALU.max, negate=True).then_inc(max_done, 1)

                def first_part(i):
                    n = b * H + i
                    dve.wait_ge(tv_done, n + 1)
                    if not (first and i < 2):
                        dve.wait_ge(pv_done, n - 1)
                    nc.vector.tensor_copy(probT[i % 2][:, 0:CV * SQ], psT[0][:, 0:CV * SQ]).then_inc(tv_out, 1)

                def reciprocal_sums(g):
                    G = b * NG + g
                    dve.wait_ge(exp_done, b * H + (g + 1) * GH)
                    if not (first and g == 0):
                        dve.wait_ge(rep_done, G + PRIMED)
                    nc.vector.reciprocal(rinv[:], rsum[:, g % 2, :]).then_inc(rinv_done, 1)

                def normalise(g):
                    G = b * NG + g
                    dve.wait_ge(rt_done[g % NG], b + (g // NG + 1 + PRIMED))
                    nc.vector.tensor_copy(rinvT[:], psO[g % 2][:, P:P + SQ]).then_inc(rinvT_done, 1)
                    dve.wait_ge(rinvT_done, G + 1)
                    out = S["attnT"][:, g % NG, bass.ds(b * SQ + g // NG * SQ, SQ)]
                    nc.vector.tensor_tensor(out, psO[g % 2][:, 0:SQ], rinvT[:], ALU.mult).then_inc(normed, 1)

                if first:
                    if L:
                        mask(0)
                    row_max(0)
                    row_max(1)
                for i in range(H):
                    if not (last and i + 2 >= H):
                        if L and i + 2 == H:
                            mask(1)
                        row_max(i + 2)
                    first_part(i)
                    if i % GH == GH - 1:
                        reciprocal_sums(i // GH)
                    if i % GH == 2 and not (first and i == 2):
                        normalise(i // GH - 1)
                if last:
                    normalise(NG - 1)

            bodies(dve, body)
            if L:
                dve.wait_ge(normed, B * NG)
                for k in range(NK):
                    nc.vector.tensor_scalar(S["attnT"][:, k, :], S["attnT"][:, k, :], S["cols"][:, C_BV + k:C_BV + k + 1], None, ALU.add)\
                        .then_inc(bv_done, 1)


def load_output_weights(sp, A, S, W, L):
    sp.dma_start(W["wo"][:], A[f"wT_o{L}"].rearrange("(c p) n -> p c n", p=P)).then_inc(W["in"], 16)
    sp.dma_start(W["bias"][:], A[f"bo{L}"].broadcast_to([SQ, D])).then_inc(W["in"], 16)


def output(nc, sem, L, A, S, W):
    tag = f"o{L}"
    with ExitStack() as ctx:
        sb = lambda name, shape, dt=F32: ctx.enter_context(nc.sbuf_tensor(f"{tag}_{name}", shape, dt))
        wo, bias, w_in = W["wo"], W["bias"], W["in"]
        t = sb("t", [SQ, 2, D])
        psY = [ctx.enter_context(nc.psum_tensor(f"{tag}_y{i}", [P, 512], F32)) for i in range(B)]
        y_done, dch, x_done, stats_done = sem(tag + "_y"), sem(tag + "_dch"), sem(tag + "_x"), sem(tag + "_stats")
        block = ctx.enter_context(nc.Block())

        @block.tensor
        def _(pe):
            pe.wait_ge(w_in, 32)
            for b in range(B):
                for k in range(NK):
                    ins = nc.tensor.matmul(psY[b][0:SQ, :], S["attnT"][:, k, b * SQ:(b + 1) * SQ], wo[:, k, :], start=k == 0, stop=k == NK - 1)
                ins.then_inc(y_done, 1)

        @block.vector
        def _(dve):
            link = Chain(dve, dch).step
            dve.wait_ge(w_in, 32)
            for b in range(B):
                dve.wait_ge(y_done, b + 1)
                link(nc.vector.tensor_tensor(t[:, b % 2], psY[b][0:SQ, :], bias[:], ALU.add))
                nc.vector.scalar_tensor_tensor(S["x"][:, b, :], t[:, b % 2], S["gates"][0:SQ, L:L + 1], S["x"][:, b, :],
                                               ALU.mult, ALU.add).then_inc(x_done, 1)
                dve.wait_ge(x_done, b + 1)
                nc.vector.bn_stats(S["stats"][:, b, :], S["x"][:, b, :]).then_inc(stats_done, 1)
            dve.wait_ge(stats_done, B)


def top_k(nc, link, vals, n, k, mx, gt, eq, ca, cb, cnt, sel):
    for b in range(B):
        ins = nc.vector.max(mx[:, b, :], vals[:, b, :])
    link(ins)
    thr = mx[:, :, k - 1:k].broadcast_to([SQ, B, n])
    nc.vector.tensor_tensor(gt, vals, thr, ALU.is_gt)
    link(nc.vector.tensor_tensor(eq, vals, thr, ALU.is_equal))
    src, dst, d = eq, ca, 1
    while d < n:
        nc.vector.tensor_copy(dst[:, :, 0:d], src[:, :, 0:d])
        link(nc.vector.tensor_tensor(dst[:, :, d:n], src[:, :, d:n], src[:, :, 0:n - d], ALU.add))
        src, dst, d = dst, (cb if dst is ca else ca), 2 * d
    link(nc.vector.tensor_reduce(cnt, gt, axis=AX, op=ALU.add))
    link(nc.vector.tensor_tensor(dst, src, cnt.unsqueeze(2).broadcast_to([SQ, B, n]), ALU.add))
    link(nc.vector.scalar_tensor_tensor(dst, dst, float(k), eq, ALU.is_le, ALU.mult))
    link(nc.vector.tensor_tensor(sel, dst, gt, ALU.add))


def positions(nc, dve, link, sh, pos, tot, cnt_e, ps_pos, ps_tot):
    view = lambda t: t[0:SQ, 0:B * sh[2]].rearrange("p (b e) -> p b e", b=B)
    link(nc.vector.tensor_copy(pos, view(ps_pos)))
    link(nc.vector.tensor_copy(tot, view(ps_tot)))
    for b in range(1, B):
        link(nc.vector.tensor_tensor(pos[:, b:, :], pos[:, b:, :], tot[:, b - 1:b, :].broadcast_to([SQ, B - b, sh[2]]), ALU.add))
    link(nc.vector.tensor_reduce(cnt_e, tot.rearrange("p b e -> p e b"), axis=AX, op=ALU.add))


class Place:

    def __init__(self, q, j):
        self.t, self.q, self.j = q * 4 + j, q, j
        self.half, self.i = q * 2 + j // 2, j % 2

    def next(self, n=1):
        return Place(self.q + (self.j + n) // 4, (self.j + n) % 4)


def block(t):
    return Place(t // 4, t % 4)


def blocks(eng, first, end, step):
    n = (end - first) // 4
    if n:
        with eng.Fori(0, n) as it:
            for i in range(4):
                step(Place(it + (first + i) // 4, (first + i) % 4))
    for t in range(first + 4 * n, end):
        step(block(t))


def experts(nc, sem, L, A, S, out):
    tag = f"f{L}"
    HALF = NT // 2
    E = (E0, E1)[L]
    NB = (MB0, E1)[L]
    TOP = (TOP0, TOP1)[L]
    AHEAD = 3
    HC = (I0 // P, NI1)[L]
    sh = [SQ, B, E]
    with ExitStack() as ctx:
        sb = lambda name, shape, dt=F32: ctx.enter_context(nc.sbuf_tensor(f"{tag}_{name}", shape, dt))
        bank = lambda name: ctx.enter_context(nc.psum_tensor(f"{tag}_{name}", [P, 512], F32))
        T = norm_tiles(sb)
        xT, xn = T["xT"], T["xn"]
        gate_w = sb("gate_w", [P, NK, E])
        sc, gt, eq, ca, cb, sel, pos, tot = (sb(n, sh) for n in ("sc", "gt", "eq", "ca", "cb", "sel", "pos", "tot"))
        mx, cnt = sb("mx", [SQ, B, 8]), sb("cnt", [SQ, B])
        cnt_e, nblk, base, base2 = (sb(n, [SQ, E]) for n in ("cnt_e", "nblk", "base", "base2"))
        block_no, ended = sb("block_no", [SQ, NB]), sb("ended", [SQ, NB, E])
        expert_f, expert_i = sb("expert_f", [SQ, NB]), sb("expert_i", [SQ, NB], I32)
        slot = sb("slot", sh)
        slot8 = sb("slot8", [SQ, B, 8])
        is_slot = sb("is_slot", [SQ, B, TOP, E])
        entry = sb("entry", [SQ, B, TOP, 2])
        unused, at_f = sb("unused", [SQ, B, TOP]), sb("at_f", [SQ, B, TOP])
        at_row = sb("at_row", [SQ, B * TOP], I32)
        empty = sb("empty", [P, NB, 2])
        info = sb("info", [P, NB, 2])
        g_row, s_row = ([sb(f"{n}{i}", [P, 1], I32) for i in range(k)] for n, k in (("g_row", 4), ("s_row", 2)))
        up_w = [sb(f"up_w{i}", [P, NK, (2 * I0, HID1)[L]]) for i in range(2 - L)]
        dn_w = [sb(f"dn_w{i}", [P, HC, D]) for i in range(2)]
        hid = [sb(f"hid{i}", [P, HC * P]) for i in range((2, 4)[L])]
        hidT = [sb(f"hidT{i}", [P, HC, P]) for i in range(2)]
        yw = [sb(f"yw{i}", [P, D]) for i in range(2)]
        acc = sb("acc", [SQ, B, D])
        zero, wait_here = sb("zero", [P, D]), sb("wait_here", [1, 2])
        if L:
            h_row = [sb(f"h_row{i}", [SQ, HID1]) for i in range(2)]
        else:
            xg = [sb(f"xg{i}", [P, D]) for i in range(4)]
            xgT = [sb(f"xgT{i}", [P, NK, P]) for i in range(2)]
            sg = sb("sg", [P, I0])
            e_bias = sb("e_bias", [SQ, E0])
            sfc = sb("sfc", sh)
            gsc, gsel = sb("gsc", [SQ, B, GRP0]), sb("gsel", [SQ, B, GRP0])
            sh_up, sh_dn = sb("sh_up", [P, NK, 4 * I0]), sb("sh_dn", [P, NK, D])
            sh_g, sh_u = sb("sh_g", [P, 2, HALF]), sb("sh_u", [P, 2, HALF])
            sh_h = sb("sh_h", [P, NK, NT])
        src_rows, got = (S["h_rows"], hid) if L else (S["x_rows"], xg)
        acc_rows, table = S["acc_rows"], S["table"][L]
        row_of = info[:].bitcast(I32)

        psX, psY = bank("x"), bank("y")
        psU, psH = [bank(f"u{i}") for i in range(2)], [bank(f"h{i}") for i in range(2)]
        ps8, ps9 = bank("r"), bank("s")
        r_in, dch = sem(tag + "_r_in"), sem(tag + "_dch")
        logit_done, exp_done, sel_done, pos_done, lm_done, base_done = (sem(f"{tag}_{n}") for n in ("logit", "exp", "sel", "pos", "lm", "base"))
        up_in, dn_in = ([sem(f"{tag}_{n}{i}") for i in range(2)] for n in ("up_in", "dn_in"))
        x_stored, acc_set, zeroed = sem(tag + "_x_stored"), sem(tag + "_acc_set"), sem(tag + "_zeroed")
        empty_done, filled, entry_done = sem(tag + "_empty"), sem(tag + "_filled"), sem(tag + "_entry")
        entered, info_in, idx_done = sem(tag + "_entered"), [sem(f"{tag}_info{i}") for i in range(2)], sem(tag + "_idx")
        gathered, scattered = [sem(f"{tag}_gath{i}") for i in range(4)], sem(tag + "_scat")
        xtr_done, xT_out, up_done, silu_done, h_done = (sem(f"{tag}_{n}") for n in ("xtr", "xTo", "up", "silu", "h"))
        htr_done, hT_out, dn_done, yw_done = (sem(f"{tag}_{n}") for n in ("htr", "hTo", "dn", "yw"))
        got_out = (xtr_done, htr_done)[L]
        hd_done, hd_out, h_stored = sem(tag + "_hd"), sem(tag + "_hdo"), [sem(f"{tag}_hst{i}") for i in range(2)]
        hT_half, waited = sem(tag + "_hT_half"), sem(tag + "_waited")
        added = sem(tag + "_added")
        acc_in = [sem(f"{tag}_acc_in{j}") for j in range(4)]
        x_done, stored, stats_done = sem(tag + "_x"), sem(tag + "_stored"), sem(tag + "_stats")
        if L == 0:
            sh_in, sg_done, su_done, sh_done, shg_out, shy_done, shy_out = \
                (sem(f"{tag}_sh{n}") for n in ("in", "g", "u", "h", "go", "y", "yo"))
        n_vector, n_scalar, n_tensor, xT_done = norm_and_transpose(nc, sem, tag, S, T, [psX, psY, *psU, *psH, ps8, ps9])
        engines = ctx.enter_context(nc.Block())
        sh_units = [(j, h) for j in range(NK) for h in range(2)]

        SPLIT = 5

        def shared_products(eng, ops, first, end):
            for u in range(first, end):
                j, h = sh_units[u]
                eng.wait_ge(shg_out, u + 1)
                eng.wait_ge(lm_done, u + 1)
                ops.tensor_tensor(sh_h[:, j, h * HALF:(h + 1) * HALF], sh_g[:, u % 2], sh_u[:, u % 2], ALU.mult).then_inc(sh_done, 1)

        @engines.sync
        def _(sp):
            sp.dma_start(gate_w[:], A[f"routerT{L}"].rearrange("(c p) n -> p c n", p=P)).then_inc(r_in, 16)
            if L == 0:
                sp.dma_start(e_bias[:], A["e_bias"].broadcast_to([SQ, E0])).then_inc(r_in, 16)
                sp.dma_start(sh_up[:], A["sh_up"]).then_inc(sh_in, 16)
                sp.dma_start(sh_dn[:], A["sh_dn"]).then_inc(sh_in, 16)
            else:
                sp.dma_start(up_w[0][:], A["wgT1"].rearrange("(c p) n -> p c n", p=P)).then_inc(up_in[0], 16)
            sp.wait_ge(empty_done, 2)
            sp.dma_start(table[0:NB * P, :].rearrange("(t p) c -> p t c", p=P), empty[:]).then_inc(filled, 16)
            sp.wait_ge(zeroed, 1)
            sp.dma_start(src_rows[NT:NT + P, 0:D], zero[:]).then_inc(x_stored, 16)
            sp.dma_start(acc_rows[NT:NT + P, :], zero[:]).then_inc(acc_set, 16)
            if L == 0:
                sp.wait_ge(T["xn_done"], B)
                sp.dma_start(src_rows[0:NT, :].rearrange("(b t) d -> t b d", t=SQ), xn[:]).then_inc(x_stored, 16)
            else:
                sp.dma_start(src_rows[NT:NT + P, D:2 * D], zero[:]).then_inc(x_stored, 16)
                for b in range(B):
                    sp.dma_start(acc_rows[b * SQ:(b + 1) * SQ, :], zero[0:SQ, :]).then_inc(acc_set, 16)

            def expert(t):
                return sp.value_load(expert_i[0:1, bass.ds(t, 1)], min_val=0, max_val=E0 - 1) if L == 0 else t

            def load_up(e, i):
                sp.dma_start(up_w[i][:], A["gu"][e]).then_inc(up_in[i], 16)

            def load_dn(e, i):
                sp.dma_start(dn_w[i][:], A[("dn", "wd1")[L]][e]).then_inc(dn_in[i], 16)

            if L == 0:
                sp.wait_ge(base_done, 1)
            for t in range(2):
                e = expert(t)
                if L == 0:
                    load_up(e, t)
                load_dn(e, t)
            if L == 0:
                for b in range(B):
                    sp.wait_ge(shy_out, b + 1)
                    sp.dma_start(acc_rows[b * SQ:(b + 1) * SQ, :], acc[:, b, :]).then_inc(acc_set, 16)

            def store_hidden(batches):
                for b in batches:
                    sp.wait_ge(hd_out, b + 1)
                    sp.dma_start(src_rows[b * SQ:(b + 1) * SQ, :], h_row[b % 2][:]).then_inc(h_stored[b % 2], 16)

            if L:
                store_hidden(range(B - 2))
            sp.wait_ge(entered, 16 * B * TOP)
            for i, (t0, t1) in enumerate(((0, AHEAD), (AHEAD, NB))):
                sp.dma_start(info[:, t0:t1, :], table[t0 * P:t1 * P, :].rearrange("(t p) c -> p t c", p=P)).then_inc(info_in[i], 16)
            if L:
                store_hidden(range(B - 2, B))

            def load(p):
                t, i = p.t, p.i
                e = expert(t)
                if L == 0:
                    sp.wait_ge(up_done, t - 1)
                    load_up(e, i)
                sp.wait_ge(dn_done, t - 1)
                load_dn(e, i)

            blocks(sp, 2, NB, load)
            sp.wait_ge(scattered, 16 * NB)
            for j in range(4):
                two = slice(2 * j, 2 * j + 2)
                sp.dma_start(acc[:, two, :], acc_rows[2 * j * SQ:2 * (j + 1) * SQ, :].rearrange("(b t) d -> t b d", t=SQ)).then_inc(acc_in[j], 16)
            if L:
                for b in range(B):
                    sp.wait_ge(x_done, b + 1)
                    sp.dma_start(out[b], S["x"][:, b, :]).then_inc(stored, 16)
                sp.wait_ge(stored, 16 * B)

        @engines.tensor
        def _(pe):
            n_tensor(pe)
            pe.wait_ge(xT_done, B)
            pe.wait_ge(r_in, (32, 16)[L])
            for b in range(B):
                for k in range(NK):
                    ins = nc.tensor.matmul(ps8[0:SQ, b * E:(b + 1) * E], xT[:, k, b * SQ:(b + 1) * SQ], gate_w[:, k, :],
                                           start=k == 0, stop=k == NK - 1)
            ins.then_inc(logit_done, 1)

            def counts():
                pe.wait_ge(sel_done, 1)
                flat = gt[:].rearrange("p b e -> p (b e)")
                nc.tensor.matmul(psX[0:SQ, 0:B * E], S["upto"][:], flat, start=True, stop=True)
                nc.tensor.matmul(psY[0:SQ, 0:B * E], S["ones"][:, 0:SQ], flat, start=True, stop=True).then_inc(pos_done, 1)

            if L:
                pe.wait_ge(up_in[0], 16)
                for b in range(B):
                    if b == 2:
                        counts()
                    if b >= 2:
                        pe.wait_ge(hd_out, b - 1)
                    for u, ps in enumerate((psU, psH)[b % 2]):
                        for k in range(NK):
                            ins = nc.tensor.matmul(ps[0:SQ, :], xT[:, k, b * SQ:(b + 1) * SQ], up_w[0][:, k, u * 512:(u + 1) * 512],
                                                   start=k == 0, stop=k == NK - 1)
                    ins.then_inc(hd_done, 1)
            else:
                pe.wait_ge(sh_in, 32)
                for u, (j, h) in enumerate(sh_units):
                    if u == 2:
                        counts()
                    if u >= 2:
                        pe.wait_ge(shg_out, u - 1)
                    for which, banks, done in ((0, psU, sg_done), (1, psH, su_done)):
                        for k in range(NK):
                            at = which * 2 * I0 + j * P
                            ins = nc.tensor.matmul(banks[u % 2][:, 0:HALF], sh_up[:, k, at:at + P], xT[:, k, h * HALF:(h + 1) * HALF],
                                                   start=k == 0, stop=k == NK - 1)
                        ins.then_inc(done, 1)
            if L == 0:
                pe.wait_ge(sh_done, len(sh_units))
                for b in range(B):
                    if b >= 2:
                        pe.wait_ge(shy_out, b - 1)
                    for j in range(NK):
                        ins = nc.tensor.matmul(psU[b % 2][0:SQ, :], sh_h[:, j, b * SQ:(b + 1) * SQ], sh_dn[:, j, :],
                                               start=j == 0, stop=j == NK - 1)
                    ins.then_inc(shy_done, 1)
                pe.wait_ge(shy_out, B)

            def x_transpose(p):
                t = p.t
                pe.wait_ge(gathered[p.j], (p.q + 1) * 16)
                pe.wait_ge(xT_out, t + PRIMED)
                for k in range(NK):
                    ins = nc.tensor.transpose(psX[:, k * P:(k + 1) * P], xg[p.j][:, k * P:(k + 1) * P], S["ident"][:])
                ins.then_inc(xtr_done, 1)

            def up(p):
                t, half, i = p.t, p.half, p.i
                pe.wait_ge(xT_out, t + 1 + PRIMED)
                pe.wait_ge(up_in[i], (half + 1) * 16)
                pe.wait_ge(h_done, t + PRIMED)
                for k in range(NK):
                    ins = nc.tensor.matmul(psU[0][:], xgT[i][:, k, :], up_w[i][:, k, :], start=k == 0, stop=k == NK - 1)
                ins.then_inc(up_done, 1)

            def h_transpose(p):
                t, h = p.t, hid[p.j if L else p.i]
                if L:
                    pe.wait_ge(gathered[p.j], (p.q + 1) * 16)
                else:
                    pe.wait_ge(h_done, t + 1 + PRIMED)
                pe.wait_ge(hT_out, t + PRIMED)
                for j in range(HC):
                    ins = nc.tensor.transpose(psH[j // 4][:, j % 4 * P:(j % 4 + 1) * P], h[:, j * P:(j + 1) * P], S["ident"][:])
                ins.then_inc(htr_done, 1)

            def down(p):
                t, half, i = p.t, p.half, p.i
                pe.wait_ge(hT_out, t + 1 + PRIMED)
                pe.wait_ge(dn_in[i], (half + 1) * 16)
                pe.wait_ge(yw_done, t + PRIMED)
                for j in range(HC):
                    ins = nc.tensor.matmul(psY[:], hidT[i][:, j, :], dn_w[i][:, j, :], start=j == 0, stop=j == HC - 1)
                ins.then_inc(dn_done, 1)

            def step(p, first=False, x_too=True):
                up(p)
                if x_too:
                    x_transpose(p.next())
                if not first:
                    down(p.next(-1))
                h_transpose(p)

            def step_1(p):
                h_transpose(p.next())
                down(p)

            if L:
                h_transpose(block(0))
                blocks(pe, 0, NB - 1, step_1)
            else:
                x_transpose(block(0))
                step(block(0), first=True)
                blocks(pe, 1, NB - 1, step)
                step(block(NB - 1), x_too=False)
            down(block(NB - 1))

        @engines.scalar
        def _(act):
            prime(act, xT_out, hT_out, silu_done)
            n_scalar(act)
            act.wait_ge((logit_done, lm_done)[L], 1)
            if L == 0:
                nc.scalar.activation(sc[:], ps8[0:SQ, 0:B * E0].rearrange("p (b e) -> p b e", b=B), ACT.Exp, scale=-1.0).then_inc(exp_done, 1)
                for u, (j, h) in enumerate(sh_units):
                    act.wait_ge(sg_done, u + 1)
                    if u >= 2:
                        act.wait_ge(sh_done, u - 1)
                    nc.scalar.activation(sh_g[:, u % 2], psU[u % 2][:, 0:HALF], ACT.Silu).then_inc(lm_done, 1)
                    act.wait_ge(su_done, u + 1)
                    nc.scalar.copy(sh_u[:, u % 2], psH[u % 2][:, 0:HALF]).then_inc(shg_out, 1)
                for b in range(B):
                    act.wait_ge(shy_done, b + 1)
                    nc.scalar.copy(acc[:, b, :], psU[b % 2][0:SQ, :]).then_inc(shy_out, 1)
            else:
                nc.scalar.activation(sc[:], sc[:], ACT.Exp).then_inc(exp_done, 1)
                for b in range(B):
                    act.wait_ge(hd_done, b + 1)
                    if b >= 2:
                        act.wait_ge(h_stored[b % 2], 16 * (b // 2))
                    ps = (psU, psH)[b % 2]
                    nc.scalar.activation(h_row[b % 2][:, 0:512], ps[0][0:SQ, :], ACT.Silu).then_inc(silu_done, 1)
                    nc.scalar.activation(h_row[b % 2][:, 512:1024], ps[1][0:SQ, :], ACT.Silu).then_inc(hd_out, 1)

            def x_out(p):
                t, i = p.t, p.i
                act.wait_ge(xtr_done, t + 1)
                nc.scalar.copy(xgT[i][:].rearrange("p c t -> p (c t)"), psX[:]).then_inc(xT_out, 1)

            def h_out(p):
                t, i = p.t, p.i
                act.wait_ge(htr_done, t + 1)
                hT = hidT[i][:].rearrange("p c t -> p (c t)")
                if L == 0:
                    nc.scalar.copy(hT, psH[0][:, 0:HC * P]).then_inc(hT_out, 1)
                else:
                    nc.scalar.copy(hT[:, 0:512], psH[0][:]).then_inc(hT_half, 1)
                    nc.scalar.copy(hT[:, 512:1024], psH[1][:]).then_inc(hT_out, 1)

            def step(p, x_too=True):
                t = p.t
                act.wait_ge(up_done, t + 1)
                act.wait_ge(h_done, t + PRIMED)
                nc.scalar.activation(sg[:], psU[0][:, 0:I0], ACT.Silu).then_inc(silu_done, 1)
                if x_too:
                    x_out(p.next())
                h_out(p)

            if L:
                blocks(act, 0, NB, h_out)
            else:
                x_out(block(0))
                blocks(act, 0, NB - 1, step)
                step(block(NB - 1), x_too=False)

        @engines.gpsimd
        def _(pool):
            prime(pool, added, waited)
            nc.gpsimd.memset(zero[:], 0.0).then_inc(zeroed, 1)
            if L == 0:
                shared_products(pool, nc.gpsimd, 0, SPLIT)
            pool.wait_ge(filled, 16)
            pool.wait_ge(entry_done, 3)
            for b in range(B):
                for k in range(TOP):
                    j = b * TOP + k
                    nc.gpsimd.indirect_dma_start(table[:, :], bass.IndirectOffsetOnAxis(ap=at_row[:, j:j + 1], axis=0), entry[:, b, k, :], None)\
                        .then_inc(entered, 16)
            pool.wait_ge(x_stored, 32)
            if L:
                for i in range(2):
                    pool.wait_ge(h_stored[i], 16 * B // 2)

            def gather(p):
                t, i = p.t, p.i
                pool.wait_ge(idx_done, t + 1)
                if not isinstance(t, int) or t >= 4:
                    pool.wait_ge(got_out, t - 3)
                pool.wait_ge(waited, t + PRIMED)
                nc.gpsimd.tensor_tensor(wait_here[:, 0:1], zero[0:1, 0:1], zero[0:1, 0:1], ALU.add).then_inc(waited, 1)
                nc.gpsimd.indirect_dma_start(got[p.j][:], None, src_rows[:, :], bass.IndirectOffsetOnAxis(ap=g_row[p.j][:, 0:1], axis=0))\
                    .then_inc(gathered[p.j], 16)

            def scatter(p):
                t, i = p.t, p.i
                pool.wait_ge(yw_done, t + 1 + PRIMED)
                if not isinstance(t, int) or t:
                    pool.wait_ge(scattered, t * 16)
                pool.wait_ge(added, t + PRIMED)
                nc.gpsimd.tensor_tensor(wait_here[:, 1:2], zero[0:1, 0:1], zero[0:1, 0:1], ALU.add).then_inc(added, 1)
                nc.gpsimd.indirect_dma_start(acc_rows[:, :], bass.IndirectOffsetOnAxis(ap=s_row[i][:, 0:1], axis=0), yw[i][:], None,
                                             compute_op=ALU.add).then_inc(scattered, 16)

            def step(p, gather_too=True):
                if gather_too:
                    gather(p.next(AHEAD))
                scatter(p)

            for t in range(AHEAD):
                gather(block(t))
            pool.wait_ge(acc_set, 16 * (B + 1))
            step(block(0))
            blocks(pool, 1, NB - AHEAD, step)
            for t in range(NB - AHEAD, NB):
                scatter(block(t))

        @engines.vector
        def _(dve):
            prime(dve, yw_done, h_done)
            link = Chain(dve, dch).step
            n_vector(dve, link)
            link(nc.vector.tensor_copy(block_no[:], S["iota"][0:SQ, 0:NB]))
            nc.vector.memset(empty[:, :, 0:1], 0.0).then_inc(empty_done, 1)
            nc.vector.tensor_copy(empty[:].bitcast(I32)[:, :, 1:2], S["spare"][:, 0:1].unsqueeze(1).broadcast_to([P, NB, 1])).then_inc(empty_done, 1)
            if L == 0:
                dve.wait_ge(exp_done, 1)
                dve.wait_ge(r_in, 32)
                link(nc.vector.tensor_scalar(sc[:], sc[:], 1.0, None, ALU.add))
                link(nc.vector.reciprocal(sc[:], sc[:]))
                link(nc.vector.tensor_tensor(sfc[:], sc[:], e_bias[:].unsqueeze(1).broadcast_to(sh), ALU.add))
                gs = E0 // GRP0
                link(nc.vector.tensor_reduce(gsc[:], sfc[:].rearrange("p b (g s) -> p b g s", s=gs), axis=AX, op=ALU.max))
                g8 = lambda t: t[:, :, 0:GRP0]
                top_k(nc, link, gsc[:], GRP0, TOPG0, mx, g8(gt), g8(eq), g8(ca), g8(cb), cnt[:], gsel[:])
                by_group = sfc[:].rearrange("p b (g s) -> p (b g) s", s=gs)
                link(nc.vector.tensor_tensor(by_group, by_group, gsel[:].rearrange("p b g -> p (b g)").unsqueeze(2)
                                             .broadcast_to([SQ, B * GRP0, gs]), ALU.mult))
                top_k(nc, link, sfc[:], E0, TOP0, mx, gt[:], eq[:], ca[:], cb[:], cnt[:], sel[:])
            else:
                dve.wait_ge(logit_done, 1)
                link(nc.vector.tensor_copy(sc[:], ps8[0:SQ, 0:B * E1].rearrange("p (b e) -> p b e", b=B)))
                link(nc.vector.tensor_reduce(cnt[:], sc[:], axis=AX, op=ALU.max))
                nc.vector.tensor_tensor(sc[:], sc[:], cnt[:].unsqueeze(2).broadcast_to(sh), ALU.subtract).then_inc(lm_done, 1)
                dve.wait_ge(exp_done, 1)
                link(nc.vector.tensor_reduce(cnt[:], sc[:], axis=AX, op=ALU.add))
                link(nc.vector.reciprocal(cnt[:], cnt[:]))
                link(nc.vector.tensor_tensor(sc[:], sc[:], cnt[:].unsqueeze(2).broadcast_to(sh), ALU.mult))
                top_k(nc, link, sc[:], E1, TOP1, mx, gt[:], eq[:], ca[:], cb[:], cnt[:], sel[:])
            nc.vector.tensor_copy(gt[:], sel[:]).then_inc(sel_done, 1)
            dve.wait_ge(pos_done, 1)
            positions(nc, dve, link, sh, pos[:], tot[:], cnt_e[:], psX, psY)
            if L:
                link(nc.vector.scalar_tensor_tensor(sel[:], pos[:], float(CAP1), sel[:], ALU.is_le, ALU.mult))
            link(nc.vector.tensor_tensor(sc[:], sel[:], sc[:], ALU.mult))
            link(nc.vector.tensor_reduce(cnt[:], sc[:], axis=AX, op=ALU.add))
            link(nc.vector.tensor_scalar(cnt[:], cnt[:], (1e-20, 1e-6)[L], None, ALU.add))
            link(nc.vector.reciprocal(cnt[:], cnt[:]))
            if L == 0:
                link(nc.vector.tensor_scalar(cnt[:], cnt[:], W0_SCALE, None, ALU.mult))
            link(nc.vector.tensor_tensor(sc[:], sc[:], cnt[:].unsqueeze(2).broadcast_to(sh), ALU.mult))
            if L == 0:
                link(nc.vector.tensor_scalar(nblk[:], cnt_e[:], 0.0, None, ALU.is_gt))
                for j in range(1, -(-NT // P)):
                    link(nc.vector.scalar_tensor_tensor(nblk[:], cnt_e[:], float(j * P), nblk[:], ALU.is_gt, ALU.add))
                src, dst, d = nblk, base, 1
                while d < E:
                    nc.vector.tensor_copy(dst[:, 0:d], src[:, 0:d])
                    link(nc.vector.tensor_tensor(dst[:, d:], src[:, d:], src[:, 0:E - d], ALU.add))
                    src, dst, d = dst, (base2 if dst is base else base), 2 * d
                first = dst
                last = src
                link(nc.vector.tensor_tensor(first[:], last[:], nblk[:], ALU.subtract))
                first_block = first[:].unsqueeze(1).broadcast_to(sh)
            else:
                first_block = S["iota"][0:SQ, 0:E].unsqueeze(1).broadcast_to(sh)
            link(nc.vector.scalar_tensor_tensor(pos[:], first_block, float(P), pos[:], ALU.mult, ALU.add))
            link(nc.vector.tensor_tensor(slot[:], pos[:], sel[:], ALU.mult))
            for b in range(B):
                ins = nc.vector.max(slot8[:, b, :], slot[:, b, :])
            link(ins)
            big = [SQ, B, TOP, E]
            link(nc.vector.tensor_tensor(is_slot[:], slot[:].unsqueeze(2).broadcast_to(big),
                                         slot8[:, :, 0:TOP].unsqueeze(3).broadcast_to(big), ALU.is_equal))
            link(nc.vector.tensor_tensor(is_slot[:], is_slot[:], sc[:].unsqueeze(2).broadcast_to(big), ALU.mult))
            nc.vector.tensor_reduce(entry[:, :, :, 0], is_slot[:], axis=AX, op=ALU.add).then_inc(entry_done, 1)
            nc.vector.tensor_copy(entry[:].bitcast(I32)[:, :, :, 1], S["token"][:].unsqueeze(2).broadcast_to([SQ, B, TOP])).then_inc(entry_done, 1)
            for k in range(TOP):
                ins = nc.vector.tensor_scalar(unused[:, :, k:k + 1], S["token"][:].unsqueeze(2), float(NB * P + k * NT + 1), None, ALU.add)
            link(ins)
            link(nc.vector.scalar_tensor_tensor(unused[:], slot8[:, :, 0:TOP], 0.0, unused[:], ALU.is_equal, ALU.mult))
            link(nc.vector.tensor_tensor(at_f[:], unused[:], slot8[:, :, 0:TOP], ALU.add))
            nc.vector.tensor_scalar(at_row[:], at_f[:].rearrange("p b k -> p (b k)"), -1.0, None, ALU.add).then_inc(entry_done, 1)
            if L == 0:
                link(nc.vector.tensor_tensor(ended[:], block_no[:].unsqueeze(2).broadcast_to([SQ, NB, E]),
                                             last[:].unsqueeze(1).broadcast_to([SQ, NB, E]), ALU.is_ge))
                link(nc.vector.tensor_reduce(expert_f[:], ended[:], axis=AX, op=ALU.add))
                nc.vector.tensor_scalar(expert_i[:], expert_f[:], float(E - 1), None, ALU.min).then_inc(base_done, 1)
                dve.wait_ge(sh_done, SPLIT)
                shared_products(dve, nc.vector, SPLIT, len(sh_units))

            def rows(p):
                t, i = p.t, p.i
                nc.vector.tensor_copy(g_row[p.j][:], row_of[:, bass.ds(t, 1), 1]).then_inc(idx_done, 1)

            def hidden(p):
                t, i = p.t, p.i
                dve.wait_ge(silu_done, t + 1 + PRIMED)
                nc.vector.tensor_tensor(hid[i][:], sg[:], psU[0][:, I0:2 * I0], ALU.mult).then_inc(h_done, 1)

            def weighted(p):
                t, i = p.t, p.i
                dve.wait_ge(dn_done, t + 1)
                dve.wait_ge(added, t + PRIMED)
                nc.vector.tensor_copy(s_row[i][:], row_of[:, bass.ds(t, 1), 1])
                nc.vector.tensor_scalar(yw[i][:], psY[:], info[:, bass.ds(t, 1), 0], None, ALU.mult).then_inc(yw_done, 1)

            def step(p, first=False, rows_too=True):
                t = p.t
                if L == 0:
                    hidden(p)
                if rows_too:
                    dve.wait_ge((xT_out, hT_out)[L], t + PRIMED)
                    rows(p.next(AHEAD))
                if not first:
                    weighted(p.next(-1))

            dve.wait_ge(info_in[0], 16)
            for t in range(AHEAD):
                rows(block(t))
            dve.wait_ge(info_in[1], 16)
            step(block(0), first=True)
            blocks(dve, 1, NB - AHEAD, step)
            for t in range(NB - AHEAD, NB):
                step(block(t), rows_too=False)
            weighted(block(NB - 1))

            def next_stats(b):
                dve.wait_ge(x_done, b + 1)
                nc.vector.bn_stats(S["stats"][:, b, :], S["x"][:, b, :]).then_inc(stats_done, 1)

            for b in range(B):
                dve.wait_ge(acc_in[b // 2], 16)
                nc.vector.scalar_tensor_tensor(S["x"][:, b, :], acc[:, b, :], S["gates"][0:SQ, 2 + L:3 + L], S["x"][:, b, :],
                                               ALU.mult, ALU.add).then_inc(x_done, 1)
                if L == 0 and b:
                    next_stats(b - 1)
            dve.wait_ge(x_done, B)
            if L == 0:
                next_stats(B - 1)
                dve.wait_ge(stats_done, B)


def setup(nc, sem, A, S):
    c_in, g_done = sem("st_c_in"), sem("st_g")
    z_done, c_done, i_done = sem("st_z"), sem("st_c"), sem("st_i")
    with (nc.sbuf_tensor("iota_i", [P, P], I32) as iota_i, nc.sbuf_tensor("token_i", [P, B], I32) as token_i,
          nc.sbuf_tensor("spare_i", [P, 1], I32) as spare_i, nc.Block() as block):
        @block.sync
        def _(sp):
            sp.dma_start(S["cols"][:], A["cols"]).then_inc(c_in, 16)

        @block.scalar
        def _(act):
            act.wait_ge(c_in, 16)
            nc.scalar.activation(S["gates"][:], S["cols"][:, C_GX:C_GX + 4], ACT.Tanh).then_inc(g_done, 1)
            act.wait_ge(g_done, 1)

        @block.vector
        def _(dve):
            nc.vector.memset(S["eps"][:], LN_EPS).then_inc(z_done, 1)
            nc.vector.memset(S["ident"][:], 0.0).then_inc(z_done, 1)
            nc.vector.memset(S["ones"][:], 1.0).then_inc(z_done, 1)
            nc.vector.memset(S["upto"][:], 1.0).then_inc(z_done, 1)
            nc.vector.memset(S["head_mean"][:], 0.0).then_inc(z_done, 1)
            dve.wait_ge(z_done, 5)
            for j in range(GH):
                nc.vector.memset(S["head_mean"][j * HD:(j + 1) * HD, j * HD:(j + 1) * HD], 1.0 / HD).then_inc(c_done, 1)

        @block.gpsimd
        def _(pool):
            pool.wait_ge(z_done, 4)
            nc.gpsimd.affine_select(out=S["ident"][:], in_=S["ident"][:], compare_op=ALU.not_equal, fill=1.0, base=0,
                                    pattern=[[-1, P]], channel_multiplier=1).then_inc(c_done, 1)
            nc.gpsimd.affine_select(out=S["upto"][:], in_=S["upto"][:], compare_op=ALU.is_ge, fill=0.0, base=0,
                                    pattern=[[1, SQ]], channel_multiplier=-1).then_inc(c_done, 1)
            nc.gpsimd.iota(iota_i[:], pattern=[[1, P]], base=0, channel_multiplier=0).then_inc(i_done, 1)
            nc.gpsimd.iota(token_i[:], pattern=[[SQ, B]], base=0, channel_multiplier=1).then_inc(i_done, 1)
            nc.gpsimd.iota(spare_i[:], pattern=[[1, 1]], base=NT, channel_multiplier=1).then_inc(i_done, 1)
            pool.wait_ge(i_done, 3)
            nc.gpsimd.tensor_copy(S["iota"][:], iota_i[:]).then_inc(c_done, 1)
            nc.gpsimd.tensor_copy(S["token"][:], token_i[0:SQ, :]).then_inc(c_done, 1)
            nc.gpsimd.tensor_copy(S["spare"][:], spare_i[:]).then_inc(c_done, 1)
            pool.wait_ge(c_done, 5 + GH)


def build(nc, A, out):
    with ExitStack() as ctx:
        sb = lambda name, shape, dt=F32: ctx.enter_context(nc.sbuf_tensor(name, shape, dt))
        layer_sems = []

        def sem(name):
            layer_sems.append(nc.alloc_semaphore(name=name))
            return layer_sems[-1]

        dram = lambda name, shape, dt: nc.dram_tensor(name, shape, dt, kind="Internal").ap()
        S = {
            "x": sb("x_sb", [SQ, B, D]), "stats": sb("bn_stats", [SQ, B, 6]),
            "cols": sb("cols_sb", [P, NCOLS]), "gates": sb("gates", [P, 4]),
            "ident": sb("ident", [P, P]), "head_mean": sb("head_mean", [P, P]), "eps": sb("eps", [P, 1]),
            "ones": sb("ones", [SQ, P]), "upto": sb("upto", [SQ, SQ]),
            "K": [dram(f"scr_k{L}", [2, D, B, SK], F32) for L in range(2)],
            "V": [dram(f"scr_v{L}", [B, SK, D], F32) for L in range(2)],
            "Q": dram("scr_q", [2, D, NT], F32),
            "x_rows": dram("scr_x", [NT + P, D], F32), "h_rows": dram("scr_h", [NT + P, HID1], F32),
            "acc_rows": dram("scr_acc", [NT + P, D], F32),
            "table": [dram(f"scr_table{L}", [(MB0, E1)[L] * P + (TOP0, TOP1)[L] * NT, 2], F32) for L in range(2)],
            "iota": sb("iota", [P, P]), "token": sb("token", [SQ, B]), "spare": sb("spare", [P, 1]),
        }
        setup(nc, sem, A, S)
        project_context(nc, sem, A, S)
        for L in range(2):
            with (nc.sbuf_tensor(f"attnT{L}", [P, NK, NT], F32) as attnT,
                  nc.sbuf_tensor(f"wo{L}", [P, NK, D], F32) as wo, nc.sbuf_tensor(f"o_bias{L}", [SQ, D], F32) as o_bias):
                S["attnT"] = attnT
                W = {"wo": wo, "bias": o_bias, "in": sem(f"o{L}_w_in")}
                with ExitStack() as kv_ctx:
                    KV = kv_tiles(nc, kv_ctx, sem, L)
                    queries(nc, sem, L, A, S, KV)
                    attention(nc, sem, L, A, S, KV, W)
                output(nc, sem, L, A, S, W)
            experts(nc, sem, L, A, S, out)
            if L == 0:
                nc.clear_and_free_semaphores(layer_sems)
                layer_sems.clear()
                nc.all_engine_barrier()


def lay_out(i):
    import numpy as np
    i = {k: np.asarray(v) for k, v in i.items()}
    a = {}
    ctxT = i["ctx_1024"].reshape(B, SK, NK, P).transpose(0, 3, 2, 1)
    a["ctxT"] = np.concatenate([ctxT, np.zeros((2, P, NK, SK), ctxT.dtype)])
    a["x"] = i["x"]
    mask = i["mask_Bx1x1xS2_ik0"].reshape(B, SK)
    a["mask"] = np.concatenate([mask, np.zeros((1, SK), mask.dtype)])
    for L in range(2):
        for n in "qkv":
            a[f"wT_{n}{L}"] = i[f"L{L}_xattn_W{n}"].T
    a["wT_o0"], a["wT_o1"] = i["L0_xattn_Wp"].T, i["L1_xattn_Wo"].T
    a["bo0"], a["bo1"] = i["L0_xattn_bp"].reshape(1, D), i["L1_xattn_bo"].reshape(1, D)
    col = lambda v: v.reshape(NK, P).T
    a["cols"] = np.concatenate([np.tile(i["L0_xattn_ln_g"], GH)[:, None], np.tile(i["L0_xattn_ln_b"], GH)[:, None],
                                col(i["L1_xattn_bk"]), col(i["L1_xattn_bq"]), col(i["L1_xattn_bv"]),
                                np.tile(i["g_xattn"], (P, 1)), np.tile(i["g_ffn"], (P, 1))], axis=1)
    a["routerT0"] = i["L0_ffn_gate_weight"].T
    a["e_bias"] = i["L0_ffn_e_score_correction_bias"].reshape(1, E0)
    a["sh_up"] = np.concatenate([i["L0_ffn_shared_gate_w"], i["L0_ffn_shared_up_w"]]).reshape(4 * I0, NK, P).transpose(2, 1, 0)
    a["sh_dn"] = i["L0_ffn_shared_down_w"].reshape(D, NK, P).transpose(2, 1, 0)
    a["gu"] = i["L0_ffn_experts_gate_up"].reshape(E0, 2 * I0, NK, P).transpose(0, 3, 2, 1)
    a["dn"] = i["L0_ffn_experts_down"].reshape(E0, D, I0 // P, P).transpose(0, 3, 2, 1)
    a["routerT1"] = i["L1_ffn_w_router"].T
    a["wgT1"] = i["L1_ffn_w_gate"].T
    a["wd1"] = i["L1_ffn_w_down"].reshape(E1, D, NI1, P).transpose(0, 3, 2, 1)
    return {k: np.ascontiguousarray(v) for k, v in a.items()}


def kernel(**inputs):
    import concourse.bacc as bacc
    from concourse.bass_utils import run_bass_kernel_spmd
    arrays = lay_out(inputs)
    nc = bacc.Bacc("TRN2", target_bir_lowering=False, num_devices=1)
    A = {k: nc.dram_tensor(f"in_{k}", list(v.shape), mybir.dt.from_np(v.dtype), kind="ExternalInput").ap() for k, v in arrays.items()}
    out = nc.dram_tensor("out_0", [B, SQ, D], F32, kind="ExternalOutput").ap()
    build(nc, A, out)
    r = run_bass_kernel_spmd(nc, [{f"in_{k}": v for k, v in arrays.items()}], core_ids=[0])
    return r.results[0]["out_0"]
```
